# Optimizing a Trainium2 kernel written in Bass

```python
import numpy as np
import jax
import jax.numpy as jnp

def _softmax(x, axis=-1):
    return jax.nn.softmax(x, axis=axis)

def _gelu(x):
    return jax.nn.gelu(x, approximate=True)

def _silu(x):
    return jax.nn.silu(x)

def _sigmoid(x):
    return jax.nn.sigmoid(x)

def _layernorm(x, axis=-1, eps=1e-05):
    m = jnp.mean(x, axis=axis, keepdims=True)
    v = jnp.var(x, axis=axis, keepdims=True)
    return (x - m) / jnp.sqrt(v + eps)

def _scatter_add(tgt, idx, src, axis=0):
    return tgt.at[idx].add(src)

def _segment_sum(src, seg, n):
    return jax.ops.segment_sum(src, seg, n)
kernel_name = 'mk_gnn_preln_d4_gnn_r32_a0469b'

def setup_inputs(seed: int=0):
    np.random.seed(seed)
    _w = jnp.asarray

    def _rec_inputs():
        import jax
        import jax.numpy as jnp
        _gk = jax.random.key(seed)
        x = -8.776e-05 + 1 * jax.random.normal(jax.random.fold_in(_gk, 1), (625, 256), jnp.float32)
        src = jax.random.randint(jax.random.fold_in(_gk, 2), (10000,), 0, 625, jnp.int32)
        dst = jax.random.randint(jax.random.fold_in(_gk, 3), (10000,), 0, 625, jnp.int32)
        _o = jnp.argsort(dst, stable=True)
        src = src[_o]
        dst = dst[_o]
        edge_type_16 = jax.random.randint(jax.random.fold_in(_gk, 13), (10000,), 0, 16, jnp.int32)
        edge_weight = jax.random.uniform(jax.random.fold_in(_gk, 14), (10000,), jnp.float32, 0.0, 1)
        edge_weight1 = jax.random.uniform(jax.random.fold_in(_gk, 15), (10000, 1), jnp.float32, 0.0, 1)
        node_vec = jax.random.uniform(jax.random.fold_in(_gk, 16), (625,), jnp.float32, 0.0, 0.999833)
        return (x, src, dst, edge_type_16, edge_weight, edge_weight1, node_vec)
    x, src, dst, edge_type_16, edge_weight, edge_weight1, node_vec = _rec_inputs()

    def _L0_gnn_setup():
        import jax, jax.numpy as jnp
        import numpy as np
        N = 625
        E = 10000
        DIN = 256
        DOUT = 256
        L = 3

        def _edge_conv(x, src, dst, W, b):
            xi = x[dst]
            xj = x[src]
            m = jnp.concatenate([xi, xj - xi], axis=-1) @ W + b
            s = jax.ops.segment_sum(m, dst, num_segments=N)
            cnt = jax.ops.segment_sum(jnp.ones((dst.shape[0],), m.dtype), dst, num_segments=N)
            return s / jnp.maximum(cnt, 1.0)[:, None]
        key = jax.random.key(seed)
        ks = jax.random.split(key, 4 + 2 * L)
        x = jax.random.normal(ks[0], (N, DIN), dtype=jnp.float32)
        edge_index = jax.random.randint(ks[1], (2, E), 0, N, dtype=jnp.int64)
        scale = 0.05
        inp = {'x': x, 'edge_index': edge_index}
        din = DIN
        for l in range(L):
            inp[f'W{l}'] = jax.random.normal(ks[2 + l], (2 * din, DOUT), dtype=jnp.float32) * scale
            inp[f'b{l}'] = jnp.zeros((DOUT,), dtype=jnp.float32)
            din = DOUT
        cat_dim = DIN + L * DOUT
        inp['Wf'] = jax.random.normal(ks[2 + L], (cat_dim, DOUT), dtype=jnp.float32) * scale
        inp['bf'] = jnp.zeros((DOUT,), dtype=jnp.float32)
        return inp
    _L0_gnn_all = _L0_gnn_setup()
    _L0_gnn_in = {k: v for k, v in _L0_gnn_all.items() if k in ('W0', 'b0', 'W1', 'b1', 'W2', 'b2', 'Wf', 'bf')}
    del _L0_gnn_all

    def _L1_gnn_setup():
        import jax, jax.numpy as jnp
        import numpy as np
        N_NODES = 50000
        N_EDGES = 25000
        NUM_RELS = 16
        FEAT = 256
        OUT = 256
        key = jax.random.key(seed)
        ks = jax.random.split(key, 7)
        h = jax.random.normal(ks[0], (N_NODES, FEAT), dtype=jnp.float32)
        norm = jax.random.uniform(ks[1], (N_EDGES, 1), dtype=jnp.float32)
        weight = jax.random.normal(ks[2], (NUM_RELS, FEAT, OUT), dtype=jnp.float32) * 0.05
        gate_weight = jax.random.normal(ks[3], (NUM_RELS, FEAT, 1), dtype=jnp.float32) * 0.05
        src = jax.random.randint(ks[4], (N_EDGES,), 0, N_NODES)
        dst = jax.random.randint(ks[5], (N_EDGES,), 0, N_NODES)
        rel_type = jax.random.randint(ks[6], (N_EDGES,), 0, NUM_RELS)
        return {'h': h, 'norm': norm, 'weight': weight, 'gate_weight': gate_weight, 'src': src, 'dst': dst, 'rel_type': rel_type}
    _L1_gnn_all = _L1_gnn_setup()
    _L1_gnn_in = {k: v for k, v in _L1_gnn_all.items() if k in ('weight', 'gate_weight')}
    del _L1_gnn_all

    def _L2_gnn_setup():
        import jax, jax.numpy as jnp
        import numpy as np
        MU = 2.0
        key = jax.random.key(seed)
        ks = jax.random.split(key, 8)
        N, E, IN, P, OUT = (3125, 50000, 256, 128, 256)
        x = jax.random.normal(ks[0], (N, IN), dtype=jnp.float32)
        edge_vals = jnp.ones((E,), dtype=jnp.float32)
        Wp = jax.random.normal(ks[1], (P, IN), dtype=jnp.float32) * (1.0 / np.sqrt(IN))
        bp = jnp.zeros((P,), dtype=jnp.float32)
        W1 = jax.random.normal(ks[2], (OUT, P), dtype=jnp.float32) * (1.0 / np.sqrt(P))
        b1 = jnp.zeros((OUT,), dtype=jnp.float32)
        W2 = jax.random.normal(ks[3], (OUT, P), dtype=jnp.float32) * (1.0 / np.sqrt(P))
        b2 = jnp.zeros((OUT,), dtype=jnp.float32)
        src = jax.random.randint(ks[4], (E,), 0, N, dtype=jnp.int32)
        dst = jax.random.randint(ks[5], (E,), 0, N, dtype=jnp.int32)
        return {'x': x, 'edge_vals': edge_vals, 'Wp': Wp, 'bp': bp, 'W1': W1, 'b1': b1, 'W2': W2, 'b2': b2, 'src': src, 'dst': dst}
    _L2_gnn_all = _L2_gnn_setup()
    _L2_gnn_in = {k: v for k, v in _L2_gnn_all.items() if k in ('Wp', 'bp', 'W1', 'b1', 'W2', 'b2')}
    del _L2_gnn_all

    def _L3_gnn_setup():
        import jax, jax.numpy as jnp
        import numpy as np
        from jax import lax
        N, E, D = (256, 8192, 256)
        NH, FOUT = (4, 64)
        D_STATE, D_CONV, DT_RANK = (16, 4, 16)

        def _layer_norm(x, g, b, eps=1e-05):
            mu = jnp.mean(x, -1, keepdims=True)
            var = jnp.var(x, -1, keepdims=True)
            return (x - mu) * lax.rsqrt(var + eps) * g + b

        def _mamba(xs, in_proj_w, conv_w, conv_b, x_proj_w, dt_proj_w, dt_proj_b, A_log, D_param, out_proj_w):
            n = xs.shape[0]
            xz = xs @ in_proj_w.T
            xc, z = jnp.split(xz, 2, axis=-1)
            K = conv_w.shape[1]
            xp = jnp.pad(xc, ((K - 1, 0), (0, 0)))
            xc = sum((xp[k:k + n] * conv_w[:, k] for k in range(K))) + conv_b
            xc = jax.nn.silu(xc)
            dbc = xc @ x_proj_w.T
            dt = jax.nn.softplus(dbc[:, :DT_RANK] @ dt_proj_w.T + dt_proj_b)
            Bm = dbc[:, DT_RANK:DT_RANK + D_STATE]
            Cm = dbc[:, DT_RANK + D_STATE:]
            A = -jnp.exp(A_log)
            dA = jnp.exp(dt[:, :, None] * A)
            dBx = (dt * xc)[:, :, None] * Bm[:, None, :]

            def step(h, t):
                dA_t, dBx_t, C_t = t
                h = dA_t * h + dBx_t
                return (h, h @ C_t)
            _, y = lax.scan(step, jnp.zeros((xc.shape[1], D_STATE), xs.dtype), (dA, dBx, Cm))
            y = y + xc * D_param
            y = y * jax.nn.silu(z)
            return y @ out_proj_w.T

        def _forward(x, edge_index, deg_noise, gat_w, gat_a_src, gat_a_tgt, gat_b, ln_local_g, ln_local_b, ln_global_g, ln_global_b, ln2_g, ln2_b, in_proj_w, conv_w, conv_b, x_proj_w, dt_proj_w, dt_proj_b, A_log, D_param, out_proj_w, wl, wg, ff1_w, ff1_b, ff2_w, ff2_b):
            n = x.shape[0]
            src, tgt = (edge_index[0], edge_index[1])
            proj = (x @ gat_w.T).reshape(n, NH, FOUT)
            s_src = jnp.sum(proj * gat_a_src, -1)
            s_tgt = jnp.sum(proj * gat_a_tgt, -1)
            e = jax.nn.leaky_relu(s_src[src] + s_tgt[tgt], 0.2)
            exp_e = jnp.exp(e - jnp.max(e))
            denom = jax.ops.segment_sum(exp_e, tgt, num_segments=n)
            attn = exp_e / (denom[tgt] + 1e-16)
            agg = jax.ops.segment_sum(proj[src] * attn[:, :, None], tgt, num_segments=n)
            h_local = jax.nn.elu((agg + x.reshape(n, NH, FOUT)).reshape(n, NH * FOUT) + gat_b)
            h_local = _layer_norm(h_local, ln_local_g, ln_local_b)
            deg = jax.ops.segment_sum(jnp.ones((src.shape[0],), x.dtype), src, num_segments=n)
            perm = jnp.argsort(deg + deg_noise, stable=True)
            inv = jnp.argsort(perm)
            y = _mamba(x[perm], in_proj_w, conv_w, conv_b, x_proj_w, dt_proj_w, dt_proj_b, A_log, D_param, out_proj_w)
            h_attn = _layer_norm(x + y[inv], ln_global_g, ln_global_b)
            gate = jax.nn.sigmoid(h_local @ wl.T + h_attn @ wg.T)
            h = gate * h_local + (1.0 - gate) * h_attn
            ff = jax.nn.relu(h @ ff1_w.T + ff1_b) @ ff2_w.T + ff2_b
            return _layer_norm(h + ff, ln2_g, ln2_b)
        key = jax.random.key(seed)
        ks = jax.random.split(key, 24)
        w = lambda i, shape, s=0.05: jax.random.normal(ks[i], shape, dtype=jnp.float32) * s
        return {'x': jax.random.normal(ks[0], (N, D), dtype=jnp.float32), 'edge_index': jax.random.randint(ks[1], (2, E), 0, N, dtype=jnp.int32), 'edge_prob': jax.random.uniform(ks[2], (E,), dtype=jnp.float32), 'deg_noise': jax.random.uniform(ks[3], (N,), dtype=jnp.float32), 'gat_w': w(4, (NH * FOUT, D)), 'gat_a_src': w(5, (NH, FOUT)), 'gat_a_tgt': w(6, (NH, FOUT)), 'gat_b': jnp.zeros((NH * FOUT,), jnp.float32), 'ln_local_g': jnp.ones((D,), jnp.float32), 'ln_local_b': jnp.zeros((D,), jnp.float32), 'ln_global_g': jnp.ones((D,), jnp.float32), 'ln_global_b': jnp.zeros((D,), jnp.float32), 'ln2_g': jnp.ones((D,), jnp.float32), 'ln2_b': jnp.zeros((D,), jnp.float32), 'in_proj_w': w(7, (2 * D, D)), 'conv_w': w(8, (D, D_CONV), 0.2), 'conv_b': jnp.zeros((D,), jnp.float32), 'x_proj_w': w(9, (DT_RANK + 2 * D_STATE, D)), 'dt_proj_w': w(10, (D, DT_RANK)), 'dt_proj_b': w(11, (D,), 0.1) - 4.0, 'A_log': jnp.log(jnp.tile(jnp.arange(1, D_STATE + 1, dtype=jnp.float32), (D, 1))), 'D_param': jnp.ones((D,), jnp.float32), 'out_proj_w': w(12, (D, D)), 'wl': w(13, (D, D)), 'wg': w(14, (D, D)), 'ff1_w': w(15, (2 * D, D)), 'ff1_b': jnp.zeros((2 * D,), jnp.float32), 'ff2_w': w(16, (D, 2 * D)), 'ff2_b': jnp.zeros((D,), jnp.float32)}
    _L3_gnn_all = _L3_gnn_setup()
    _L3_gnn_in = {k: v for k, v in _L3_gnn_all.items() if k in ('gat_w', 'gat_a_src', 'gat_a_tgt', 'gat_b', 'ln_local_g', 'ln_local_b', 'ln_global_g', 'ln_global_b', 'ln2_g', 'ln2_b', 'in_proj_w', 'conv_w', 'conv_b', 'x_proj_w', 'dt_proj_w', 'dt_proj_b', 'A_log', 'D_param', 'out_proj_w', 'wl', 'wg', 'ff1_w', 'ff1_b', 'ff2_w', 'ff2_b')}
    del _L3_gnn_all
    return {'x': x, 'src': src, 'dst': dst, 'edge_type_16': edge_type_16, 'edge_weight': edge_weight, 'edge_weight1': edge_weight1, 'node_vec': node_vec, 'L0_gnn_W0': _L0_gnn_in['W0'], 'L0_gnn_b0': _L0_gnn_in['b0'], 'L0_gnn_W1': _L0_gnn_in['W1'], 'L0_gnn_b1': _L0_gnn_in['b1'], 'L0_gnn_W2': _L0_gnn_in['W2'], 'L0_gnn_b2': _L0_gnn_in['b2'], 'L0_gnn_Wf': _L0_gnn_in['Wf'], 'L0_gnn_bf': _L0_gnn_in['bf'], 'L1_gnn_weight': _L1_gnn_in['weight'], 'L1_gnn_gate_weight': _L1_gnn_in['gate_weight'], 'L2_gnn_Wp': _L2_gnn_in['Wp'], 'L2_gnn_bp': _L2_gnn_in['bp'], 'L2_gnn_W1': _L2_gnn_in['W1'], 'L2_gnn_b1': _L2_gnn_in['b1'], 'L2_gnn_W2': _L2_gnn_in['W2'], 'L2_gnn_b2': _L2_gnn_in['b2'], 'L3_gnn_gat_w': _L3_gnn_in['gat_w'], 'L3_gnn_gat_a_src': _L3_gnn_in['gat_a_src'], 'L3_gnn_gat_a_tgt': _L3_gnn_in['gat_a_tgt'], 'L3_gnn_gat_b': _L3_gnn_in['gat_b'], 'L3_gnn_ln_local_g': _L3_gnn_in['ln_local_g'], 'L3_gnn_ln_local_b': _L3_gnn_in['ln_local_b'], 'L3_gnn_ln_global_g': _L3_gnn_in['ln_global_g'], 'L3_gnn_ln_global_b': _L3_gnn_in['ln_global_b'], 'L3_gnn_ln2_g': _L3_gnn_in['ln2_g'], 'L3_gnn_ln2_b': _L3_gnn_in['ln2_b'], 'L3_gnn_in_proj_w': _L3_gnn_in['in_proj_w'], 'L3_gnn_conv_w': _L3_gnn_in['conv_w'], 'L3_gnn_conv_b': _L3_gnn_in['conv_b'], 'L3_gnn_x_proj_w': _L3_gnn_in['x_proj_w'], 'L3_gnn_dt_proj_w': _L3_gnn_in['dt_proj_w'], 'L3_gnn_dt_proj_b': _L3_gnn_in['dt_proj_b'], 'L3_gnn_A_log': _L3_gnn_in['A_log'], 'L3_gnn_D_param': _L3_gnn_in['D_param'], 'L3_gnn_out_proj_w': _L3_gnn_in['out_proj_w'], 'L3_gnn_wl': _L3_gnn_in['wl'], 'L3_gnn_wg': _L3_gnn_in['wg'], 'L3_gnn_ff1_w': _L3_gnn_in['ff1_w'], 'L3_gnn_ff1_b': _L3_gnn_in['ff1_b'], 'L3_gnn_ff2_w': _L3_gnn_in['ff2_w'], 'L3_gnn_ff2_b': _L3_gnn_in['ff2_b']}

def reference(x, src, dst, edge_type_16, edge_weight, edge_weight1, node_vec, L0_gnn_W0, L0_gnn_b0, L0_gnn_W1, L0_gnn_b1, L0_gnn_W2, L0_gnn_b2, L0_gnn_Wf, L0_gnn_bf, L1_gnn_weight, L1_gnn_gate_weight, L2_gnn_Wp, L2_gnn_bp, L2_gnn_W1, L2_gnn_b1, L2_gnn_W2, L2_gnn_b2, L3_gnn_gat_w, L3_gnn_gat_a_src, L3_gnn_gat_a_tgt, L3_gnn_gat_b, L3_gnn_ln_local_g, L3_gnn_ln_local_b, L3_gnn_ln_global_g, L3_gnn_ln_global_b, L3_gnn_ln2_g, L3_gnn_ln2_b, L3_gnn_in_proj_w, L3_gnn_conv_w, L3_gnn_conv_b, L3_gnn_x_proj_w, L3_gnn_dt_proj_w, L3_gnn_dt_proj_b, L3_gnn_A_log, L3_gnn_D_param, L3_gnn_out_proj_w, L3_gnn_wl, L3_gnn_wg, L3_gnn_ff1_w, L3_gnn_ff1_b, L3_gnn_ff2_w, L3_gnn_ff2_b):
    import jax
    import jax.numpy as jnp

    def _L0_gnn_ref(x, edge_index, W0, b0, W1, b1, W2, b2, Wf, bf):
        import jax, jax.numpy as jnp
        import numpy as np
        N = 625
        E = 10000
        DIN = 256
        DOUT = 256
        L = 3

        def _edge_conv(x, src, dst, W, b):
            xi = x[dst]
            xj = x[src]
            m = jnp.concatenate([xi, xj - xi], axis=-1) @ W + b
            s = jax.ops.segment_sum(m, dst, num_segments=N)
            cnt = jax.ops.segment_sum(jnp.ones((dst.shape[0],), m.dtype), dst, num_segments=N)
            return s / jnp.maximum(cnt, 1.0)[:, None]
        src, dst = (edge_index[0], edge_index[1])
        xs = [x]
        h = x
        for W, b in ((W0, b0), (W1, b1), (W2, b2)):
            h = jax.nn.relu(_edge_conv(h, src, dst, W, b))
            xs.append(h)
        cat = jnp.concatenate(xs, axis=-1)
        return cat @ Wf + bf

    def _L1_gnn_ref(h, norm, weight, gate_weight, src, dst, rel_type):
        import jax, jax.numpy as jnp
        import numpy as np
        N_NODES = 50000
        N_EDGES = 25000
        NUM_RELS = 16
        FEAT = 256
        OUT = 256
        n_nodes = h.shape[0]
        all_msg = jnp.einsum('nf,rfo->rno', h, weight)
        msg = all_msg[rel_type, src] * norm
        all_gate = jnp.einsum('nf,rf->rn', h, gate_weight[..., 0])
        gate = jax.nn.sigmoid(all_gate[rel_type, src])[:, None]
        msg = msg * gate
        agg = jax.ops.segment_sum(msg, dst, num_segments=n_nodes)
        return jax.nn.relu(agg)

    def _L2_gnn_ref(x, edge_vals, Wp, bp, W1, b1, W2, b2, src, dst):
        import jax, jax.numpy as jnp
        import numpy as np
        MU = 2.0
        N = x.shape[0]
        h = jax.nn.relu(x @ Wp.T + bp)
        hp = h ** MU
        msgs = edge_vals[:, None] * hp[src]
        agg = jax.ops.segment_sum(msgs, dst, num_segments=N)
        agg = agg ** (1.0 / MU)
        return h @ W1.T + b1 + agg @ W2.T + b2

    def _L3_gnn_ref(x, edge_index, edge_prob, deg_noise, gat_w, gat_a_src, gat_a_tgt, gat_b, ln_local_g, ln_local_b, ln_global_g, ln_global_b, ln2_g, ln2_b, in_proj_w, conv_w, conv_b, x_proj_w, dt_proj_w, dt_proj_b, A_log, D_param, out_proj_w, wl, wg, ff1_w, ff1_b, ff2_w, ff2_b):
        import jax, jax.numpy as jnp
        import numpy as np
        from jax import lax
        N, E, D = (256, 8192, 256)
        NH, FOUT = (4, 64)
        D_STATE, D_CONV, DT_RANK = (16, 4, 16)

        def _layer_norm(x, g, b, eps=1e-05):
            mu = jnp.mean(x, -1, keepdims=True)
            var = jnp.var(x, -1, keepdims=True)
            return (x - mu) * lax.rsqrt(var + eps) * g + b

        def _mamba(xs, in_proj_w, conv_w, conv_b, x_proj_w, dt_proj_w, dt_proj_b, A_log, D_param, out_proj_w):
            n = xs.shape[0]
            xz = xs @ in_proj_w.T
            xc, z = jnp.split(xz, 2, axis=-1)
            K = conv_w.shape[1]
            xp = jnp.pad(xc, ((K - 1, 0), (0, 0)))
            xc = sum((xp[k:k + n] * conv_w[:, k] for k in range(K))) + conv_b
            xc = jax.nn.silu(xc)
            dbc = xc @ x_proj_w.T
            dt = jax.nn.softplus(dbc[:, :DT_RANK] @ dt_proj_w.T + dt_proj_b)
            Bm = dbc[:, DT_RANK:DT_RANK + D_STATE]
            Cm = dbc[:, DT_RANK + D_STATE:]
            A = -jnp.exp(A_log)
            dA = jnp.exp(dt[:, :, None] * A)
            dBx = (dt * xc)[:, :, None] * Bm[:, None, :]

            def step(h, t):
                dA_t, dBx_t, C_t = t
                h = dA_t * h + dBx_t
                return (h, h @ C_t)
            _, y = lax.scan(step, jnp.zeros((xc.shape[1], D_STATE), xs.dtype), (dA, dBx, Cm))
            y = y + xc * D_param
            y = y * jax.nn.silu(z)
            return y @ out_proj_w.T

        def _forward(x, edge_index, deg_noise, gat_w, gat_a_src, gat_a_tgt, gat_b, ln_local_g, ln_local_b, ln_global_g, ln_global_b, ln2_g, ln2_b, in_proj_w, conv_w, conv_b, x_proj_w, dt_proj_w, dt_proj_b, A_log, D_param, out_proj_w, wl, wg, ff1_w, ff1_b, ff2_w, ff2_b):
            n = x.shape[0]
            src, tgt = (edge_index[0], edge_index[1])
            proj = (x @ gat_w.T).reshape(n, NH, FOUT)
            s_src = jnp.sum(proj * gat_a_src, -1)
            s_tgt = jnp.sum(proj * gat_a_tgt, -1)
            e = jax.nn.leaky_relu(s_src[src] + s_tgt[tgt], 0.2)
            exp_e = jnp.exp(e - jnp.max(e))
            denom = jax.ops.segment_sum(exp_e, tgt, num_segments=n)
            attn = exp_e / (denom[tgt] + 1e-16)
            agg = jax.ops.segment_sum(proj[src] * attn[:, :, None], tgt, num_segments=n)
            h_local = jax.nn.elu((agg + x.reshape(n, NH, FOUT)).reshape(n, NH * FOUT) + gat_b)
            h_local = _layer_norm(h_local, ln_local_g, ln_local_b)
            deg = jax.ops.segment_sum(jnp.ones((src.shape[0],), x.dtype), src, num_segments=n)
            perm = jnp.argsort(deg + deg_noise, stable=True)
            inv = jnp.argsort(perm)
            y = _mamba(x[perm], in_proj_w, conv_w, conv_b, x_proj_w, dt_proj_w, dt_proj_b, A_log, D_param, out_proj_w)
            h_attn = _layer_norm(x + y[inv], ln_global_g, ln_global_b)
            gate = jax.nn.sigmoid(h_local @ wl.T + h_attn @ wg.T)
            h = gate * h_local + (1.0 - gate) * h_attn
            ff = jax.nn.relu(h @ ff1_w.T + ff1_b) @ ff2_w.T + ff2_b
            return _layer_norm(h + ff, ln2_g, ln2_b)
        return _forward(x, edge_index, deg_noise, gat_w, gat_a_src, gat_a_tgt, gat_b, ln_local_g, ln_local_b, ln_global_g, ln_global_b, ln2_g, ln2_b, in_proj_w, conv_w, conv_b, x_proj_w, dt_proj_w, dt_proj_b, A_log, D_param, out_proj_w, wl, wg, ff1_w, ff1_b, ff2_w, ff2_b)
    edge_index = jnp.stack([src, dst])
    h = jnp.maximum(_layernorm(x, axis=-1), 0.0)
    x = x + _L0_gnn_ref(h, edge_index, L0_gnn_W0, L0_gnn_b0, L0_gnn_W1, L0_gnn_b1, L0_gnn_W2, L0_gnn_b2, L0_gnn_Wf, L0_gnn_bf)
    h = jnp.maximum(_layernorm(x, axis=-1), 0.0)
    x = x + _L1_gnn_ref(h, edge_weight1, L1_gnn_weight, L1_gnn_gate_weight, src, dst, edge_type_16)
    h = jnp.maximum(_layernorm(x, axis=-1), 0.0)
    x = x + _L2_gnn_ref(h, edge_weight, L2_gnn_Wp, L2_gnn_bp, L2_gnn_W1, L2_gnn_b1, L2_gnn_W2, L2_gnn_b2, src, dst)
    h = jnp.maximum(_layernorm(x, axis=-1), 0.0)
    x = x + _L3_gnn_ref(h, edge_index, edge_weight, node_vec, L3_gnn_gat_w, L3_gnn_gat_a_src, L3_gnn_gat_a_tgt, L3_gnn_gat_b, L3_gnn_ln_local_g, L3_gnn_ln_local_b, L3_gnn_ln_global_g, L3_gnn_ln_global_b, L3_gnn_ln2_g, L3_gnn_ln2_b, L3_gnn_in_proj_w, L3_gnn_conv_w, L3_gnn_conv_b, L3_gnn_x_proj_w, L3_gnn_dt_proj_w, L3_gnn_dt_proj_b, L3_gnn_A_log, L3_gnn_D_param, L3_gnn_out_proj_w, L3_gnn_wl, L3_gnn_wg, L3_gnn_ff1_w, L3_gnn_ff1_b, L3_gnn_ff2_w, L3_gnn_ff2_b)
    return x

_drawn_inputs = setup_inputs


def setup_inputs(seed=0):
    import zlib

    import numpy as np

    out = dict(_drawn_inputs(seed))
    spreads = {'L0_gnn_b0': (0.0, 0.1),
     'L0_gnn_b1': (0.0, 0.1),
     'L0_gnn_b2': (0.0, 0.1),
     'L0_gnn_bf': (0.0, 0.1),
     'L2_gnn_bp': (0.0, 0.1),
     'L2_gnn_b1': (0.0, 0.1),
     'L2_gnn_b2': (0.0, 0.1),
     'L3_gnn_gat_b': (0.0, 0.327),
     'L3_gnn_ln_local_g': (1.0, 0.2),
     'L3_gnn_ln_local_b': (0.0, 0.396),
     'L3_gnn_ln_global_g': (1.0, 0.2),
     'L3_gnn_ln_global_b': (0.0, 0.386),
     'L3_gnn_ln2_g': (1.0, 0.2),
     'L3_gnn_ln2_b': (0.0, 0.1),
     'L3_gnn_conv_b': (0.0, 0.8),
     'L3_gnn_D_param': (1.0, 0.6),
     'L3_gnn_ff1_b': (0.0, 0.342),
     'L3_gnn_ff2_b': (0.0, 0.1)}
    factors = {'node_vec': 8.0,
     'L3_gnn_gat_a_src': 8.0,
     'L3_gnn_gat_a_tgt': 44.988,
     'L3_gnn_in_proj_w': 4.963,
     'L3_gnn_conv_w': 5.916,
     'L3_gnn_x_proj_w': 8.0,
     'L3_gnn_dt_proj_w': 8.0,
     'L3_gnn_dt_proj_b': 28.387,
     'L3_gnn_A_log': 8.0,
     'L3_gnn_out_proj_w': 5.24}
    for name, (base, spread) in spreads.items():
        noise = np.random.default_rng([zlib.crc32(name.encode()), seed]).standard_normal(out[name].shape)
        drawn = base * np.exp(spread * noise) if base else spread * noise
        out[name] = jnp.asarray(drawn.astype(out[name].dtype))
    for name, factor in factors.items():
        out[name] = (out[name] * factor).astype(out[name].dtype)
    return out
```

```python
from contextlib import ExitStack

import numpy as np
import concourse.bass as bass
from concourse import mybir

ALU = mybir.AluOpType
ACT = mybir.ActivationFunctionType
F32 = mybir.dt.float32
F16 = mybir.dt.float16
I32 = mybir.dt.int32
AX_X = mybir.AxisListType.X
ds = bass.ds

N = 625
T = 125
NT = N // T
E = 10000
ET = E // T
D = 256
C = D // 128
R = 16
Q = 128
NH, FH = 4, 64
NS = 16
RK = 16
DB = RK + 2 * NS
K4 = 4
EPS = 1e-5
BANK = 512
FAR = -1.0e30

PC = {}
at = 0
for name, n in [("b0", 2), ("b1", 2), ("b2", 2), ("bp", 1), ("conv_w", 8), ("conv_b", 2), ("dt_b", 2),
                ("A_log", 32), ("D", 2), ("ff1_b", 4), ("a_tgt", 2)]:
    PC[name] = at
    at += n
PCOLS = at
ROW = {name: i for i, name in enumerate(["bf", "b1", "b2", "a_src", "gat_b", "lnl_g", "lnl_b", "lng_g", "lng_b",
                                         "ln2_g", "ln2_b", "ff2_b"])}
NROW = len(ROW)
GT = 4
GROUPS = ET // GT
RING = 2 * GT
EARLY = 3
W3 = {}
at = 0
for name, n in [("gat", C * D), ("in", C * 2 * D), ("x", C * DB), ("out", C * D), ("wl", C * D), ("wg", C * D),
                ("ff1", C * 2 * D), ("ff2", 2 * C * D)]:
    W3[name] = at
    at += n
W3COLS = at


def pieces(lo, hi):
    out = []
    while lo < hi:
        end = min(hi, (lo // BANK + 1) * BANK)
        out.append((lo, end))
        lo = end
    return out


def gnn_kernel(nc, x_in, edge_int, edge_flt, noise, pcols_in, rows_in, w0_in, w1_in, gw_in, w2_in, w3_in, dtw_in,
               out, table):
    ctx = ExitStack()
    with ctx:
        def sb(name, shape, dt=F32):
            return ctx.enter_context(nc.sbuf_tensor(name, shape, dt))

        sems = {}

        def S(name):
            if name not in sems:
                sems[name] = ctx.enter_context(nc.semaphore(name))
            return sems[name]

        ident = sb("ident", [128, 128])
        ones = sb("ones", [128, 1])
        iota = sb("iota", [128, N], F16)
        pcol = sb("pcol", [128, 1])
        ncol = sb("ncol", [128, NT])
        edgei = sb("edgei", [T, 3, ET], I32)
        edgef = sb("edgef", [T, 3, ET])
        edgew = sb("edgew", [T, 2, ET])
        idx = sb("idx", [T, ET], I32)
        x = sb("x", [T, NT, D])
        hn = sb("hn", [T, NT, D])
        CT = sb("CT", [T, NT, N])
        CTf = CT[:, :, :].rearrange("p s n -> p (s n)")
        pcols = sb("pcols", [128, PCOLS])
        rows_early = sb("rows_early", [128, EARLY, D])
        key = sb("key", [T, NT])
        noise_sb = sb("noise_sb", [T, NT])
        deg = sb("deg", [T, NT])
        rank = sb("rank", [T, NT])
        rank2 = sb("rank2", [T, NT])
        st = sb("st", [T, NT, 6])
        mv = sb("mv", [T, NT, 2])
        ve = sb("ve", [T, NT])
        sd = sb("sd", [T, NT])
        rstd = sb("rstd", [T, NT])
        small = sb("small", [T, 64])
        dtw = sb("dtw", [RK, D])
        Aneg = sb("Aneg", [128, C, NS])
        half = sb("half", [128, 2])
        atgt = sb("atgt", [128, NH])
        gw_sb = sb("gw_sb", [128, C * R])
        zero = sb("zero", [128, T], F16)
        span = sb("span", [ET, 2])
        spans = sb("spans", [1, 3, GROUPS])
        reached = sb("reached", [1, GROUPS, NT], I32)
        A0 = sb("A0", [128, 25000])
        A1 = sb("A1", [128, 19656])
        PS = ctx.enter_context(nc.psum_tensor("PS", [128, 8 * BANK], F32))

        def a0(lo, n, rows_=128):
            return A0[0:rows_, lo:lo + n]

        def a1(lo, n, rows_=128):
            return A1[0:rows_, lo:lo + n]

        def cut(ap, k):
            return ap.rearrange("p (k n) -> p k n", k=k)

        ohd = A0[0:T, 0:ET * N // 2].bitcast(F16)
        wl0 = [a1(1024 * l, 1024).rearrange("p (k n) -> p k n", k=4) for l in range(3)]
        wf = a1(3072, 2048).rearrange("p (k n) -> p k n", k=8)
        hTs = [cut(a1(5120 + 1250 * l, 1250), C) for l in range(4)]
        g = cut(a1(10120, NT * D, T), NT)
        ohs = A1[0:T, 17025:17025 + RING * N // 2].bitcast(F16).rearrange("p (j n) -> p j n", j=RING)
        tmp = cut(a1(11400, 1250), C)
        idxf = a1(13900, ET, T)
        rcB = a1(12650, N)
        zB = a1(13275, N)
        CTn = cut(a1(13900, NT * N, T), NT)
        wring = a1(0, 2048).rearrange("p (j c n) -> p j c n", j=4, c=C)
        hT = cut(a1(2048, 1250), C)
        gate = a1(3298, NT * R, T).rearrange("p (s r) -> p s r", s=NT)
        ystage = a1(3378, 2 * NT * D, T).rearrange("p (j s n) -> p j s n", j=2, s=NT)
        GR = 40
        GG = 4
        gath = [a1(D * j if j < 8 else 10880 + D * (j - 8), D, T) for j in range(GR)]
        hilo = [A1[0:T, at_ + D * j:at_ + D * j + D].bitcast(F16).rearrange("p (k n) -> p k n", k=2)
                for at_ in (5938, 3378) for j in range(RING // 2)]
        gw = gw_sb[:, :].rearrange("p (c r) -> p c r", c=C)
        AwTf = a1(6962, NT * N, T)
        AwT = cut(AwTf, NT)
        wohs = [A1[0:T, at_ + N * j:at_ + N * j + N].bitcast(F16).rearrange("p (k n) -> p k n", k=2)
                for at_ in (3378, 6962) for j in range(RING // 2)]
        wsplit = cut(a1(2048, 2 * ET, T), 2)
        wsplit16 = a1(2208, ET // 2, T).bitcast(F16)
        keyB = a1(3378, N, T)
        junk = a1(4003, N, T)
        low = a1(4628, N, T)
        rankB = a1(5253, N, T)
        w2 = a1(10087, 768)
        w3 = a1(10880, W3COLS)
        rows_late = a1(16096, (NROW - EARLY) * D).rearrange("p (r n) -> p r n", n=D)
        qT = a1(0, N)
        hpT = a1(625, N)
        hpn = a1(1250, NT * Q, T).rearrange("p (s n) -> p s n", s=NT)
        aggT = a1(625, N)
        P = a0(0, 12500, T).rearrange("p (s h n) -> p s h n", s=NT, h=NH)
        V = a0(12500, 5000, T).rearrange("p (j h n) -> p j h n", j=2, h=NH)
        stgt = a0(17500, 2500, T).rearrange("p (h n) -> p h n", h=NH)
        far = cut(a0(20000, NT * N, T), NT)
        projT = cut(a0(23125, 1250), C)
        projn = a1(0, NT * NH * 65, T).rearrange("p (s h f) -> p s h f", s=NT, h=NH)
        hl = cut(a1(3378, NT * D, T), NT)
        sa = cut(a1(5938, NT * D, T), NT)
        sb_ = cut(a1(7218, NT * D, T), NT)
        ha = cut(a1(8498, NT * D, T), NT)
        ssrc = small[:, 0:20].rearrange("p (s h) -> p s h", s=NT)
        mx = small[:, 20:25]
        m1 = small[:, 25:26]
        gm = small[:, 26:27]
        den = small[:, 30:50].rearrange("p (s h) -> p s h", s=NT)
        PT = A1[0:T, 7218:7218 + 1563].bitcast(F16)[:, 0:NT * N].rearrange("p (s n) -> p s n", s=NT)
        hn16 = A1[0:T, 8782:8782 + 1280].bitcast(F16).rearrange("p (k s n) -> p k s n", k=2, s=NT)
        xsT = hT
        xcp = cut(a1(18400, 1256), C)
        zT = cut(a0(23125, 1250), C)
        xc = cut(a0(12500, 1250), C)
        dbc = a0(13750, N, DB)
        dt = cut(a0(14375, 1250), C)
        dtx = cut(a0(15625, 1250), C)
        dBx = cut(a0(16875, 1250), 2)
        hs = cut(a0(18125, 1250), 2)
        Cs = cut(a0(19375, 1250), 2)
        hc = cut(a0(20625, 1250), 2)
        Bs = cut(a0(21875, 1250), 2)
        dA = a0(0, 2500).rearrange("p (j c n) -> p j c n", j=2, c=C)
        PTt = cut(a0(2500, NT * N, T), NT)
        yn = cut(a0(5625, NT * D, T), NT)
        hlT = cut(a0(5400, 1250), C)
        haT = cut(a0(6650, 1250), C)
        hfT = cut(a0(7900, 1250), C)
        f1T = cut(a0(9150, 2500), 2 * C)
        gt = cut(a0(0, NT * D, T), NT)
        hf = cut(a0(1280, NT * D, T), NT)

        def row(name):
            i = ROW[name]
            src = rows_early[:, i:i + 1, :] if i < EARLY else rows_late[:, i - EARLY:i - EARLY + 1, :]
            return src[0:T].to_broadcast([T, NT, D])

        def pc(name, c=0):
            return pcols[:, PC[name] + c:PC[name] + c + 1]

        def W(name, n):
            return w3[:, W3[name]:W3[name] + n]

        def nat(b, s):
            return PS[0:T, b * BANK + s * D:b * BANK + s * D + D]

        def nat_all(b):
            return PS[0:T, b * BANK:b * BANK + NT * D].rearrange("p (s n) -> p s n", s=NT)

        def adjacency(lo, hi):
            return PS[0:T, 128 * lo:128 * hi].rearrange("p (b n) -> p b n", n=128)[:, :, 0:T]

        def squares(flat, lo, hi):
            return flat[:, T * lo:T * hi].rearrange("p (b n) -> p b n", n=T)

        def tr(b, c, rows_=128):
            return PS[0:rows_, (b + 2 * c) * BANK:(b + 2 * c) * BANK + N]

        POOL_TILES = (0, 3)
        keyB_ps = PS[0:T, 3 * BANK:3 * BANK + 640].rearrange("p (s n) -> p s n", s=NT)[:, :, 0:T]
        block = ctx.enter_context(nc.Block())

        @block.sync
        def _(sp):
            sp.dma_start(edgei[:, :, :], edge_int).then_inc(S("edges_in"), 16)
            sp.dma_start(x[:, :, :], x_in.rearrange("(s p) f -> p s f", p=T)).then_inc(S("x_in"), 16)
            sp.dma_start(edgew[:, :, :], edge_flt).then_inc(S("edgew_in"), 16)
            sp.dma_start(pcols[:, :], pcols_in).then_inc(S("params_in"), 16)
            sp.dma_start(a1(0, 5120), w0_in).then_inc(S("w0_in"), 16)
            sp.dma_start(rows_early[:, :, :], rows_in[0:EARLY].partition_broadcast(128)).then_inc(S("rows_in"), 16)
            sp.dma_start(gw_sb[:, :], gw_in).then_inc(S("gw_in"), 16)
            sp.dma_start(noise_sb[:, :], noise).then_inc(S("noise_in"), 16)
            sp.dma_start(dtw[:, :], dtw_in).then_inc(S("params_in"), 16)
            sp.wait_ge(S("l0_mm_done"), 1)
            sp.wait_ge(S("wd_ready"), 3)
            for r in range(4):
                sp.dma_start(wring[:, r], w1_in[:, r]).then_inc(S(f"wr_in{r}"), 16)
            sp.dma_start(w2, w2_in).then_inc(S("w2_in"), 16)
            def store_rows(r, j):
                sp.wait_ge(S("y_act"), r + 1)
                sp.wait_ge(S("y_dve"), r + 1)
                sp.dma_start(table[ds(r, 1)].rearrange("r (p s) n -> p (r s) n", s=NT),
                             ystage[:, j % 2]).then_inc(S(f"y_stored{j % 2}"), 16)

            with sp.Fori(0, R // 4 - 1) as i:
                for j in range(4):
                    store_rows(i * 4 + j, j)
                    sp.wait_ge(S("y_mm"), i * 4 + j + 1)
                    sp.dma_start(wring[:, j], w1_in[:, ds(i * 4 + j + 4, 1)].rearrange("p r c n -> p (r c) n")
                                 ).then_inc(S(f"wr_in{j}"), 16)
            for j in range(4):
                store_rows(R - 4 + j, j)
            for j in range(2):
                sp.wait_ge(S(f"y_stored{j}"), 16 * R // 2)
            sp.sem_inc(S("table_ready"), 1)
            sp.wait_ge(S("lo_ready"), ET)
            sp.dma_start(w3, w3_in).then_inc(S("w3_in"), 16)
            sp.dma_start(rows_late, rows_in[EARLY:NROW].partition_broadcast(128)).then_inc(S("rows_late_in"), 16)
            sp.wait_ge(S("out_ready"), 1)
            sp.dma_start(out.rearrange("(s p) f -> p s f", p=T), x[:, :, :]).then_inc(S("out_done"), 16)
            sp.wait_ge(S("out_done"), 16)

        @block.gpsimd
        def _(pool):
            pool.iota(iota[:, :], pattern=[[1, N]], base=0, channel_multiplier=0,
                      allow_small_or_imprecise_dtypes=True).then_inc(S("iota_ready"), 1)
            pool.iota(pcol[:, :], pattern=[[1, 1]], base=0, channel_multiplier=1,
                      allow_small_or_imprecise_dtypes=True).then_inc(S("iota_ready"), 1)
            pool.iota(ncol[:, :], pattern=[[T, NT]], base=0, channel_multiplier=1,
                      allow_small_or_imprecise_dtypes=True).then_inc(S("iota_ready"), 1)
            pool.memset(zero[:, :], 0.0).then_inc(S("zero_ready"), 1)
            pool.memset(ones[:, :], 1.0).then_inc(S("ones_ready"), 1)
            pool.wait_ge(S("idx_ready"), 1)
            pool.wait_ge(S("table_ready"), 1)
            for t in range(ET):
                if t >= GR:
                    pool.wait_ge(S("lo_ready"), t - GR + 1)
                pool.indirect_dma_start(gath[t % GR], None, table.rearrange("r n f -> (r n) f"),
                                        bass.IndirectOffsetOnAxis(idx[:, t:t + 1], 0)
                                        ).then_inc(S(f"gathered{t % GR // GG}"), 16)
            for s in POOL_TILES:
                pool.wait_ge(S(f"e_exp{s}"), 1)
                pool.tensor_tensor(P[:, s], P[:, s], CT[:, s:s + 1].to_broadcast([T, NH, N]), ALU.mult
                                   ).then_inc(S("p_pool"), 1)
            for n in range(NS):
                for c in range(C):
                    k = C * n + c
                    pool.wait_ge(S("scanned"), k + 1)
                    pool.wait_ge(S("C_ready"), n + 1)
                    if k >= 2:
                        pool.wait_ge(S("y_added"), k - 1)
                    pool.tensor_tensor(hc[:, c], hs[:, c], Cs[:, n % 2], ALU.mult).then_inc(S("hc_ready"), 1)

        @block.scalar
        def _(act):
            count = [0]

            def link(ins):
                count[0] += 1
                ins.then_inc(S("act_chain"), 1)
                act.wait_ge(S("act_chain"), count[0])

            def norm_sqrt(k):
                act.wait_ge(S("var_ready"), k)
                act.activation(sd[:, :], ve[:, :], ACT.Sqrt).then_inc(S("std_ready"), 1)

            norm_sqrt(1)
            act.wait_ge(S("tr_done"), 1)
            for c in range(C):
                act.activation(hTs[0][:, c], PS[:, 2 * c * BANK:2 * c * BANK + 640]
                               .rearrange("p (s n) -> p s n", s=NT)[:, :, 0:T], ACT.Relu).then_inc(S("hT_ready"), 1)
            act.wait_ge(S("adjacency_done"), 1)
            act.activation(squares(CTf, 0, 12), adjacency(0, 12), ACT.Copy).then_inc(S("CT_act"), 1)
            for l in range(3):
                act.wait_ge(S("g_mm"), l + 1)
                act.activation(g, nat_all(0), ACT.Copy).then_inc(S("g_ready"), 1)
                for c in range(C):
                    act.wait_ge(S("pre_masked"), C * l + c + 1)
                    act.activation(hTs[l + 1][:, c], tmp[:, c], ACT.Relu).then_inc(S("hT_ready"), 1)

            def relu_transposed(k, dst):
                act.wait_ge(S("tr_done"), k)
                for c in range(C):
                    act.activation(dst[:, c], PS[:, 2 * c * BANK:2 * c * BANK + 640]
                                   .rearrange("p (s n) -> p s n", s=NT)[:, :, 0:T], ACT.Relu
                                   ).then_inc(S("hT_ready"), 1)

            norm_sqrt(2)
            relu_transposed(2, hT)
            act.wait_ge(S("gate_mm"), 1)
            act.activation(gate, PS[0:T, 6 * BANK:6 * BANK + NT * R].rearrange("p (s r) -> p s r", s=NT),
                           ACT.Sigmoid).then_inc(S("gate_ready"), 1)
            act.wait_ge(S("gate_ready"), 1)
            with act.Fori(0, R // 2) as i:
                for j in range(2):
                    r = i * 2 + j
                    act.wait_ge(S("y_mm"), r + 1)
                    act.wait_ge(S(f"y_stored{j}"), 16 * i)
                    for s in range(2):
                        last = act.activation(ystage[:, j, s], nat(3 * j, s), ACT.Copy,
                                              scale=gate[:, s, ds(r, 1)])
                    last.then_inc(S("y_act"), 1)

            act.wait_ge(S("adjacency_done"), 2)
            act.activation(squares(AwTf, 0, 12), adjacency(0, 12), ACT.Copy).then_inc(S("AwT_act"), 1)
            act.wait_ge(S("edgew_in"), 16)
            with act.Fori(0, ET // GR) as i:
                for j in range(GR):
                    t = i * GR + j
                    if j % GG == 0:
                        act.wait_ge(S(f"gathered{j // GG}"), 16 * GG * (i + 1))
                    act.wait_ge(S("split_free"), t + 1)
                    act.activation(hilo[j % RING][:, 0], gath[j], ACT.Copy, scale=edgew[:, 1, ds(t, 1)]
                                   ).then_inc(S("hi_ready"), 1)
            act.wait_ge(S("keyB_mm"), 1)
            act.activation(keyB.rearrange("p (s n) -> p s n", s=NT), keyB_ps, ACT.Copy).then_inc(S("keyB_ready"), 1)
            norm_sqrt(3)
            relu_transposed(3, hT)
            act.wait_ge(S("q_mm"), 1)
            act.activation(qT, tr(4, 0), ACT.Relu, bias=pc("bp")).then_inc(S("qT_ready"), 1)
            act.wait_ge(S("qT_ready"), 1)
            act.activation(hpT, qT, ACT.Square).then_inc(S("hpT_ready"), 1)
            act.wait_ge(S("hpn_mm"), 1)
            act.activation(hpn, PS[0:T, 6 * BANK:6 * BANK + NT * Q].rearrange("p (s n) -> p s n", s=NT), ACT.Copy
                           ).then_inc(S("hpn_ready"), 1)
            act.wait_ge(S("agg2_mm"), 1)
            act.activation(aggT, tr(0, 0), ACT.Sqrt).then_inc(S("aggT_ready"), 1)
            act.wait_ge(S("keyB_mm"), 2)
            act.activation(rankB.rearrange("p (s n) -> p s n", s=NT), keyB_ps, ACT.Copy).then_inc(S("rankB_ready"), 1)
            norm_sqrt(4)
            relu_transposed(4, hT)
            act.wait_ge(S("proj_mm"), 1)
            act.activation(projn[:, :, :, 0:FH], nat_all(4).rearrange("p s (h f) -> p s h f", h=NH), ACT.Copy
                           ).then_inc(S("projn_ready"), 1)
            act.wait_ge(S("projT_mm"), 1)
            for c in range(C):
                act.activation(projT[:, c], tr(0, c), ACT.Copy).then_inc(S("projT_ready"), 1)
            act.wait_ge(S("stgt_mm"), 1)
            act.activation(stgt, PS[0:T, 0:NH * N].rearrange("p (h n) -> p h n", h=NH), ACT.Copy
                           ).then_inc(S("stgt_ready"), 1)
            act.wait_ge(S("stgt_ready"), 1)
            act.wait_ge(S("ssrc_ready"), 1)

            def add_source(s):
                if s >= 2:
                    act.wait_ge(S("max_done"), s - 1)
                for h in range(NH):
                    last = act.activation(V[:, s % 2, h], stgt[:, h], ACT.Identity, bias=ssrc[:, s, h:h + 1])
                last.then_inc(S("v_ready"), 1)

            add_source(0)
            add_source(1)
            act.wait_ge(S("xs_mm"), 1)
            for c in range(C):
                act.activation(xsT[:, c], tr(4, c), ACT.Copy).then_inc(S("xsT_ready"), 1)
            add_source(2)
            act.wait_ge(S("in_mm"), 1)
            for c in range(C):
                act.activation(xcp[:, c, 3:3 + N], tr(0, c), ACT.Copy).then_inc(S("xcp_ready"), 1)
            add_source(3)
            for c in range(C):
                act.activation(zT[:, c], tr(4, c), ACT.Silu).then_inc(S("zT_ready"), 1)
            add_source(4)
            for c in range(C):
                act.wait_ge(S("conv_done"), c + 1)
                act.activation(xc[:, c], xc[:, c], ACT.Silu, bias=pc("conv_b", c)).then_inc(S("xc_ready"), 1)
            act.wait_ge(S("dbc_mm"), 1)
            act.activation(dbc, tr(4, 0, DB), ACT.Copy).then_inc(S("dbc_ready"), 1)
            act.activation(Aneg[:, :, :], pcols[:, PC["A_log"]:PC["A_log"] + C * NS]
                           .rearrange("p (c n) -> p c n", c=C), ACT.Exp).then_inc(S("A_exp"), 1)
            act.wait_ge(S("gm_ready"), 1)
            for s in (0, 1, 3, 2, 4):
                act.activation(P[:, s], P[:, s], ACT.Exp, bias=gm).then_inc(S(f"e_exp{s}"), 1)
            act.wait_ge(S("sp_abs"), 1)
            act.activation(hs, dBx, ACT.Exp, scale=-1.0).then_inc(S("sp_exp"), 1)
            act.wait_ge(S("sp_w"), 1)
            act.activation(Cs, hc, ACT.Ln).then_inc(S("sp_ln"), 1)
            act.wait_ge(S("elu_in"), 1)
            act.activation(sb_, sb_, ACT.Exp).then_inc(S("elu_exp"), 1)
            norm_sqrt(5)
            act.wait_ge(S("dt_ready"), 1)
            act.wait_ge(S("A_ready"), 1)
            for n in range(NS):
                for c in range(C):
                    k = C * n + c
                    if k >= 2 * C:
                        act.wait_ge(S("scanned"), k - 2 * C + 1)
                    act.activation(dA[:, n % 2, c], dt[:, c], ACT.Exp, scale=Aneg[:, c, n:n + 1]
                                   ).then_inc(S("dA_ready"), 1)
                act.wait_ge(S("B_mm"), n + 1)
                if n >= 2:
                    act.wait_ge(S("scanned"), C * (n - 1))
                act.activation(Bs[:, n % 2], tr(0, 0), ACT.Copy).then_inc(S("B_ready"), 1)
                act.wait_ge(S("C_mm"), n + 1)
                if n >= 2:
                    act.wait_ge(S("hc_ready"), C * (n - 1))
                act.activation(Cs[:, n % 2], tr(2, 0), ACT.Copy).then_inc(S("C_ready"), 1)
            act.wait_ge(S("yn_mm"), 1)
            act.activation(yn, nat_all(0), ACT.Copy).then_inc(S("yn_ready"), 1)
            norm_sqrt(6)
            for k, dst in ((5, hlT), (6, haT)):
                act.wait_ge(S("tr_done"), k)
                for c in range(C):
                    act.activation(dst[:, c], PS[:, 2 * c * BANK:2 * c * BANK + 640]
                                   .rearrange("p (s n) -> p s n", s=NT)[:, :, 0:T], ACT.Copy
                                   ).then_inc(S("hT_ready"), 1)
            act.wait_ge(S("g2_mm"), 1)
            act.activation(gt, nat_all(4), ACT.Sigmoid).then_inc(S("gt_ready"), 1)
            act.wait_ge(S("tr_done"), 7)
            for c in range(C):
                act.activation(hfT[:, c], PS[:, 2 * c * BANK:2 * c * BANK + 640]
                               .rearrange("p (s n) -> p s n", s=NT)[:, :, 0:T], ACT.Copy
                               ).then_inc(S("hT_ready"), 1)
            for m in range(2 * C):
                act.wait_ge(S("ff1_mm"), m + 1)
                act.activation(f1T[:, m], tr(0, m), ACT.Relu, bias=pc("ff1_b", m)).then_inc(S("f1_ready"), 1)
            norm_sqrt(7)

        @block.tensor
        def _(pe):
            mm = pe.matmul

            def transposes(src, k):
                for c in range(C):
                    for s in range(NT):
                        last = pe.transpose(PS[:, 2 * c * BANK + 128 * s:2 * c * BANK + 128 * s + T],
                                            src[:, s, 128 * c:128 * c + 128], ident[0:T, 0:T])
                last.then_inc(S("tr_done"), 1)

            def wide(out_at, rows_, ops, last_sem=None):
                for lo, hi in pieces(out_at, out_at + N):
                    for i, (l, r) in enumerate(ops):
                        last = mm(PS[0:rows_, lo:hi], l, r[:, lo - out_at:hi - out_at],
                                  start=i == 0, stop=i == len(ops) - 1)
                return last

            pe.wait_ge(S("ident_ready"), 1)
            pe.wait_ge(S("edgef_ready"), 1)
            pe.transpose(PS[0:ET, 7 * BANK:7 * BANK + T], edgef[:, 1], ident[0:T, 0:T]).then_inc(S("targets_mm"), 1)
            pe.wait_ge(S("hn_ready"), 1)
            transposes(hn, 1)
            pe.wait_ge(S("hT_ready"), 2)

            pe.wait_ge(S("span_ready"), 1)
            for k in range(2):
                last = pe.transpose(PS[0:1, 7 * BANK + 128 * k:7 * BANK + 128 * k + ET], span[:, k:k + 1],
                                    ident[0:ET, 0:ET])
            last.then_inc(S("spans_mm"), 1)
            pe.wait_ge(S("reached_ready"), 1)
            reached_reg = [pe.alloc_register(f"reached{d}") for d in range(NT)]

            def load_reached(i):
                pe.load(reached_reg, reached[0:1, ds(i, 1)])

            def clear(banks, rows_):
                for b in banks:
                    mm(PS[0:T, b * BANK:(b + 1) * BANK], zero[0:T, :], iota[0:T, 0:BANK], start=True, stop=False,
                       skip_group_check=True)

            def close(at_):
                return mm(PS[0:T, at_:at_ + 16], zero[0:T, :], iota[0:T, 0:16], start=False, stop=False,
                          skip_group_check=True)

            def add_edges(i, u, sources):
                load_reached(i * 2 + u)
                for d in range(NT):
                    with pe.If_ne(reached_reg[d], 0):
                        for j in range(GT):
                            onehot = ohd[:, ds(i * (2 * GT * N) + ((GT * u + j) * N + d * T), T)]
                            for s in range(NT):
                                at_ = d * 128 + s * 640
                                for src_ in sources[j]:
                                    mm(PS[0:T, at_:at_ + T], src_[:, s * T:s * T + T], onehot, start=False,
                                       stop=False, skip_group_check=True)

            pe.wait_ge(S("zero_ready"), 1)
            clear(range(7), T)
            pe.sem_inc(S("ohs_used"), RING)
            with pe.Fori(0, GROUPS // 2) as i:
                for u in range(2):
                    pe.wait_ge(S("onehots"), 2 * GT * (i * 2 + u + 1))
                    add_edges(i, u, [[ohs[:, GT * u + j]] for j in range(GT)])
                    close(0).then_inc(S("ohs_used"), GT)
            close(0).then_inc(S("adjacency_done"), 1)
            pe.wait_ge(S("CT_act"), 1)
            pe.wait_ge(S("CT_dve"), 1)
            pe.wait_ge(S("ones_ready"), 1)
            wide(0, 128, [(ones[0:T, :].to_broadcast([T, 128]), CT[:, s]) for s in range(NT)]).then_inc(S("cnt_mm"), 1)
            pe.wait_ge(S("w0_in"), 16)
            pe.wait_ge(S("cnt_used"), 1)
            for l in range(3):
                h, w = hTs[l], wl0[l]
                if l:
                    pe.wait_ge(S("hT_ready"), 2 + C * l)
                for s in range(NT):
                    for c in range(C):
                        last = mm(nat(0, s), h[:, c, s * T:s * T + T], w[:, 2 + c], start=c == 0, stop=c == C - 1)
                last.then_inc(S("g_mm"), 1)
                pe.wait_ge(S("wd_ready"), l + 1)
                pe.wait_ge(S("g_ready"), l + 1)
                pe.wait_ge(S("CTn_ready"), 1)
                for m in range(C):
                    wide((3 + 2 * m) * BANK, 128,
                         [(w[:, c, 128 * m:128 * m + 128], h[:, c]) for c in range(C)] +
                         [(g[:, s, 128 * m:128 * m + 128], CTn[:, s]) for s in range(NT)]
                         ).then_inc(S("pre_mm"), 1)
            pe.wait_ge(S("hT_ready"), 8)
            for s in range(NT):
                for k in range(4 * C):
                    last = mm(nat(0, s), hTs[k // C][:, k % C, s * T:s * T + T], wf[:, k],
                              start=k == 0, stop=k == 4 * C - 1)
            last.then_inc(S("l0_mm_done"), 1)
            pe.wait_ge(S("hn_ready"), 2)
            transposes(hn, 2)
            pe.wait_ge(S("hT_ready"), 10)
            pe.wait_ge(S("gw_in"), 16)

            def spread(c, s):
                return hT[:, c].rearrange("p (n s) -> p s n", s=NT)[:, s]

            for s in range(NT):
                for c in range(C):
                    last = mm(PS[0:T, 6 * BANK + s * R:6 * BANK + s * R + R], spread(c, s), gw[:, c],
                              start=c == 0, stop=c == C - 1)
            last.then_inc(S("gate_mm"), 1)
            def relation(i, j, first):
                pe.wait_ge(S(f"wr_in{j}"), 16 * (i + 1))
                if not first:
                    pe.wait_ge(S("y_act"), i * 4 + j - 1)
                    pe.wait_ge(S("y_dve"), i * 4 + j - 1)
                for s in range(NT):
                    for c in range(C):
                        last = mm(nat(3 * (j % 2), s), spread(c, s), wring[:, j, c], start=c == 0, stop=c == C - 1)
                last.then_inc(S("y_mm"), 1)

            for j in range(4):
                relation(0, j, j < 2)
            with pe.Fori(1, R // 4) as i:
                for j in range(4):
                    relation(i, j, False)
            pe.wait_ge(S("y_act"), R)
            pe.wait_ge(S("y_dve"), R)
            clear(range(7), T)
            pe.sem_inc(S("wohs_used"), RING)
            with pe.Fori(0, GROUPS // 2) as i:
                for u in range(2):
                    pe.wait_ge(S("wonehots"), GT * (i * 2 + u + 1))
                    add_edges(i, u, [[wohs[GT * u + j][:, k] for k in range(2)] for j in range(GT)])
                    close(0).then_inc(S("wohs_used"), GT)
            close(0).then_inc(S("adjacency_done"), 1)
            pe.wait_ge(S("AwT_act"), 1)
            pe.wait_ge(S("AwT_dve"), 1)

            clear(range(3), T)
            pe.sem_inc(S("split_free"), RING)
            with pe.Fori(0, GROUPS // 2) as i:
                for u in range(2):
                    load_reached(i * 2 + u)
                    pe.wait_ge(S("hi_ready"), GT * (i * 2 + u + 1))
                    pe.wait_ge(S("lo_ready"), GT * (i * 2 + u + 1))
                    for d in range(NT):
                        with pe.If_ne(reached_reg[d], 0):
                            for j in range(GT):
                                for k in range(2):
                                    mm(PS[0:T, d * D:d * D + D],
                                       ohd[:, ds(i * (2 * GT * N) + ((GT * u + j) * N + d * T), T)],
                                       hilo[GT * u + j][:, k], start=False, stop=False, skip_group_check=True)
                    close(0).then_inc(S("split_free"), GT)

            def along_columns(col):
                for s in range(NT):
                    last = pe.transpose(PS[0:T, 3 * BANK + s * 128:3 * BANK + s * 128 + T],
                                        col[:, s:s + 1].to_broadcast([T, T]), ident[0:T, 0:T])
                last.then_inc(S("keyB_mm"), 1)

            along_columns(key)
            pe.wait_ge(S("keyB_ready"), 1)
            pe.wait_ge(S("hn_ready"), 3)
            transposes(hn, 3)
            pe.wait_ge(S("hT_ready"), 12)
            pe.wait_ge(S("w2_in"), 16)
            wide(4 * BANK, 128, [(w2[:, 128 * c:128 * c + 128], hT[:, c]) for c in range(C)]).then_inc(S("q_mm"), 1)
            pe.wait_ge(S("hpT_ready"), 1)
            for s in range(NT):
                last = pe.transpose(PS[0:T, 6 * BANK + s * Q:6 * BANK + s * Q + Q], hpT[:, s * T:s * T + T],
                                    ident[:, :])
            last.then_inc(S("hpn_mm"), 1)
            pe.wait_ge(S("hpn_ready"), 1)
            wide(0, 128, [(hpn[:, s], AwT[:, s]) for s in range(NT)]).then_inc(S("agg2_mm"), 1)
            pe.wait_ge(S("rank_ready"), 1)
            along_columns(rank)
            pe.wait_ge(S("aggT_ready"), 1)
            for s in range(NT):
                mm(nat(5, s), qT[:, s * T:s * T + T], w2[:, 256:512], start=True, stop=False)
                last = mm(nat(5, s), aggT[:, s * T:s * T + T], w2[:, 512:768], start=False, stop=True)
            last.then_inc(S("l2_mm"), 1)
            pe.wait_ge(S("w3_in"), 16)
            pe.wait_ge(S("rankB_ready"), 1)
            pe.wait_ge(S("hn_ready"), 4)
            transposes(hn, 4)
            pe.wait_ge(S("hT_ready"), 14)
            gatw = W("gat", C * D).rearrange("p (c n) -> p c n", c=C)
            for s in range(NT):
                for c in range(C):
                    last = mm(nat(4, s), hT[:, c, s * T:s * T + T], gatw[:, c], start=c == 0, stop=c == C - 1)
            last.then_inc(S("proj_mm"), 1)
            for m in range(C):
                last = wide(2 * m * BANK, 128, [(gatw[:, c, 128 * m:128 * m + 128], hT[:, c]) for c in range(C)])
            last.then_inc(S("projT_mm"), 1)
            pe.wait_ge(S("projT_ready"), 2)
            pe.wait_ge(S("projn_ready"), 1)
            pe.wait_ge(S("atgt_ready"), 1)
            for h in range(NH):
                a = atgt[:, h:h + 1].to_broadcast([128, T])
                for lo, hi in pieces(h * N, h * N + N):
                    last = mm(PS[0:T, lo:hi], a, projT[:, h // 2, lo - h * N:hi - h * N],
                              start=True, stop=True)
            last.then_inc(S("stgt_mm"), 1)
            pe.wait_ge(S("PT_ready"), 1)
            pe.wait_ge(S("hn16_ready"), 1)
            pe.wait_ge(S("stgt_ready"), 1)
            for m in range(C):
                last = wide((4 + 2 * m) * BANK, 128, [(hn16[:, k, s, 128 * m:128 * m + 128], PT[:, s])
                                                      for s in range(NT) for k in range(2)])
            last.then_inc(S("xs_mm"), 1)
            pe.wait_ge(S("xsT_ready"), 2)
            inw = W("in", 2 * C * D).rearrange("p (c n) -> p c n", c=C)
            for m in range(2 * C):
                last = wide(2 * m * BANK, 128, [(inw[:, c, 128 * m:128 * m + 128], xsT[:, c]) for c in range(C)])
            last.then_inc(S("in_mm"), 1)
            pe.wait_ge(S("mx_ready"), 1)
            pe.wait_ge(S("xcp_ready"), 2)
            pe.transpose(PS[0:T, 0:T], m1.to_broadcast([T, T]), ident[0:T, 0:T]).then_inc(S("mxT"), 1)
            pe.wait_ge(S("xc_ready"), 2)
            pe.wait_ge(S("zT_ready"), 2)
            xw = W("x", C * DB).rearrange("p (c n) -> p c n", c=C)
            wide(4 * BANK, DB, [(xw[:, c], xc[:, c]) for c in range(C)]).then_inc(S("dbc_mm"), 1)
            pe.wait_ge(S("dbc_ready"), 1)
            for m in range(C):
                last = wide((4 + 2 * m) * BANK, 128, [(dtw[:, 128 * m:128 * m + 128], dbc[0:RK])])
            last.then_inc(S("dt_mm"), 1)
            pe.wait_ge(S("p_dve"), NT - len(POOL_TILES))
            pe.wait_ge(S("p_pool"), len(POOL_TILES))
            pe.wait_ge(S("dt_read"), 1)
            for d in range(NT):
                for h in range(NH):
                    for s in range(NT):
                        last = mm(PS[0:T, d * BANK + h * 65:d * BANK + h * 65 + 65], P[:, s, h, d * T:d * T + T],
                                  projn[:, s, h], start=s == 0, stop=s == NT - 1)
            last.then_inc(S("att_mm"), 1)
            pe.wait_ge(S("att_used"), 1)
            pe.wait_ge(S("dt_ready"), 1)

            def add_states(n):
                for c in range(C):
                    pe.wait_ge(S("hc_ready"), C * n + c + 1)
                    for lo, hi in pieces(0, N):
                        last = mm(tr(4, c)[:, lo:hi], ident[:, :], hc[:, c, lo:hi],
                                  start=n == 0, stop=n == NS - 1, skip_group_check=True)
                    last.then_inc(S("y_added"), 1)

            for n in range(NS):
                for k, (name, first) in enumerate((("B", RK), ("C", RK + NS))):
                    if n:
                        pe.wait_ge(S(f"{name}_ready"), n)
                    pick = ident[0:DB, first + n:first + n + 1].to_broadcast([DB, 128])
                    wide(2 * k * BANK, 128, [(pick, dbc)]).then_inc(S(f"{name}_mm"), 1)
                if n:
                    add_states(n - 1)
            add_states(NS - 1)
            pe.wait_ge(S("yT_ready"), 1)
            pe.wait_ge(S("B_ready"), NS)
            pe.wait_ge(S("C_ready"), NS)
            ow = W("out", C * D).rearrange("p (c n) -> p c n", c=C)
            for s in range(NT):
                for c in range(C):
                    last = mm(nat(0, s), xc[:, c, s * T:s * T + T], ow[:, c], start=c == 0, stop=c == C - 1)
            last.then_inc(S("yn_mm"), 1)
            pe.wait_ge(S("yn_ready"), 1)
            pe.wait_ge(S("PTt_ready"), 1)
            for d in range(NT):
                for s in range(NT):
                    last = mm(nat(4, d), PTt[:, s, d * T:d * T + T], yn[:, s], start=s == 0, stop=s == NT - 1)
            last.then_inc(S("back_mm"), 1)
            pe.wait_ge(S("hl_ready"), 1)
            transposes(hl, 5)
            pe.wait_ge(S("hT_ready"), 16)
            pe.wait_ge(S("ha_ready"), 1)
            transposes(ha, 6)
            pe.wait_ge(S("hT_ready"), 18)
            wl = W("wl", C * D).rearrange("p (c n) -> p c n", c=C)
            wg = W("wg", C * D).rearrange("p (c n) -> p c n", c=C)
            for s in range(NT):
                ops = [(hlT[:, c], wl[:, c]) for c in range(C)] + [(haT[:, c], wg[:, c]) for c in range(C)]
                for k, (l, r) in enumerate(ops):
                    last = mm(nat(4, s), l[:, s * T:s * T + T], r, start=k == 0, stop=k == 2 * C - 1)
            last.then_inc(S("g2_mm"), 1)
            pe.wait_ge(S("hf_ready"), 1)
            transposes(hf, 7)
            pe.wait_ge(S("hT_ready"), 20)
            w1 = W("ff1", 2 * C * D).rearrange("p (c n) -> p c n", c=C)
            w2_ = W("ff2", 2 * C * D).rearrange("p (c n) -> p c n", c=2 * C)
            for m in range(2 * C):
                wide(2 * m * BANK, 128, [(w1[:, c, 128 * m:128 * m + 128], hfT[:, c]) for c in range(C)]
                     ).then_inc(S("ff1_mm"), 1)
            pe.wait_ge(S("f1_ready"), 2 * C)
            for s in range(NT):
                for k in range(2 * C):
                    last = mm(nat(0, s), f1T[:, k, s * T:s * T + T], w2_[:, k], start=k == 0, stop=k == 2 * C - 1)
            last.then_inc(S("ff2_mm"), 1)

        @block.vector
        def _(dve):
            count = [0]

            def link(ins):
                count[0] += 1
                ins.then_inc(S("dve_chain"), 1)
                dve.wait_ge(S("dve_chain"), count[0])

            def norm(src, dst, k):
                for s in range(NT):
                    last = dve.bn_stats(st[:, s], src[:, s])
                link(last)
                for s in range(NT):
                    last = dve.bn_aggr(mv[:, s], st[:, s])
                link(last)
                dve.tensor_scalar(ve[:, :], mv[:, :, 1], EPS, None, ALU.add).then_inc(S("var_ready"), 1)
                dve.wait_ge(S("std_ready"), k)
                link(dve.reciprocal(rstd[:, :], sd[:, :]))
                link(dve.tensor_tensor(sd[:, :], rstd[:, :], rstd[:, :], ALU.mult))
                link(dve.tensor_tensor(sd[:, :], sd[:, :], ve[:, :], ALU.mult))
                link(dve.tensor_scalar(sd[:, :], sd[:, :], -0.5, 1.5, ALU.mult, ALU.add))
                link(dve.tensor_tensor(rstd[:, :], rstd[:, :], sd[:, :], ALU.mult))
                for s in range(NT):
                    last = dve.tensor_scalar(dst[:, s], src[:, s], mv[:, s, 0:1], rstd[:, s:s + 1],
                                             ALU.subtract, ALU.mult)
                return last

            dve.wait_ge(S("iota_ready"), 3)
            dve.tensor_scalar(ident[:, :], iota[:, 0:128], pcol[:, 0:1], None, ALU.is_equal
                              ).then_inc(S("ident_ready"), 1)
            dve.wait_ge(S("edges_in"), 16)
            dve.tensor_copy(edgef[:, :, :], edgei[:, :, :]).then_inc(S("edgef_ready"), 1)
            dve.wait_ge(S("edgef_ready"), 1)
            dve.wait_ge(S("targets_mm"), 1)
            dve.tensor_reduce(span[:, 0:1], PS[0:ET, 7 * BANK:7 * BANK + T], AX_X, ALU.min)
            dve.tensor_reduce(span[:, 1:2], PS[0:ET, 7 * BANK:7 * BANK + T], AX_X, ALU.max
                              ).then_inc(S("span_ready"), 1)
            dve.wait_ge(S("x_in"), 16)
            norm(x, hn, 1).then_inc(S("hn_ready"), 1)
            dve.wait_ge(S("spans_mm"), 1)
            for k, op in enumerate((ALU.min, ALU.max)):
                link(dve.tensor_reduce(spans[:, k], PS[0:1, 7 * BANK + 128 * k:7 * BANK + 128 * k + ET]
                                       .rearrange("p (g j) -> p g j", j=GT), AX_X, op))
            for d in range(NT):
                link(dve.tensor_scalar(spans[:, 2], spans[:, 0], float(T * (d + 1)), None, ALU.is_lt))
                link(dve.scalar_tensor_tensor(reached[:, :, d], spans[:, 1], float(T * d), spans[:, 2],
                                              ALU.is_ge, ALU.mult))
            dve.sem_inc(S("reached_ready"), 1)
            link(dve.tensor_scalar(idxf, edgef[:, 2], float(N), None, ALU.mult))
            link(dve.tensor_tensor(idxf, idxf, edgef[:, 0], ALU.add))
            dve.tensor_copy(idx[:, :], idxf).then_inc(S("idx_ready"), 1)
            with dve.Fori(0, ET // RING) as i:
                for j in range(RING):
                    t = i * RING + j
                    dve.tensor_scalar(ohd[:, ds(t * N, N)], iota[0:T, :], edgef[:, 1, ds(t, 1)], None, ALU.is_equal
                                      ).then_inc(S("onehots"), 1)
                    dve.wait_ge(S("ohs_used"), t + 1)
                    dve.tensor_scalar(ohs[:, j], iota[0:T, :], edgef[:, 0, ds(t, 1)], None, ALU.is_equal
                                      ).then_inc(S("onehots"), 1)
            dve.wait_ge(S("w0_in"), 16)
            for l in range(3):
                dve.tensor_tensor(wl0[l][:, 0:2], wl0[l][:, 0:2], wl0[l][:, 2:4], ALU.subtract
                                  ).then_inc(S("wd_ready"), 1)
            dve.wait_ge(S("adjacency_done"), 1)
            dve.tensor_copy(squares(CTf, 12, 25), adjacency(12, 25)).then_inc(S("CT_dve"), 1)
            dve.wait_ge(S("cnt_mm"), 1)
            link(dve.tensor_scalar(rcB, tr(0, 0), 1.0, None, ALU.max))
            dve.tensor_scalar(zB, tr(0, 0), 1.0, None, ALU.min).then_inc(S("cnt_used"), 1)
            link(dve.reciprocal(rcB, rcB))
            dve.wait_ge(S("CT_dve"), 1)
            dve.tensor_tensor(CTn, CT[:, :, :], A1[0:T, 12650:12650 + N].rearrange("p (s n) -> p s n", s=1)
                              .to_broadcast([T, NT, N]), ALU.mult).then_inc(S("CTn_ready"), 1)
            link(dve.tensor_reduce(deg[:, :], CT[:, :, :], AX_X, ALU.add))
            dve.wait_ge(S("noise_in"), 16)
            link(dve.tensor_tensor(key[:, :], deg[:, :], noise_sb[:, :], ALU.add))
            dve.wait_ge(S("rows_in"), 16)
            link(dve.tensor_tensor(x[:, :, :], x[:, :, :], row("bf"), ALU.add))
            dve.wait_ge(S("params_in"), 32)
            dve.tensor_scalar(half[:, 0:1], pcol[:, :], float(FH), None, ALU.is_lt)
            link(dve.tensor_scalar(half[:, 1:2], pcol[:, :], float(FH), None, ALU.is_ge))
            for c in range(C):
                last = dve.tensor_scalar(atgt[:, 2 * c:2 * c + 2], half[:, :], pc("a_tgt", c), None, ALU.mult)
            last.then_inc(S("atgt_ready"), 1)
            for l in range(3):
                for c in range(C):
                    dve.wait_ge(S("pre_mm"), C * l + c + 1)
                    if l:
                        dve.wait_ge(S("hT_ready"), C * l + c + 1)
                    dve.scalar_tensor_tensor(tmp[:, c], tr(3, c), pc(f"b{l}", c), zB, ALU.add, ALU.mult
                                             ).then_inc(S("pre_masked"), 1)
            dve.wait_ge(S("l0_mm_done"), 1)
            link(dve.tensor_tensor(x[:, :, :], x[:, :, :], nat_all(0), ALU.add))
            norm(x, hn, 2).then_inc(S("hn_ready"), 1)
            dve.wait_ge(S("gate_ready"), 1)
            with dve.Fori(0, R // 2) as i:
                for j in range(2):
                    r = i * 2 + j
                    dve.wait_ge(S("y_mm"), r + 1)
                    dve.wait_ge(S(f"y_stored{j}"), 16 * i)
                    dve.tensor_tensor(ystage[:, j, 2:5], nat_all(3 * j)[:, 2:5],
                                      gate[:, 2:5, ds(r, 1)].to_broadcast([T, 3, D]), ALU.mult
                                      ).then_inc(S("y_dve"), 1)

            dve.wait_ge(S("edgew_in"), 16)
            for j in range(2):
                dve.wait_ge(S(f"y_stored{j}"), 16 * R // 2)
            link(dve.tensor_copy(wsplit16, edgew[:, 0]))
            link(dve.tensor_copy(wsplit[:, 0], wsplit16))
            link(dve.tensor_tensor(wsplit[:, 1], edgew[:, 0], wsplit[:, 0], ALU.subtract))
            with dve.Fori(0, ET // RING) as i:
                for j in range(RING):
                    t = i * RING + j
                    dve.wait_ge(S("wohs_used"), t + 1)
                    for k in range(2):
                        last = dve.tensor_scalar(wohs[j][:, k], iota[0:T, :], edgef[:, 0, ds(t, 1)],
                                                 wsplit[:, k, ds(t, 1)], ALU.is_equal, ALU.mult)
                    last.then_inc(S("wonehots"), 1)
            dve.wait_ge(S("adjacency_done"), 2)
            dve.tensor_copy(squares(AwTf, 12, 25), adjacency(12, 25)).then_inc(S("AwT_dve"), 1)
            with dve.Fori(0, ET // GR) as i:
                for j in range(GR):
                    t = i * GR + j
                    dve.wait_ge(S("hi_ready"), t + 1)
                    dve.scalar_tensor_tensor(hilo[j % RING][:, 1], gath[j], edgew[:, 1, ds(t, 1)], hilo[j % RING][:, 0],
                                             ALU.mult, ALU.subtract).then_inc(S("lo_ready"), 1)
            dve.wait_ge(S("split_free"), RING + ET)
            link(dve.scalar_tensor_tensor(x[:, :, :], nat_all(0), 0.0, x[:, :, :], ALU.max, ALU.add))
            norm(x, hn, 3).then_inc(S("hn_ready"), 1)
            dve.wait_ge(S("keyB_ready"), 1)
            for s in range(NT):
                link(dve.tensor_scalar(low, iota[0:T, :], ncol[0:T, s:s + 1], None, ALU.is_lt))
                link(dve.tensor_scalar(junk, keyB, key[:, s:s + 1], None, ALU.is_lt, ALU.add,
                                       accum_out=rank[:, s:s + 1]))
                link(dve.scalar_tensor_tensor(junk, keyB, key[:, s:s + 1], low, ALU.is_equal, ALU.mult,
                                              accum_out=rank2[:, s:s + 1]))
            dve.tensor_tensor(rank[:, :], rank[:, :], rank2[:, :], ALU.add).then_inc(S("rank_ready"), 1)
            link(dve.tensor_tensor(x[:, :, :], x[:, :, :], row("b1"), ALU.add))
            link(dve.tensor_tensor(x[:, :, :], x[:, :, :], row("b2"), ALU.add))
            dve.wait_ge(S("l2_mm"), 1)
            link(dve.tensor_tensor(x[:, :, :], x[:, :, :], nat_all(5), ALU.add))
            link(norm(x, hn, 4))
            dve.tensor_scalar(hn[:, :, :], hn[:, :, :], 0.0, None, ALU.max).then_inc(S("hn_ready"), 1)
            dve.memset(projn[:, :, :, FH:FH + 1], 1.0).then_inc(S("projn_one"), 1)
            dve.wait_ge(S("hn_ready"), 4)
            link(dve.tensor_copy(hn16[:, 0], hn[:, :, :]))
            dve.tensor_tensor(hn16[:, 1], hn[:, :, :], hn16[:, 0], ALU.subtract).then_inc(S("hn16_ready"), 1)
            for s in range(NT):
                last = dve.tensor_scalar(PT[:, s], iota[0:T, :], rank[:, s:s + 1], None, ALU.is_equal)
            last.then_inc(S("PT_ready"), 1)
            dve.tensor_scalar(far, CT[:, :, :], 0.0, FAR, ALU.is_equal, ALU.mult).then_inc(S("far_ready"), 1)
            dve.wait_ge(S("rows_late_in"), 16)
            dve.wait_ge(S("projn_ready"), 1)
            sa4 = sa.rearrange("p s (h f) -> p s h f", h=NH)
            asrc = row("a_src").rearrange("p s (h f) -> p s h f", h=NH)
            link(dve.tensor_tensor(sa4, projn[:, :, :, 0:FH], asrc, ALU.mult))
            dve.tensor_reduce(ssrc, sa4, AX_X, ALU.add).then_inc(S("ssrc_ready"), 1)
            dve.memset(xcp[:, :, 0:3], 0.0).then_inc(S("xpad"), 1)
            dve.wait_ge(S("far_ready"), 1)
            for s in range(NT):
                dve.wait_ge(S("v_ready"), s + 1)
                link(dve.scalar_tensor_tensor(P[:, s], V[:, s % 2], 0.2, V[:, s % 2], ALU.mult, ALU.max))
                dve.tensor_tensor_reduce(out=P[:, s], in0=P[:, s],
                                         in1=far[:, s:s + 1].to_broadcast([T, NH, N]), scale=1.0, scalar=-3.0e38,
                                         op0=ALU.add, op1=ALU.max, accum_out=mx[:, s:s + 1]
                                         ).then_inc(S("max_done"), 1)
            dve.wait_ge(S("max_done"), NT)
            dve.tensor_reduce(m1, mx, AX_X, ALU.max).then_inc(S("mx_ready"), 1)
            dve.wait_ge(S("xpad"), 1)
            for c in range(C):
                dve.wait_ge(S("xcp_ready"), c + 1)
                link(dve.tensor_scalar(xc[:, c], xcp[:, c, 0:N], pc("conv_w", K4 * c), None, ALU.mult))
                for k in range(1, K4):
                    last = dve.scalar_tensor_tensor(xc[:, c], xcp[:, c, k:k + N], pc("conv_w", K4 * c + k), xc[:, c],
                                                    ALU.mult, ALU.add)
                    if k < K4 - 1:
                        link(last)
                last.then_inc(S("conv_done"), 1)
                if c == 0:
                    dve.wait_ge(S("mxT"), 1)
                    link(dve.tensor_reduce(gm, PS[0:T, 0:T], AX_X, ALU.max))
                    dve.tensor_scalar(gm, gm, -1.0, None, ALU.mult).then_inc(S("gm_ready"), 1)
            dve.wait_ge(S("A_exp"), 1)
            dve.tensor_scalar(Aneg[:, :, :], Aneg[:, :, :], -1.0, None, ALU.mult).then_inc(S("A_ready"), 1)
            for s in range(NT):
                if s not in POOL_TILES:
                    dve.wait_ge(S(f"e_exp{s}"), 1)
                    dve.tensor_tensor(P[:, s], P[:, s], CT[:, s:s + 1].to_broadcast([T, NH, N]), ALU.mult
                                      ).then_inc(S("p_dve"), 1)
            dve.wait_ge(S("dt_mm"), 1)
            for c in range(C):
                last = dve.tensor_scalar(dtx[:, c], tr(4, c), pc("dt_b", c), None, ALU.add)
            last.then_inc(S("dt_read"), 1)
            dve.wait_ge(S("dt_read"), 1)
            dve.scalar_tensor_tensor(dBx, dtx, -1.0, dtx, ALU.mult, ALU.max).then_inc(S("sp_abs"), 1)
            link(dve.tensor_scalar(dt, dtx, 0.0, None, ALU.max))
            dve.wait_ge(S("sp_exp"), 1)
            dve.tensor_scalar(hc, hs, 1.0, None, ALU.add).then_inc(S("sp_w"), 1)
            dve.wait_ge(S("sp_w"), 1)
            link(dve.scalar_tensor_tensor(dBx, hc, -1.0, hs, ALU.add, ALU.subtract))
            dve.wait_ge(S("sp_ln"), 1)
            link(dve.scalar_tensor_tensor(Cs, hc, 1.0, Cs, ALU.not_equal, ALU.mult))
            link(dve.tensor_tensor(Cs, Cs, dBx, ALU.subtract))
            link(dve.tensor_tensor(dt, dt, Cs, ALU.add))
            dve.tensor_tensor(dtx, dt, xc, ALU.mult).then_inc(S("dt_ready"), 1)
            dve.wait_ge(S("att_mm"), 1)
            att = PS[0:T, 0:NT * BANK].rearrange("p (s n) -> p s n", s=NT)[:, :, 0:NH * 65] \
                .rearrange("p s (h f) -> p s h f", h=NH)
            link(dve.tensor_scalar(den, att[:, :, :, FH], 1e-16, None, ALU.add))
            link(dve.reciprocal(den, den))
            for s in range(NT):
                last = dve.tensor_tensor(sa4[:, s], att[:, s, :, 0:FH],
                                         den[:, s].rearrange("p (h f) -> p h f", f=1).to_broadcast([T, NH, FH]),
                                         ALU.mult)
            last.then_inc(S("att_used"), 1)
            dve.wait_ge(S("att_used"), 1)
            link(dve.tensor_tensor(sa, sa, hn[:, :, :], ALU.add))
            link(dve.tensor_tensor(sa, sa, row("gat_b"), ALU.add))
            dve.tensor_scalar(sb_, sa, 0.0, None, ALU.min).then_inc(S("elu_in"), 1)
            link(dve.tensor_scalar(sa, sa, 0.0, None, ALU.max))
            dve.wait_ge(S("elu_exp"), 1)
            link(dve.scalar_tensor_tensor(sa, sb_, -1.0, sa, ALU.add, ALU.add))
            link(norm(sa, hl, 5))
            link(dve.tensor_tensor(hl, hl, row("lnl_g"), ALU.mult))
            dve.tensor_tensor(hl, hl, row("lnl_b"), ALU.add).then_inc(S("hl_ready"), 1)
            dve.wait_ge(S("dt_ready"), 1)
            for n in range(NS):
                dve.wait_ge(S("B_ready"), n + 1)
                for c in range(C):
                    last = dve.tensor_tensor(dBx[:, c], dtx[:, c], Bs[:, n % 2], ALU.mult)
                link(last)
                for c in range(C):
                    k = C * n + c
                    dve.wait_ge(S("dA_ready"), k + 1)
                    if n:
                        dve.wait_ge(S("hc_ready"), k - C + 1)
                    dve.tensor_tensor_scan(hs[:, c], dA[:, n % 2, c], dBx[:, c], 0.0, ALU.mult, ALU.add
                                           ).then_inc(S("scanned"), 1)
                dve.wait_ge(S("scanned"), C * (n + 1))
            dve.wait_ge(S("rankB_ready"), 1)
            for s in range(NT):
                last = dve.tensor_scalar(PTt[:, s], rankB, ncol[0:T, s:s + 1], None, ALU.is_equal)
            last.then_inc(S("PTt_ready"), 1)
            dve.wait_ge(S("y_added"), C * NS)
            for c in range(C):
                last = dve.scalar_tensor_tensor(xc[:, c], xc[:, c], pc("D", c), tr(4, c), ALU.mult, ALU.add)
            link(last)
            dve.tensor_tensor(xc, xc, zT, ALU.mult).then_inc(S("yT_ready"), 1)
            dve.wait_ge(S("back_mm"), 1)
            link(dve.tensor_tensor(sa, hn[:, :, :], nat_all(4), ALU.add))
            link(norm(sa, ha, 6))
            link(dve.tensor_tensor(ha, ha, row("lng_g"), ALU.mult))
            dve.tensor_tensor(ha, ha, row("lng_b"), ALU.add).then_inc(S("ha_ready"), 1)
            dve.wait_ge(S("ha_ready"), 1)
            link(dve.tensor_tensor(sa, hl, ha, ALU.subtract))
            dve.wait_ge(S("gt_ready"), 1)
            link(dve.tensor_tensor(sa, sa, gt, ALU.mult))
            dve.tensor_tensor(hf, sa, ha, ALU.add).then_inc(S("hf_ready"), 1)
            dve.wait_ge(S("hf_ready"), 1)
            link(dve.tensor_tensor(sa, hf, row("ff2_b"), ALU.add))
            dve.wait_ge(S("ff2_mm"), 1)
            link(dve.tensor_tensor(sa, sa, nat_all(0), ALU.add))
            link(norm(sa, hl, 7))
            link(dve.tensor_tensor(hl, hl, row("ln2_g"), ALU.mult))
            link(dve.tensor_tensor(hl, hl, row("ln2_b"), ALU.add))
            dve.tensor_tensor(x[:, :, :], x[:, :, :], hl, ALU.add).then_inc(S("out_ready"), 1)


def kernel(x, src, dst, edge_type_16, edge_weight, edge_weight1, node_vec, L1_gnn_weight, L1_gnn_gate_weight, **w):
    import concourse.bacc as bacc
    from concourse.bass_utils import run_bass_kernel_spmd

    f = {k: np.asarray(v) for k, v in w.items()}

    def edges(a):
        return np.asarray(a).reshape(ET, T).T

    def chunks(a):
        a = np.asarray(a)
        return a.reshape(-1, 128, a.shape[1]).transpose(1, 0, 2).reshape(128, -1)

    def vec(name):
        return f[name].reshape(-1, 128).T

    L3 = "L3_gnn_"
    arrays = {
        "x": np.ascontiguousarray(x),
        "edge_int": np.ascontiguousarray(np.stack([edges(src), edges(dst), edges(edge_type_16)], 1)),
        "edge_flt": np.ascontiguousarray(np.stack([edges(edge_weight), edges(edge_weight1)], 1)),
        "noise": np.ascontiguousarray(np.asarray(node_vec).reshape(NT, T).T),
        "pcols": np.ascontiguousarray(np.concatenate(
            [vec("L0_gnn_b0"), vec("L0_gnn_b1"), vec("L0_gnn_b2"), vec("L2_gnn_bp"), chunks(f[L3 + "conv_w"]),
             vec(L3 + "conv_b"), vec(L3 + "dt_proj_b"), chunks(f[L3 + "A_log"]), vec(L3 + "D_param"),
             vec(L3 + "ff1_b"), vec(L3 + "gat_a_tgt")], 1)),
        "rows": np.ascontiguousarray(np.stack(
            [f["L0_gnn_bf"], f["L2_gnn_b1"], f["L2_gnn_b2"], f[L3 + "gat_a_src"].reshape(-1), f[L3 + "gat_b"]] +
            [f[L3 + k] for k in ("ln_local_g", "ln_local_b", "ln_global_g", "ln_global_b", "ln2_g", "ln2_b",
                                 "ff2_b")], 0)),
        "w0": np.ascontiguousarray(np.concatenate([chunks(f["L0_gnn_" + k]) for k in ("W0", "W1", "W2", "Wf")], 1)),
        "w1": np.ascontiguousarray(np.asarray(L1_gnn_weight).reshape(R, C, 128, D).transpose(2, 0, 1, 3)),
        "gw": np.ascontiguousarray(np.asarray(L1_gnn_gate_weight).reshape(R, C, 128).transpose(2, 1, 0)),
        "w2": np.ascontiguousarray(np.concatenate([chunks(f["L2_gnn_" + k].T) for k in ("Wp", "W1", "W2")], 1)),
        "w3": np.ascontiguousarray(np.concatenate(
            [chunks(f[L3 + k].T) for k in ("gat_w", "in_proj_w", "x_proj_w", "out_proj_w", "wl", "wg", "ff1_w",
                                           "ff2_w")], 1)),
        "dtw": np.ascontiguousarray(f[L3 + "dt_proj_w"].T),
    }
    nc = bacc.Bacc("TRN2", target_bir_lowering=False, num_devices=1)
    args = [nc.dram_tensor("in_" + name, a.shape, mybir.dt.from_np(a.dtype), kind="ExternalInput").ap()
            for name, a in arrays.items()]
    out = nc.dram_tensor("out_x", (N, D), F32, kind="ExternalOutput").ap()
    table = nc.dram_tensor("table", (R, N, D), F32, kind="Internal").ap()
    gnn_kernel(nc, *args, out, table)
    return run_bass_kernel_spmd(nc, [{"in_" + k: a for k, a in arrays.items()}], core_ids=[0]).results[0]["out_x"]
```

```python
from contextlib import ExitStack

import numpy as np
import concourse.bass as bass
from concourse import mybir

ALU = mybir.AluOpType
ACT = mybir.ActivationFunctionType
F32 = mybir.dt.float32
F16 = mybir.dt.float16
BF16 = mybir.dt.bfloat16
I32 = mybir.dt.int32
AX_X = mybir.AxisListType.X
ds = bass.ds

N = 625
T = 125
NT = N // T
E = 10000
ET = E // T
D = 256
C = D // 128
R = 16
Q = 128
NH, FH = 4, 64
NS = 16
RK = 16
DB = RK + 2 * NS
K4 = 4
EPS = 1e-5
BANK = 512
FAR = -1.0e30

PC = {}
at = 0
for name, n in [("b0", 2), ("b1", 2), ("b2", 2), ("bp", 1), ("conv_w", 8), ("conv_b", 2), ("dt_b", 2),
                ("A_log", 32), ("D", 2), ("ff1_b", 4), ("a_tgt", 2)]:
    PC[name] = at
    at += n
PCOLS = at
ROW = {name: i for i, name in enumerate(["bf", "b1", "b2", "a_src", "gat_b", "lnl_g", "lnl_b", "lng_g", "lng_b",
                                         "ln2_g", "ln2_b", "ff2_b"])}
NROW = len(ROW)
W0SCALE = 16.0
HALVES = ((0, 0), (0, 1), (1, 0))
WSCALE = 256.0
GT = 4
GROUPS = ET // GT
LOW = NT // 2
UN = 4
MT = 5
MGROUPS = ET // MT
MRING = 4 * MT
RING = 2 * GT
EARLY = 3
X_ROWS = list(range(RK)) * 2 + list(range(RK, DB)) * 3
W3 = {}
at = 0
for name, n in [("gat", C * D), ("in", C * 2 * D), ("out", C * D), ("wl", C * D), ("wg", C * D),
                ("ff1", C * 2 * D), ("ff2", 2 * C * D)]:
    W3[name] = at
    at += n
W3COLS = at


def pieces(lo, hi):
    out = []
    while lo < hi:
        end = min(hi, (lo // BANK + 1) * BANK)
        out.append((lo, end))
        lo = end
    return out


def gnn_kernel(nc, x_in, edge_int, edge_flt, noise, pcols_in, rows_in, w0_in, w1_in, gw_in, w2_in, w3_in, xw_in, dtw_in,
               out, table):
    ctx = ExitStack()
    with ctx:
        def sb(name, shape, dt=F32):
            return ctx.enter_context(nc.sbuf_tensor(name, shape, dt))

        sems = {}

        def S(name):
            if name not in sems:
                sems[name] = ctx.enter_context(nc.semaphore(name))
            return sems[name]

        ident = sb("ident", [128, 128])
        ones = sb("ones", [128, 1], F16)
        iota = sb("iota", [128, N], F16)
        pcol = sb("pcol", [128, 1])
        ncol = sb("ncol", [128, NT])
        edgei = sb("edgei", [T, 3, ET], I32)
        edgef = sb("edgef", [T, 3, ET])
        edgew = sb("edgew", [T, 2, ET])
        idx = sb("idx", [T, ET], I32)
        x = sb("x", [T, NT, D])
        hn = sb("hn", [T, NT, D])
        CT = sb("CT", [T, NT, N])
        CTf = CT[:, :, :].rearrange("p s n -> p (s n)")
        pcols = sb("pcols", [128, PCOLS])
        rows_early = sb("rows_early", [128, EARLY, D])
        key = sb("key", [T, NT])
        noise_sb = sb("noise_sb", [T, NT])
        deg = sb("deg", [T, NT])
        rank = sb("rank", [T, NT])
        rank2 = sb("rank2", [T, NT])
        st = sb("st", [T, NT, 6])
        mv = sb("mv", [T, NT, 2])
        ve = sb("ve", [T, NT])
        sd = sb("sd", [T, NT])
        rstd = sb("rstd", [T, NT])
        small = sb("small", [T, 64])
        dtw = sb("dtw", [RK, D])
        Aneg = sb("Aneg", [128, C, NS])
        half = sb("half", [128, 2])
        atgt = sb("atgt", [128, NH])
        gw_sb = sb("gw_sb", [128, C * R])
        zero = sb("zero", [128, 128], F16)
        pick = sb("pick", [128, 2 * NS], BF16)
        span = sb("span", [ET, 2])
        spans = sb("spans", [1, 3, GROUPS])
        reached = sb("reached", [1, GROUPS, NT + 2], I32)
        A0 = sb("A0", [128, 25000])
        A1 = sb("A1", [128, 19656])
        spans_m = A1[0:1, 19584:19584 + 3 * MGROUPS].rearrange("p (k g) -> p k g", k=3)
        reached_m = A1[0:1, 3072:3072 + MGROUPS * (NT + 2)].bitcast(I32).rearrange("p (g k) -> p g k", g=MGROUPS)
        PS = ctx.enter_context(nc.psum_tensor("PS", [128, 8 * BANK], F32))

        def a0(lo, n, rows_=128):
            return A0[0:rows_, lo:lo + n]

        def a1(lo, n, rows_=128):
            return A1[0:rows_, lo:lo + n]

        def cut(ap, k):
            return ap.rearrange("p (k n) -> p k n", k=k)

        ohd = A0[0:T, 0:ET * N // 2].bitcast(F16)
        w_first, w_last = a1(10120, 3072), a1(13980, 2048)
        w_first16 = A1[:, 0:3072].bitcast(F16).rearrange("p (l k n) -> p l k n", l=3, k=2)
        w_last16 = A1[:, 3072:5120].bitcast(F16).rearrange("p (k n) -> p k n", k=2)
        wl0 = [w_first16[:, l].rearrange("p k (c n) -> p k c n", c=2 * C) for l in range(3)]
        wf = w_last16.rearrange("p k (c n) -> p k c n", c=4 * C)
        hTs = [A1[:, 5120 + 1250 * l:6370 + 1250 * l].bitcast(F16).rearrange("p (k c n) -> p k c n", k=2, c=C)
               for l in range(4)]
        g = A1[0:T, 10120:11400].bitcast(F16).rearrange("p (k s n) -> p k s n", k=2, s=NT)
        ohs = A1[0:T, 17025:17025 + RING * N // 2].bitcast(F16).rearrange("p (j n) -> p j n", j=RING)
        tmp = cut(a1(11400, 1250), C)
        idxf = a1(13900, ET, T)
        rcB = a1(12650, N)
        zB = a1(13275, N)
        CTn = A1[0:T, 13900:17025].bitcast(F16).rearrange("p (k s n) -> p k s n", k=2, s=NT)
        CTn_parts = [((0, 2), cut(a1(17025, 1250, T), 2)), ((2, 4), cut(a1(18275, 1250, T), 2)),
                     ((4, 5), cut(a1(11400, 625, T), 1))]
        wring = a1(0, 2048).rearrange("p (j c n) -> p j c n", j=4, c=C)
        hT = cut(a1(2048, 1250), C)
        gate = a1(3298, NT * R, T).rearrange("p (s r) -> p s r", s=NT)
        ystage = a1(3378, 2 * NT * D, T).rearrange("p (j s n) -> p j s n", j=2, s=NT)
        w16 = [A1[:, 5938 + 512 * j:5938 + 512 * j + 512].bitcast(F16)
                      .rearrange("p (k c n) -> p k c n", k=2, c=C) for j in range(4)]
        hT16 = A1[:, 7986:7986 + 1250].bitcast(F16).rearrange("p (k c s n) -> p k c s n", k=2, c=C, s=NT)
        GR = 40
        GG = 5
        gath = [a1(D * j if j < 8 else 10880 + D * (j - 8), D, T) for j in range(GR)]
        hilo = [A1[0:T, at_ + D * j:at_ + D * j + D].bitcast(F16).rearrange("p (k n) -> p k n", k=2)
                for at_, n in ((3378, 14), (2048, 4), (19072, 2)) for j in range(n)]
        gw = gw_sb[:, :].rearrange("p (c r) -> p c r", c=C)
        AwTf = a1(6962, NT * N, T)
        AwT = cut(AwTf, NT)
        wohs = [A1[0:T, at_ + N * j:at_ + N * j + N].bitcast(F16).rearrange("p (k n) -> p k n", k=2)
                for at_ in (6962, 3378) for j in range(RING // 2)]
        wsplit = cut(a1(9500, 2 * ET, T), 2)
        wsplit16 = a1(9660, ET // 2, T).bitcast(F16)
        keyB = a1(3378, N, T)
        junk = a1(4003, N, T)
        low = a1(4628, N, T)
        rankB = a1(5253, N, T)
        w2 = a1(10087, 768)
        w3 = a1(10880, W3COLS)
        rows_late = a1(16096, (NROW - EARLY) * D).rearrange("p (r n) -> p r n", n=D)
        qT = a1(0, N)
        hpT = a1(625, N)
        hpn = a1(1250, NT * Q, T).rearrange("p (s n) -> p s n", s=NT)
        aggT = a1(625, N)
        P = a0(0, 12500, T).rearrange("p (s h n) -> p s h n", s=NT, h=NH)
        V = a0(12500, 5000, T).rearrange("p (j h n) -> p j h n", j=2, h=NH)
        stgt = a0(17500, 2500, T).rearrange("p (h n) -> p h n", h=NH)
        far = cut(a0(20000, NT * N, T), NT)
        projT = cut(a0(23125, 1250), C)
        projn = a1(0, NT * NH * 65, T).rearrange("p (s h f) -> p s h f", s=NT, h=NH)
        hl = cut(a1(3378, NT * D, T), NT)
        sa = cut(a1(5938, NT * D, T), NT)
        sb_ = hl
        ha = cut(a1(8498, NT * D, T), NT)
        ssrc = small[:, 0:20].rearrange("p (s h) -> p s h", s=NT)
        mx = small[:, 20:25]
        m1 = small[:, 25:26]
        gm = small[:, 26:27]
        den = small[:, 30:50].rearrange("p (s h) -> p s h", s=NT)
        PT = A1[0:T, 7218:7218 + 1563].bitcast(F16)[:, 0:NT * N].rearrange("p (s n) -> p s n", s=NT)
        hn16 = A1[0:T, 8782:8782 + 1280].bitcast(F16).rearrange("p (k s n) -> p k s n", k=2, s=NT)
        xsT = hT
        xcp = cut(a1(18400, 1256), C)
        zT = cut(a0(23125, 1250), C)
        xc = cut(a1(7218, 1250), C)
        dbc = a1(8498, N)
        parts = A0[:, 24632:24632 + 313].bitcast(BF16)[:, 0:N]
        rest = a0(21875, N)
        xw = cut(a0(24375, C * 128), C)
        dt = cut(a0(14375, 1250), C)
        dtx = cut(a1(3378, 1250), C)
        dBx = cut(a0(16875, 1250), 2)
        hs = cut(a0(18125, 1250), 2)
        Cs = cut(a0(19375, 1250), 2)
        hc = cut(a0(20625, 1250), 2)
        Bs = cut(a0(21875, 1250), 2)
        dBxs, hss = [dBx, cut(a0(8200, 1250), C)], [hs, cut(a0(9450, 1250), C)]
        dA = a0(0, 2500).rearrange("p (j c n) -> p j c n", j=2, c=C)
        PTt = cut(a0(2500, NT * N, T), NT)
        yn = cut(a0(5625, NT * D, T), NT)
        attT = a0(5625, NH * N, FH + 1)
        hlT = cut(a0(5400, 1250), C)
        haT = cut(a0(6650, 1250), C)
        hfT = cut(a0(7900, 1250), C)
        f1T = cut(a0(9150, 2500), 2 * C)
        gt = cut(a0(0, NT * D, T), NT)
        hf = cut(a0(1280, NT * D, T), NT)

        def row(name):
            i = ROW[name]
            src = rows_early[:, i:i + 1, :] if i < EARLY else rows_late[:, i - EARLY:i - EARLY + 1, :]
            return src[0:T].to_broadcast([T, NT, D])

        def pc(name, c=0):
            return pcols[:, PC[name] + c:PC[name] + c + 1]

        def W(name, n):
            return w3[:, W3[name]:W3[name] + n]

        def nat(b, s):
            return PS[0:T, b * BANK + s * D:b * BANK + s * D + D]

        def nat_all(b):
            return PS[0:T, b * BANK:b * BANK + NT * D].rearrange("p (s n) -> p s n", s=NT)

        def adjacency(lo, hi):
            return PS[0:T, 128 * lo:128 * hi].rearrange("p (b n) -> p b n", n=128)[:, :, 0:T]

        def squares(flat, lo, hi):
            return flat[:, T * lo:T * hi].rearrange("p (b n) -> p b n", n=T)

        def tr(b, c, rows_=128):
            return PS[0:rows_, (b + 2 * c) * BANK:(b + 2 * c) * BANK + N]

        EXP_ORDER = (0, 1, 3, 2, 4)
        POOL_TILES, DVE_TILES, P_ORDER = (0, 3), (1, 2, 4), (1, 0, 2, 3, 4)
        keyB_ps = PS[0:T, 3 * BANK:3 * BANK + 640].rearrange("p (s n) -> p s n", s=NT)[:, :, 0:T]
        block = ctx.enter_context(nc.Block())

        @block.sync
        def _(sp):
            sp.dma_start(edgei[:, :, :], edge_int).then_inc(S("edges_in"), 16)
            sp.dma_start(x[:, :, :], x_in.rearrange("(s p) f -> p s f", p=T)).then_inc(S("x_in"), 16)
            sp.dma_start(edgew[:, :, :], edge_flt).then_inc(S("edgew_in"), 16)
            sp.dma_start(pcols[:, :], pcols_in).then_inc(S("params_in"), 16)
            sp.dma_start(w_first, w0_in[:, 0:3072]).then_inc(S("w0_in"), 16)
            sp.dma_start(w_last, w0_in[:, 3072:5120]).then_inc(S("w0_in"), 16)
            sp.dma_start(rows_early[:, :, :], rows_in[0:EARLY].partition_broadcast(128)).then_inc(S("rows_in"), 16)
            sp.dma_start(gw_sb[:, :], gw_in).then_inc(S("params_in"), 16)
            sp.dma_start(noise_sb[:, :], noise).then_inc(S("params_in"), 16)
            sp.dma_start(dtw[:, :], dtw_in).then_inc(S("params_in"), 16)
            sp.wait_ge(S("l0_mm_done"), 1)
            for r in range(4):
                sp.dma_start(wring[:, r], w1_in[:, r]).then_inc(S(f"wr_in{r}"), 16)
            sp.dma_start(w2, w2_in).then_inc(S("w2_in"), 16)
            def store_rows(r, j):
                sp.wait_ge(S("y_act"), r + 1)
                sp.wait_ge(S("y_dve"), r + 1)
                sp.dma_start(table[ds(r, 1)].rearrange("r (p s) n -> p (r s) n", s=NT),
                             ystage[:, j % 2]).then_inc(S(f"y_stored{j % 2}"), 16)

            with sp.Fori(0, R // 4 - 1) as i:
                for j in range(4):
                    sp.wait_ge(S("wlow_ready"), i * 4 + j + 1)
                    sp.dma_start(wring[:, j], w1_in[:, ds(i * 4 + j + 4, 1)].rearrange("p r c n -> p (r c) n")
                                 ).then_inc(S(f"wr_in{j}"), 16)
                    store_rows(i * 4 + j, j)
            for j in range(4):
                store_rows(R - 4 + j, j)
            for j in range(2):
                sp.wait_ge(S(f"y_stored{j}"), 16 * R // 2)
            sp.sem_inc(S("table_ready"), 1)
            sp.wait_ge(S("lo_ready"), ET)
            sp.dma_start(w3, w3_in).then_inc(S("w3_in"), 16)
            sp.dma_start(rows_late, rows_in[EARLY:NROW].partition_broadcast(128)).then_inc(S("rows_late_in"), 16)
            sp.wait_ge(S("hn_ready"), 3)
            sp.dma_start(xw, xw_in).then_inc(S("xw_in"), 16)
            sp.wait_ge(S("out_ready"), 1)
            sp.dma_start(out.rearrange("(s p) f -> p s f", p=T), x[:, :, :]).then_inc(S("out_done"), 16)
            sp.wait_ge(S("out_done"), 16)

        @block.gpsimd
        def _(pool):
            pool.iota(iota[:, :], pattern=[[1, N]], base=0, channel_multiplier=0,
                      allow_small_or_imprecise_dtypes=True).then_inc(S("iota_ready"), 1)
            pool.iota(pcol[:, :], pattern=[[1, 1]], base=0, channel_multiplier=1,
                      allow_small_or_imprecise_dtypes=True).then_inc(S("iota_ready"), 1)
            pool.iota(ncol[:, :], pattern=[[T, NT]], base=0, channel_multiplier=1,
                      allow_small_or_imprecise_dtypes=True).then_inc(S("iota_ready"), 1)
            pool.memset(zero[:, :], 0.0).then_inc(S("constants_ready"), 1)
            pool.memset(ones[:, :], 1.0).then_inc(S("constants_ready"), 1)
            pool.wait_ge(S("w0_in"), 32)
            for l in range(3):
                wl = cut(w_first[:, 1024 * l:1024 * l + 1024], 2)
                pool.tensor_tensor(wl[:, 0], wl[:, 0], wl[:, 1], ALU.subtract).then_inc(S("wd_ready"), 1)
            pool.wait_ge(S("w0_high"), 2)
            pool.tensor_tensor(w_first16[:, :, 1], cut(w_first, 3), w_first16[:, :, 0], ALU.subtract
                               ).then_inc(S("w0_low"), 1)
            pool.tensor_tensor(w_last16[:, 1], w_last, w_last16[:, 0], ALU.subtract).then_inc(S("w0_low"), 1)
            pool.wait_ge(S("idx_ready"), 1)
            pool.wait_ge(S("table_ready"), 1)
            for t in range(ET):
                if t >= GR:
                    pool.wait_ge(S("lo_ready"), t - GR + 1)
                pool.indirect_dma_start(gath[t % GR], None, table.rearrange("r n f -> (r n) f"),
                                        bass.IndirectOffsetOnAxis(idx[:, t:t + 1], 0)
                                        ).then_inc(S(f"gathered{t % GR // GG}"), 16)
            for s in POOL_TILES:
                pool.wait_ge(S("e_exp"), EXP_ORDER.index(s) + 1)
                pool.tensor_tensor(P[:, s], P[:, s], CT[:, s:s + 1].to_broadcast([T, NH, N]), ALU.mult
                                   ).then_inc(S("p_pool"), 1)
            pool.wait_ge(S("att_used"), 1)
            pool.tensor_tensor(sa, sa, hn[:, :, :], ALU.add).then_inc(S("sa_sum"), 1)
            pool.wait_ge(S("rows_late_in"), 16)
            pool.wait_ge(S("sa_sum"), 1)
            pool.tensor_tensor(sa, sa, row("gat_b"), ALU.add).then_inc(S("sa_sum"), 1)
            for n in range(NS):
                for c in range(C):
                    k = C * n + c
                    pool.wait_ge(S("scanned"), k + 1)
                    pool.wait_ge(S("C_ready"), n + 1)
                    if k >= 2:
                        pool.wait_ge(S("y_added"), k - 1)
                    pool.tensor_tensor(hc[:, c], hss[n % 2][:, c], Cs[:, n % 2], ALU.mult).then_inc(S("hc_ready"), 1)

        @block.scalar
        def _(act):
            count = [0]

            def link(ins):
                count[0] += 1
                ins.then_inc(S("act_chain"), 1)
                act.wait_ge(S("act_chain"), count[0])

            def norm_sqrt(k):
                act.wait_ge(S("var_ready"), k)
                act.activation(sd[:, :], ve[:, :], ACT.Sqrt).then_inc(S("std_ready"), 1)

            norm_sqrt(1)
            act.wait_ge(S("tr_done"), 1)
            for c in range(C):
                act.activation(hTs[0][:, 0, c], PS[:, 2 * c * BANK:2 * c * BANK + 640]
                               .rearrange("p (s n) -> p s n", s=NT)[:, :, 0:T], ACT.Relu).then_inc(S("hT_ready"), 1)
            act.wait_ge(S("wd_ready"), 3)
            act.activation(w_first, w_first, ACT.Copy, scale=W0SCALE)
            link(act.activation(w_last, w_last, ACT.Copy, scale=W0SCALE))
            act.activation(w_first16[:, :, 0], cut(w_first, 3), ACT.Copy).then_inc(S("w0_high"), 1)
            act.activation(w_last16[:, 0], w_last, ACT.Copy).then_inc(S("w0_high"), 1)
            act.wait_ge(S("adjacency_done"), 1)
            act.activation(squares(CTf, 0, 12), adjacency(0, 12), ACT.Copy).then_inc(S("CT_act"), 1)
            for l in range(3):
                act.wait_ge(S("g_mm"), l + 1)
                act.activation(g[:, 0], nat_all(0), ACT.Copy).then_inc(S("g_ready"), 1)
                if l == 0:
                    for k, ((lo, hi), part) in enumerate(CTn_parts):
                        act.wait_ge(S("CTn_part"), k + 1)
                        act.activation(CTn[:, 0, lo:hi], part, ACT.Copy).then_inc(S("CTn_high"), 1)
                for c in range(C):
                    act.wait_ge(S("pre_masked"), C * l + c + 1)
                    act.activation(hTs[l + 1][:, 0, c], tmp[:, c], ACT.Relu).then_inc(S("hT_ready"), 1)

            def relu_transposed(k, dst):
                act.wait_ge(S("tr_done"), k)
                for c in range(C):
                    act.activation(dst[:, c], PS[:, 2 * c * BANK:2 * c * BANK + 640]
                                   .rearrange("p (s n) -> p s n", s=NT)[:, :, 0:T], ACT.Relu
                                   ).then_inc(S("hT_ready"), 1)

            norm_sqrt(2)
            relu_transposed(2, hT)
            act.wait_ge(S("gate_mm"), 1)
            act.activation(gate, PS[0:T, 6 * BANK:6 * BANK + NT * R].rearrange("p (s r) -> p s r", s=NT),
                           ACT.Sigmoid).then_inc(S("gate_ready"), 1)
            act.wait_ge(S("gate_ready"), 1)
            act.activation(gate, gate, ACT.Copy, scale=1 / WSCALE).then_inc(S("gate_ready"), 1)
            act.wait_ge(S("gate_ready"), 2)

            def high_weights(i, j):
                act.wait_ge(S(f"wr_in{j % 4}"), 16 * (i + j // 4 + 1))
                act.activation(w16[j % 4][:, 0], wring[:, j % 4], ACT.Copy, scale=WSCALE
                               ).then_inc(S("whigh_ready"), 1)

            def two_rows(i, j):
                act.wait_ge(S("y_mm"), i * 4 + j + 1)
                if j >= 2 or not isinstance(i, int) or i:
                    act.wait_ge(S(f"y_stored{j % 2}"), 16 * (i * 2 + j // 2))
                for s in range(2):
                    last = act.activation(ystage[:, j % 2, s], nat(3 * (j % 2), s), ACT.Copy,
                                          scale=gate[:, s, ds(i * 4 + j, 1)])
                last.then_inc(S("y_act"), 1)

            high_weights(0, 0)
            high_weights(0, 1)
            with act.Fori(0, R // 4 - 1) as i:
                for j in range(4):
                    high_weights(i, j + 2)
                    two_rows(i, j)
            for j in range(4):
                if j < 2:
                    high_weights(R // 4 - 1, j + 2)
                two_rows(R // 4 - 1, j)

            act.wait_ge(S("adjacency_done"), 2)
            act.activation(squares(AwTf, 0, 12), adjacency(0, 12), ACT.Copy).then_inc(S("AwT_act"), 1)
            act.wait_ge(S("edgew_in"), 16)
            with act.Fori(0, ET // GR) as i:
                for j in range(GR):
                    t = i * GR + j
                    if j % GG == 0:
                        act.wait_ge(S(f"gathered{j // GG}"), 16 * GG * (i + 1))
                    act.wait_ge(S("split_free"), t + 1)
                    act.activation(hilo[j % MRING][:, 0], gath[j], ACT.Copy, scale=edgew[:, 1, ds(t, 1)]
                                   ).then_inc(S("hi_ready"), 1)
            act.wait_ge(S("keyB_mm"), 1)
            act.activation(keyB.rearrange("p (s n) -> p s n", s=NT), keyB_ps, ACT.Copy).then_inc(S("keyB_ready"), 1)
            norm_sqrt(3)
            relu_transposed(3, hT)
            act.wait_ge(S("q_mm"), 1)
            act.activation(qT, tr(4, 0), ACT.Relu, bias=pc("bp")).then_inc(S("qT_ready"), 1)
            act.wait_ge(S("qT_ready"), 1)
            act.activation(hpT, qT, ACT.Square).then_inc(S("hpT_ready"), 1)
            act.wait_ge(S("hpn_mm"), 1)
            act.activation(hpn, PS[0:T, 6 * BANK:6 * BANK + NT * Q].rearrange("p (s n) -> p s n", s=NT), ACT.Copy
                           ).then_inc(S("hpn_ready"), 1)
            act.wait_ge(S("agg2_mm"), 1)
            act.activation(aggT, tr(0, 0), ACT.Sqrt).then_inc(S("aggT_ready"), 1)
            act.wait_ge(S("keyB_mm"), 2)
            act.activation(rankB.rearrange("p (s n) -> p s n", s=NT), keyB_ps, ACT.Copy).then_inc(S("rankB_ready"), 1)
            norm_sqrt(4)
            relu_transposed(4, hT)
            act.wait_ge(S("proj_mm"), 1)
            act.activation(projn[:, :, :, 0:FH], nat_all(4).rearrange("p s (h f) -> p s h f", h=NH), ACT.Copy
                           ).then_inc(S("projn_ready"), 1)
            act.wait_ge(S("projT_mm"), 1)
            for c in range(C):
                act.activation(projT[:, c], tr(0, c), ACT.Copy).then_inc(S("projT_ready"), 1)
            act.wait_ge(S("stgt_mm"), 1)
            act.activation(stgt, PS[0:T, 0:NH * N].rearrange("p (h n) -> p h n", h=NH), ACT.Copy
                           ).then_inc(S("stgt_ready"), 1)
            act.wait_ge(S("stgt_ready"), 1)
            act.wait_ge(S("ssrc_ready"), 1)

            def add_source(s):
                if s >= 2:
                    act.wait_ge(S("max_done"), s - 1)
                for h in range(NH):
                    last = act.activation(V[:, s % 2, h], stgt[:, h], ACT.Identity, bias=ssrc[:, s, h:h + 1])
                last.then_inc(S("v_ready"), 1)

            add_source(0)
            add_source(1)
            act.wait_ge(S("xs_mm"), 1)
            for c in range(C):
                act.activation(xsT[:, c], tr(4, c), ACT.Copy).then_inc(S("xsT_ready"), 1)
            add_source(2)
            act.wait_ge(S("in_mm"), 1)
            for c in range(C):
                act.activation(xcp[:, c, 3:3 + N], tr(0, c), ACT.Copy).then_inc(S("xcp_ready"), 1)
            add_source(3)
            for c in range(C):
                act.activation(zT[:, c], tr(4, c), ACT.Silu).then_inc(S("zT_ready"), 1)
            add_source(4)
            for c in range(C):
                act.wait_ge(S("conv_done"), c + 1)
                act.activation(xc[:, c], xc[:, c], ACT.Silu, bias=pc("conv_b", c)).then_inc(S("xc_ready"), 1)
            act.wait_ge(S("dbc_mm"), 1)
            act.activation(dbc, PS[:, 5 * BANK:5 * BANK + N], ACT.Copy).then_inc(S("dbc_ready"), 1)
            act.activation(parts, PS[:, 5 * BANK:5 * BANK + N], ACT.Copy).then_inc(S("dbc_ready"), 1)
            act.activation(Aneg[:, :, :], pcols[:, PC["A_log"]:PC["A_log"] + C * NS]
                           .rearrange("p (c n) -> p c n", c=C), ACT.Exp).then_inc(S("A_exp"), 1)
            act.wait_ge(S("gm_ready"), 1)
            for s in EXP_ORDER:
                if s == 1:
                    act.wait_ge(S("sp_abs"), 1)
                    act.activation(hs, dBx, ACT.Exp, scale=-1.0).then_inc(S("sp_exp"), 1)
                act.activation(P[:, s], P[:, s], ACT.Exp, bias=gm).then_inc(S("e_exp"), 1)
            act.wait_ge(S("sp_w"), 1)
            act.activation(Cs, hc, ACT.Ln).then_inc(S("sp_ln"), 1)
            act.wait_ge(S("attT_mm"), 1)
            act.activation(attT, PS[0:FH + 1, 0:NH * N], ACT.Copy).then_inc(S("attT_ready"), 1)
            act.wait_ge(S("dt_ready"), 1)
            act.wait_ge(S("A_ready"), 1)
            for n in range(NS):
                for c in range(C):
                    k = C * n + c
                    if k >= 2 * C:
                        act.wait_ge(S("scanned"), k - 2 * C + 1)
                    act.activation(dA[:, n % 2, c], dt[:, c], ACT.Exp, scale=Aneg[:, c, n:n + 1]
                                   ).then_inc(S("dA_ready"), 1)
                act.wait_ge(S("C_mm"), n + 1)
                if n >= 2:
                    act.wait_ge(S("hc_ready"), C * (n - 1))
                act.activation(Cs[:, n % 2], tr(2, 0), ACT.Copy).then_inc(S("C_ready"), 1)
            act.wait_ge(S("elu_in"), 1)
            act.activation(sb_, sb_, ACT.Exp).then_inc(S("elu_exp"), 1)
            act.wait_ge(S("yn_mm"), 1)
            act.activation(yn, nat_all(0), ACT.Copy).then_inc(S("yn_ready"), 1)
            norm_sqrt(5)
            norm_sqrt(6)
            for k, dst in ((5, hlT), (6, haT)):
                act.wait_ge(S("tr_done"), k)
                for c in range(C):
                    act.activation(dst[:, c], PS[:, 2 * c * BANK:2 * c * BANK + 640]
                                   .rearrange("p (s n) -> p s n", s=NT)[:, :, 0:T], ACT.Copy
                                   ).then_inc(S("hT_ready"), 1)
            act.wait_ge(S("g2_mm"), 1)
            act.activation(gt, nat_all(4), ACT.Sigmoid).then_inc(S("gt_ready"), 1)
            act.wait_ge(S("tr_done"), 7)
            for c in range(C):
                act.activation(hfT[:, c], PS[:, 2 * c * BANK:2 * c * BANK + 640]
                               .rearrange("p (s n) -> p s n", s=NT)[:, :, 0:T], ACT.Copy
                               ).then_inc(S("hT_ready"), 1)
            for m in range(2 * C):
                act.wait_ge(S("ff1_mm"), m + 1)
                act.activation(f1T[:, m], tr(0, m % 2), ACT.Relu, bias=pc("ff1_b", m)).then_inc(S("f1_ready"), 1)
            norm_sqrt(7)

        @block.tensor
        def _(pe):
            mm = pe.matmul

            def transposes(src, k):
                for c in range(C):
                    for s in range(NT):
                        last = pe.transpose(PS[:, 2 * c * BANK + 128 * s:2 * c * BANK + 128 * s + T],
                                            src[:, s, 128 * c:128 * c + 128], ident[0:T, 0:T])
                last.then_inc(S("tr_done"), 1)

            def rows_product(bank, lT, r, first):
                for s in range(NT):
                    last = mm(nat(bank, s), lT[:, s * T:s * T + T], r, start=first and s % 2 == 0, stop=False,
                              skip_group_check=True)
                return last

            def wide(out_at, rows_, ops):
                for lo, hi in pieces(out_at, out_at + N):
                    for i, (l, r) in enumerate(ops):
                        last = mm(PS[0:rows_, lo:hi], l, r[:, lo - out_at:hi - out_at],
                                  start=i == 0, stop=i == len(ops) - 1)
                return last

            pe.wait_ge(S("ident_ready"), 1)
            pe.wait_ge(S("edgef_ready"), 1)
            pe.transpose(PS[0:ET, 7 * BANK:7 * BANK + T], edgef[:, 1], ident[0:T, 0:T]).then_inc(S("targets_mm"), 1)
            pe.wait_ge(S("hn_ready"), 1)
            transposes(hn, 1)
            pe.wait_ge(S("hlow_ready"), 2)

            pe.wait_ge(S("span_ready"), 1)
            for k in range(2):
                last = pe.transpose(PS[0:1, 7 * BANK + 128 * k:7 * BANK + 128 * k + ET], span[:, k:k + 1],
                                    ident[0:ET, 0:ET])
            last.then_inc(S("spans_mm"), 1)
            pe.wait_ge(S("reached_ready"), 1)
            reached_regs = [pe.alloc_register(f"reached{d}") for d in range(UN * (NT + 2))]

            def for_reached(table_, i, u, add):
                if u == 0:
                    pe.load(reached_regs, table_[0:1, ds(i * UN, UN)])
                reached_reg = reached_regs[(NT + 2) * u:]
                for half_, tiles in enumerate((range(LOW), range(LOW, NT))):
                    with pe.If_ne(reached_reg[NT + half_], 0):
                        for d in tiles:
                            with pe.If_ne(reached_reg[d], 0):
                                add(d)

            def clear(banks):
                for b in banks:
                    mm(PS[:, b * BANK:(b + 1) * BANK], zero[0:T, :], iota[0:T, 0:BANK], start=True, stop=False,
                       skip_group_check=True)

            def close(at_):
                return mm(PS[:, at_:at_ + 16], zero[0:T, :], iota[0:T, 0:16], start=False, stop=False,
                          skip_group_check=True)

            def add_edges(i, u, sources, counted=False):
                def add(d):
                    for j in range(GT):
                        onehot = ohd[:, ds(i * (UN * GT * N) + ((GT * u + j) * N + d * T), T)]
                        for s in range(NT):
                            at_ = d * 128 + s * 640
                            for src_ in sources[j]:
                                mm(PS[0:T, at_:at_ + T], src_[:, s * T:s * T + T], onehot, start=False,
                                   stop=False, skip_group_check=True)
                        if counted:
                            mm(PS[:, (NT * NT + d) * 128:(NT * NT + d) * 128 + T], ones[0:T, :].to_broadcast([T, 128]), onehot,
                               start=False, stop=False, skip_group_check=True)

                for_reached(reached, i, u, add)

            pe.wait_ge(S("constants_ready"), 2)
            clear(range(8))
            pe.sem_inc(S("ohs_used"), RING)
            with pe.Fori(0, GROUPS // UN) as i:
                for u in range(UN):
                    pe.wait_ge(S("onehots"), 2 * GT * (i * UN + u + 1))
                    add_edges(i, u, [[ohs[:, (GT * u + j) % RING]] for j in range(GT)], True)
                    close(0).then_inc(S("ohs_used"), GT)
            close(0).then_inc(S("adjacency_done"), 1)
            pe.wait_ge(S("w0_low"), 2)
            pe.wait_ge(S("CT_act"), 1)
            for l in range(3):
                h, w = hTs[l], wl0[l]
                for c in range(C):
                    if l:
                        pe.wait_ge(S("hlow_ready"), C * l + c + 1)
                    for a, b in HALVES:
                        last = rows_product(0, h[:, a, c], w[:, b, 2 + c], c + a + b == 0)
                last.then_inc(S("g_mm"), 1)
                if l == 0:
                    pe.wait_ge(S("CT_dve"), 1)
                    pe.wait_ge(S("cnt_used"), 1)

                def sums(m, ops, first):
                    at_ = (3 + 2 * m) * BANK
                    for lo, hi in pieces(at_, at_ + N):
                        for i, (l_, r) in enumerate(ops):
                            last = mm(PS[:, lo:hi], l_, r[:, lo - at_:hi - at_], start=first and i == 0, stop=False,
                                      skip_group_check=True)
                    return last

                for m in range(C):
                    sums(m, [(w[:, b, c, 128 * m:128 * m + 128], h[:, a, c]) for c in range(C) for a, b in HALVES],
                         True)
                pe.wait_ge(S("glow_ready"), l + 1)
                pe.wait_ge(S("CTn_ready"), len(CTn_parts))
                for m in range(C):
                    sums(m, [(g[:, a, s, 128 * m:128 * m + 128], CTn[:, b, s]) for s in range(NT) for a, b in HALVES],
                         False).then_inc(S("pre_mm"), 1)
            for k in range(4 * C):
                if k >= 3 * C:
                    pe.wait_ge(S("hlow_ready"), k + 1)
                for a, b in HALVES:
                    last = rows_product(0, hTs[k // C][:, a, k % C], wf[:, b, k], k + a + b == 0)
            last.then_inc(S("l0_mm_done"), 1)
            pe.wait_ge(S("hn_ready"), 2)
            transposes(hn, 2)
            pe.wait_ge(S("hT_ready"), 10)
            pe.wait_ge(S("params_in"), 64)

            def spread(c, s):
                return hT[:, c].rearrange("p (n s) -> p s n", s=NT)[:, s]

            for s in range(NT):
                for c in range(C):
                    last = mm(PS[0:T, 6 * BANK + s * R:6 * BANK + s * R + R], spread(c, s), gw[:, c],
                              start=c == 0, stop=c == C - 1)
            last.then_inc(S("gate_mm"), 1)
            pe.wait_ge(S("hT16_ready"), 1)
            def relation(i, j, first):
                pe.wait_ge(S("wlow_ready"), i * 4 + j + 1)
                if not first:
                    pe.wait_ge(S("y_act"), i * 4 + j - 1)
                    pe.wait_ge(S("y_dve"), i * 4 + j - 1)
                for s in range(NT):
                    for c in range(C):
                        for k, (a, b) in enumerate(HALVES):
                            last = mm(nat(3 * (j % 2), s), hT16[:, a, c, s], w16[j][:, b, c],
                                      start=c + k == 0, stop=c + k == C + 1)
                last.then_inc(S("y_mm"), 1)

            for j in range(4):
                relation(0, j, j < 2)
            with pe.Fori(1, R // 4) as i:
                for j in range(4):
                    relation(i, j, False)
            pe.wait_ge(S("y_act"), R)
            pe.wait_ge(S("y_dve"), R)
            clear(range(7))
            pe.sem_inc(S("wohs_used"), RING)
            with pe.Fori(0, GROUPS // UN) as i:
                for u in range(UN):
                    pe.wait_ge(S("wonehots"), GT * (i * UN + u + 1))
                    add_edges(i, u, [[wohs[(GT * u + j) % RING][:, k] for k in range(2)] for j in range(GT)])
                    close(0).then_inc(S("wohs_used"), GT)
            close(0).then_inc(S("adjacency_done"), 1)
            pe.wait_ge(S("AwT_act"), 1)
            pe.wait_ge(S("AwT_dve"), 1)

            clear(range(3))
            pe.wait_ge(S("reached_ready"), 2)
            pe.sem_inc(S("split_free"), MRING)
            with pe.Fori(0, MGROUPS // UN) as i:
                for u in range(UN):
                    pe.wait_ge(S("hi_ready"), MT * (i * UN + u + 1))
                    pe.wait_ge(S("lo_ready"), MT * (i * UN + u + 1))

                    def add(d):
                        for j in range(MT * u, MT * (u + 1)):
                            for k in range(2):
                                mm(PS[0:T, d * D:d * D + D], ohd[:, ds(i * (UN * MT * N) + (j * N + d * T), T)],
                                   hilo[j % MRING][:, k], start=False, stop=False, skip_group_check=True)

                    for_reached(reached_m, i, u, add)
                    close(0).then_inc(S("split_free"), MT)

            def along_columns(col):
                for s in range(NT):
                    last = pe.transpose(PS[0:T, 3 * BANK + s * 128:3 * BANK + s * 128 + T],
                                        col[:, s:s + 1].to_broadcast([T, T]), ident[0:T, 0:T])
                last.then_inc(S("keyB_mm"), 1)

            along_columns(key)
            pe.wait_ge(S("keyB_ready"), 1)
            pe.wait_ge(S("hn_ready"), 3)
            transposes(hn, 3)
            pe.wait_ge(S("hT_ready"), 12)
            pe.wait_ge(S("w2_in"), 16)
            wide(4 * BANK, 128, [(w2[:, 128 * c:128 * c + 128], hT[:, c]) for c in range(C)]).then_inc(S("q_mm"), 1)
            pe.wait_ge(S("hpT_ready"), 1)
            for s in range(NT):
                last = pe.transpose(PS[0:T, 6 * BANK + s * Q:6 * BANK + s * Q + Q], hpT[:, s * T:s * T + T],
                                    ident[:, :])
            last.then_inc(S("hpn_mm"), 1)
            pe.wait_ge(S("hpn_ready"), 1)
            wide(0, 128, [(hpn[:, s], AwT[:, s]) for s in range(NT)]).then_inc(S("agg2_mm"), 1)
            pe.wait_ge(S("rank_ready"), 1)
            along_columns(rank)
            pe.wait_ge(S("aggT_ready"), 1)
            for s in range(NT):
                mm(nat(5, s), qT[:, s * T:s * T + T], w2[:, 256:512], start=True, stop=False)
                last = mm(nat(5, s), aggT[:, s * T:s * T + T], w2[:, 512:768], start=False, stop=True)
            last.then_inc(S("l2_mm"), 1)
            pe.wait_ge(S("w3_in"), 16)
            pe.wait_ge(S("rankB_ready"), 1)
            pe.wait_ge(S("hn_ready"), 4)
            transposes(hn, 4)
            pe.wait_ge(S("hT_ready"), 14)
            gatw = W("gat", C * D).rearrange("p (c n) -> p c n", c=C)
            for s in range(NT):
                for c in range(C):
                    last = mm(nat(4, s), hT[:, c, s * T:s * T + T], gatw[:, c], start=c == 0, stop=c == C - 1)
            last.then_inc(S("proj_mm"), 1)
            for m in range(C):
                last = wide(2 * m * BANK, 128, [(gatw[:, c, 128 * m:128 * m + 128], hT[:, c]) for c in range(C)])
            last.then_inc(S("projT_mm"), 1)
            pe.wait_ge(S("projT_ready"), 2)
            pe.wait_ge(S("projn_ready"), 1)
            pe.wait_ge(S("atgt_ready"), 1)
            for h in range(NH):
                a = atgt[:, h:h + 1].to_broadcast([128, T])
                for lo, hi in pieces(h * N, h * N + N):
                    last = mm(PS[0:T, lo:hi], a, projT[:, h // 2, lo - h * N:hi - h * N],
                              start=True, stop=True)
            last.then_inc(S("stgt_mm"), 1)
            pe.wait_ge(S("PT_ready"), 1)
            pe.wait_ge(S("hn16_ready"), 1)
            pe.wait_ge(S("stgt_ready"), 1)
            for m in range(C):
                last = wide((4 + 2 * m) * BANK, 128, [(hn16[:, k, s, 128 * m:128 * m + 128], PT[:, s])
                                                      for s in range(NT) for k in range(2)])
            last.then_inc(S("xs_mm"), 1)
            pe.wait_ge(S("xsT_ready"), 2)
            inw = W("in", 2 * C * D).rearrange("p (c n) -> p c n", c=C)
            for m in range(2 * C):
                last = wide(2 * m * BANK, 128, [(inw[:, c, 128 * m:128 * m + 128], xsT[:, c]) for c in range(C)])
            last.then_inc(S("in_mm"), 1)
            pe.wait_ge(S("xc_ready"), 2)
            pe.wait_ge(S("zT_ready"), 2)
            pe.wait_ge(S("xw_in"), 16)
            wide(5 * BANK, 128, [(xw[:, c], xc[:, c]) for c in range(C)]).then_inc(S("dbc_mm"), 1)
            pe.wait_ge(S("dbc_ready"), 2)
            for m in range(C):
                last = wide(5 * BANK + N * m, 128, [(dtw[:, 128 * m:128 * m + 128], dbc[0:RK])])
            last.then_inc(S("dt_mm"), 1)
            pe.wait_ge(S("mx_ready"), 1)
            pe.transpose(PS[0:T, 0:T], m1.to_broadcast([T, T]), ident[0:T, 0:T]).then_inc(S("mxT"), 1)
            started = set()
            for k, s in enumerate(P_ORDER):
                if s in POOL_TILES:
                    pe.wait_ge(S("p_pool"), POOL_TILES.index(s) + 1)
                else:
                    pe.wait_ge(S("p_dve"), DVE_TILES.index(s) + 1)
                for h in range(NH):
                    for lo, hi in pieces(h * N, h * N + N):
                        first = lo // BANK not in started
                        started.add(lo // BANK)
                        last = mm(PS[0:FH + 1, lo:hi], projn[:, s, h], P[:, s, h, lo - h * N:hi - h * N],
                                  start=first, stop=k == NT - 1, skip_group_check=True)
            last.then_inc(S("attT_mm"), 1)
            pe.wait_ge(S("attT_ready"), 1)
            for d in range(NT):
                for h in range(NH):
                    last = pe.transpose(PS[0:T, d * BANK + h * 65:d * BANK + h * 65 + 65],
                                        attT[:, h * N + d * T:h * N + d * T + T], ident[0:FH + 1, 0:FH + 1])
            last.then_inc(S("att_mm"), 1)
            pe.wait_ge(S("att_used"), 1)
            pe.wait_ge(S("dt_ready"), 1)
            pe.wait_ge(S("parts_ready"), 1)

            def add_states(n):
                for c in range(C):
                    pe.wait_ge(S("hc_ready"), C * n + c + 1)
                    for lo, hi in pieces(0, N):
                        last = mm(tr(4, c)[:, lo:hi], ident[:, :], hc[:, c, lo:hi],
                                  start=n == 0, stop=n == NS - 1, skip_group_check=True)
                    last.then_inc(S("y_added"), 1)

            for n in range(NS):
                for k, name in enumerate("BC"):
                    if n:
                        pe.wait_ge(S("C_ready" if k else "B_used"), n if k else C * n)
                    row_ = pick[:, k * NS + n:k * NS + n + 1].to_broadcast([128, 128])
                    wide(2 * k * BANK, 128, [(row_, parts)]).then_inc(S(f"{name}_mm"), 1)
                if n >= 2:
                    add_states(n - 2)
            add_states(NS - 2)
            add_states(NS - 1)
            pe.wait_ge(S("C_ready"), NS)
            ow = W("out", C * D).rearrange("p (c n) -> p c n", c=C)
            for c in range(C):
                pe.wait_ge(S("yT_ready"), c + 1)
                last = rows_product(0, xc[:, c], ow[:, c], c == 0)
            last.then_inc(S("yn_mm"), 1)
            pe.wait_ge(S("yn_ready"), 1)
            pe.wait_ge(S("PTt_ready"), 1)
            for d in range(NT):
                for s in range(NT):
                    last = mm(nat(4, d), PTt[:, s, d * T:d * T + T], yn[:, s], start=s == 0, stop=s == NT - 1)
            last.then_inc(S("back_mm"), 1)
            pe.wait_ge(S("hl_ready"), 1)
            transposes(hl, 5)
            pe.wait_ge(S("hT_ready"), 16)
            pe.wait_ge(S("back_used"), 1)
            wl = W("wl", C * D).rearrange("p (c n) -> p c n", c=C)
            wg = W("wg", C * D).rearrange("p (c n) -> p c n", c=C)
            for c in range(C):
                rows_product(4, hlT[:, c], wl[:, c], c == 0)
            pe.wait_ge(S("ha_ready"), 1)
            transposes(ha, 6)
            pe.wait_ge(S("hT_ready"), 18)
            for c in range(C):
                last = rows_product(4, haT[:, c], wg[:, c], False)
            last.then_inc(S("g2_mm"), 1)
            pe.wait_ge(S("hf_ready"), 1)
            transposes(hf, 7)
            pe.wait_ge(S("hT_ready"), 20)
            w1 = W("ff1", 2 * C * D).rearrange("p (c n) -> p c n", c=C)
            w2_ = W("ff2", 2 * C * D).rearrange("p (c n) -> p c n", c=2 * C)
            for m in range(2 * C + 1):
                if m < 2 * C:
                    if m >= 2:
                        pe.wait_ge(S("f1_ready"), m - 1)
                    wide(2 * (m % 2) * BANK, 128, [(w1[:, c, 128 * m:128 * m + 128], hfT[:, c]) for c in range(C)]
                         ).then_inc(S("ff1_mm"), 1)
                if m:
                    pe.wait_ge(S("f1_ready"), m)
                    last = rows_product(4, f1T[:, m - 1], w2_[:, m - 1], m == 1)
            last.then_inc(S("ff2_mm"), 1)

        @block.vector
        def _(dve):
            count = [0]

            def link(ins):
                count[0] += 1
                ins.then_inc(S("dve_chain"), 1)
                dve.wait_ge(S("dve_chain"), count[0])

            def norm(src, dst, k, g=None, b=None, middle=None):
                for s in range(NT):
                    last = dve.bn_stats(st[:, s], src[:, s])
                link(last)
                for s in range(NT):
                    last = dve.bn_aggr(mv[:, s], st[:, s])
                link(last)
                dve.tensor_scalar(ve[:, :], mv[:, :, 1], EPS, None, ALU.add).then_inc(S("var_ready"), 1)
                dve.wait_ge(S("std_ready"), k)
                link(dve.reciprocal(rstd[:, :], sd[:, :]))
                link(dve.tensor_tensor(sd[:, :], rstd[:, :], rstd[:, :], ALU.mult))
                link(dve.tensor_tensor(sd[:, :], sd[:, :], ve[:, :], ALU.mult))
                link(dve.tensor_scalar(sd[:, :], sd[:, :], -0.5, 1.5, ALU.mult, ALU.add))
                link(dve.tensor_tensor(rstd[:, :], rstd[:, :], sd[:, :], ALU.mult))
                for s in range(NT):
                    if g is None:
                        last = dve.tensor_scalar(dst[:, s], src[:, s], mv[:, s, 0:1], rstd[:, s:s + 1],
                                                 ALU.subtract, ALU.mult)
                    else:
                        last = dve.scalar_tensor_tensor(middle[:, s], src[:, s], mv[:, s, 0:1], g[:, s],
                                                        ALU.subtract, ALU.mult)
                if g is not None:
                    link(last)
                    for s in range(NT):
                        last = dve.scalar_tensor_tensor(dst[:, s], middle[:, s], rstd[:, s:s + 1], b[:, s],
                                                        ALU.mult, ALU.add)
                return last

            dve.wait_ge(S("iota_ready"), 3)
            dve.tensor_scalar(ident[:, :], iota[:, 0:128], pcol[:, 0:1], None, ALU.is_equal
                              ).then_inc(S("ident_ready"), 1)
            dve.wait_ge(S("ident_ready"), 1)
            link(dve.tensor_tensor(pick[:, :], ident[:, 32:64], ident[:, 64:96], ALU.add))
            dve.tensor_tensor(pick[:, :], pick[:, :], ident[:, 96:128], ALU.add)
            dve.wait_ge(S("edges_in"), 16)
            dve.tensor_copy(edgef[:, :, :], edgei[:, :, :]).then_inc(S("edgef_ready"), 1)
            dve.wait_ge(S("edgef_ready"), 1)
            dve.wait_ge(S("targets_mm"), 1)
            dve.tensor_reduce(span[:, 0:1], PS[0:ET, 7 * BANK:7 * BANK + T], AX_X, ALU.min)
            dve.tensor_reduce(span[:, 1:2], PS[0:ET, 7 * BANK:7 * BANK + T], AX_X, ALU.max
                              ).then_inc(S("span_ready"), 1)
            dve.wait_ge(S("x_in"), 16)
            norm(x, hn, 1).then_inc(S("hn_ready"), 1)
            dve.wait_ge(S("hT_ready"), C)
            for c in range(C):
                dve.scalar_tensor_tensor(cut(hTs[0][:, 1, c], NT), PS[:, 2 * c * BANK:2 * c * BANK + 640]
                                         .rearrange("p (s n) -> p s n", s=NT)[:, :, 0:T], 0.0,
                                         cut(hTs[0][:, 0, c], NT), ALU.max, ALU.subtract
                                         ).then_inc(S("hlow_ready"), 1)
            dve.wait_ge(S("spans_mm"), 1)
            for k, op in enumerate((ALU.min, ALU.max)):
                at_ = 7 * BANK + 128 * k
                dve.tensor_reduce(spans_m[:, k], PS[0:1, at_:at_ + ET].rearrange("p (g j) -> p g j", j=MT), AX_X, op)
                link(dve.tensor_reduce(spans[:, k], PS[0:1, at_:at_ + ET].rearrange("p (g j) -> p g j", j=GT),
                                       AX_X, op))

            def reach(spans_, table_):
                for k, (first, end) in enumerate([(d, d + 1) for d in range(NT)] + [(0, LOW), (LOW, NT)]):
                    link(dve.tensor_scalar(spans_[:, 2], spans_[:, 0], float(T * end), None, ALU.is_lt))
                    link(dve.scalar_tensor_tensor(table_[:, :, k], spans_[:, 1], float(T * first), spans_[:, 2],
                                                  ALU.is_ge, ALU.mult))

            reach(spans, reached)
            dve.sem_inc(S("reached_ready"), 1)
            link(dve.tensor_scalar(idxf, edgef[:, 2], float(N), None, ALU.mult))
            link(dve.tensor_tensor(idxf, idxf, edgef[:, 0], ALU.add))
            dve.tensor_copy(idx[:, :], idxf).then_inc(S("idx_ready"), 1)
            with dve.Fori(0, ET // RING) as i:
                for j in range(RING):
                    t = i * RING + j
                    dve.tensor_scalar(ohd[:, ds(t * N, N)], iota[0:T, :], edgef[:, 1, ds(t, 1)], None, ALU.is_equal
                                      ).then_inc(S("onehots"), 1)
                    dve.wait_ge(S("ohs_used"), t + 1)
                    dve.tensor_scalar(ohs[:, j], iota[0:T, :], edgef[:, 0, ds(t, 1)], None, ALU.is_equal
                                      ).then_inc(S("onehots"), 1)
            dve.wait_ge(S("adjacency_done"), 1)
            dve.wait_ge(S("w0_low"), 2)
            cnt = PS[:, NT * NT * 128:(NT * NT + NT) * 128].rearrange("p (d n) -> p d n", d=NT)[:, :, 0:T]
            link(dve.tensor_scalar(cut(rcB, NT), cnt, 1.0, None, ALU.max))
            dve.tensor_scalar(cut(zB, NT), cnt, 1.0, 1 / W0SCALE, ALU.min, ALU.mult).then_inc(S("cnt_used"), 1)
            link(dve.reciprocal(rcB, rcB))
            dve.tensor_copy(squares(CTf, 12, 25), adjacency(12, 25)).then_inc(S("CT_dve"), 1)
            dve.wait_ge(S("CT_dve"), 1)
            dve.wait_ge(S("CT_act"), 1)
            for (lo, hi), part in CTn_parts:
                dve.tensor_tensor(part, CT[:, lo:hi], A1[0:T, 12650:12650 + N].rearrange("p (s n) -> p s n", s=1)
                                  .to_broadcast([T, hi - lo, N]), ALU.mult).then_inc(S("CTn_part"), 1)
            for l in range(3):
                dve.wait_ge(S("g_ready"), l + 1)
                dve.tensor_tensor(g[:, 1], nat_all(0), g[:, 0], ALU.subtract).then_inc(S("glow_ready"), 1)
                if l == 0:
                    for k, ((lo, hi), part) in enumerate(CTn_parts):
                        dve.wait_ge(S("CTn_high"), k + 1)
                        dve.tensor_tensor(CTn[:, 1, lo:hi], part, CTn[:, 0, lo:hi], ALU.subtract).then_inc(S("CTn_ready"), 1)
                    link(dve.tensor_reduce(deg[:, :], CT[:, :, :], AX_X, ALU.add))
                    dve.wait_ge(S("params_in"), 64)
                    link(dve.tensor_tensor(key[:, :], deg[:, :], noise_sb[:, :], ALU.add))
                    dve.wait_ge(S("rows_in"), 16)
                    link(dve.tensor_tensor(x[:, :, :], x[:, :, :], row("bf"), ALU.add))
                    dve.wait_ge(S("params_in"), 64)
                    dve.tensor_scalar(half[:, 0:1], pcol[:, :], float(FH), None, ALU.is_lt)
                    link(dve.tensor_scalar(half[:, 1:2], pcol[:, :], float(FH), None, ALU.is_ge))
                    for c in range(C):
                        last = dve.tensor_scalar(atgt[:, 2 * c:2 * c + 2], half[:, :], pc("a_tgt", c), None, ALU.mult)
                    last.then_inc(S("atgt_ready"), 1)
                    link(dve.tensor_scalar(pcols[:, 0:3 * C], pcols[:, 0:3 * C], W0SCALE, None, ALU.mult))
                for c in range(C):
                    dve.wait_ge(S("pre_mm"), C * l + c + 1)
                    dve.scalar_tensor_tensor(tmp[:, c], tr(3, c), pc(f"b{l}", c), zB, ALU.add, ALU.mult
                                             ).then_inc(S("pre_masked"), 1)
                    dve.wait_ge(S("hT_ready"), C * (l + 1) + c + 1)
                    dve.scalar_tensor_tensor(hTs[l + 1][:, 1, c], tmp[:, c], 0.0, hTs[l + 1][:, 0, c],
                                             ALU.max, ALU.subtract).then_inc(S("hlow_ready"), 1)
            dve.wait_ge(S("l0_mm_done"), 1)
            link(dve.scalar_tensor_tensor(x[:, :, :], nat_all(0), 1 / W0SCALE, x[:, :, :], ALU.mult, ALU.add))
            norm(x, hn, 2).then_inc(S("hn_ready"), 1)
            dve.wait_ge(S("hT_ready"), 10)
            hTs_ = hT.rearrange("p c (n s) -> p c s n", s=NT)
            link(dve.tensor_copy(hT16[:, 0], hTs_))
            dve.tensor_tensor(hT16[:, 1], hTs_, hT16[:, 0], ALU.subtract).then_inc(S("hT16_ready"), 1)

            def low_weights(i, j):
                dve.wait_ge(S("whigh_ready"), i * 4 + j + 1)
                dve.scalar_tensor_tensor(w16[j % 4][:, 1], wring[:, j % 4], WSCALE, w16[j % 4][:, 0],
                                         ALU.mult, ALU.subtract).then_inc(S("wlow_ready"), 1)

            def three_rows(i, j):
                dve.wait_ge(S("y_mm"), i * 4 + j + 1)
                if j >= 2 or not isinstance(i, int) or i:
                    dve.wait_ge(S(f"y_stored{j % 2}"), 16 * (i * 2 + j // 2))
                dve.tensor_tensor(ystage[:, j % 2, 2:5], nat_all(3 * (j % 2))[:, 2:5],
                                  gate[:, 2:5, ds(i * 4 + j, 1)].to_broadcast([T, 3, D]), ALU.mult
                                  ).then_inc(S("y_dve"), 1)

            low_weights(0, 0)
            low_weights(0, 1)
            dve.wait_ge(S("gate_ready"), 1)
            reach(spans_m, reached_m)
            dve.sem_inc(S("reached_ready"), 1)
            dve.wait_ge(S("edgew_in"), 16)
            link(dve.tensor_copy(wsplit16, edgew[:, 0]))
            link(dve.tensor_copy(wsplit[:, 0], wsplit16))
            link(dve.tensor_tensor(wsplit[:, 1], edgew[:, 0], wsplit[:, 0], ALU.subtract))
            dve.wait_ge(S("gate_ready"), 2)
            with dve.Fori(0, R // 4 - 1) as i:
                for j in range(4):
                    low_weights(i, j + 2)
                    three_rows(i, j)
            for j in range(4):
                if j < 2:
                    low_weights(R // 4 - 1, j + 2)
                three_rows(R // 4 - 1, j)

            with dve.Fori(0, ET // RING) as i:
                for j in range(RING):
                    t = i * RING + j
                    dve.wait_ge(S("wohs_used"), t + 1)
                    if j == RING // 2:
                        dve.wait_ge(S("y_stored0"), 16 * R // 2)
                        dve.wait_ge(S("y_stored1"), 16 * R // 2)
                    for k in range(2):
                        last = dve.tensor_scalar(wohs[j][:, k], iota[0:T, :], edgef[:, 0, ds(t, 1)],
                                                 wsplit[:, k, ds(t, 1)], ALU.is_equal, ALU.mult)
                    last.then_inc(S("wonehots"), 1)
            dve.wait_ge(S("adjacency_done"), 2)
            dve.tensor_copy(squares(AwTf, 12, 25), adjacency(12, 25)).then_inc(S("AwT_dve"), 1)
            with dve.Fori(0, ET // GR) as i:
                for j in range(GR):
                    t = i * GR + j
                    dve.wait_ge(S("hi_ready"), t + 1)
                    dve.scalar_tensor_tensor(hilo[j % MRING][:, 1], gath[j], edgew[:, 1, ds(t, 1)], hilo[j % MRING][:, 0],
                                             ALU.mult, ALU.subtract).then_inc(S("lo_ready"), 1)
            dve.wait_ge(S("split_free"), MRING + ET)
            link(dve.scalar_tensor_tensor(x[:, :, :], nat_all(0), 0.0, x[:, :, :], ALU.max, ALU.add))
            norm(x, hn, 3).then_inc(S("hn_ready"), 1)
            dve.wait_ge(S("keyB_ready"), 1)
            for s in range(NT):
                link(dve.tensor_scalar(low, iota[0:T, :], ncol[0:T, s:s + 1], None, ALU.is_lt))
                link(dve.tensor_scalar(junk, keyB, key[:, s:s + 1], None, ALU.is_lt, ALU.add,
                                       accum_out=rank[:, s:s + 1]))
                link(dve.scalar_tensor_tensor(junk, keyB, key[:, s:s + 1], low, ALU.is_equal, ALU.mult,
                                              accum_out=rank2[:, s:s + 1]))
            dve.tensor_tensor(rank[:, :], rank[:, :], rank2[:, :], ALU.add).then_inc(S("rank_ready"), 1)
            link(dve.tensor_tensor(x[:, :, :], x[:, :, :], row("b1"), ALU.add))
            link(dve.tensor_tensor(x[:, :, :], x[:, :, :], row("b2"), ALU.add))
            dve.wait_ge(S("l2_mm"), 1)
            link(dve.tensor_tensor(x[:, :, :], x[:, :, :], nat_all(5), ALU.add))
            link(norm(x, hn, 4))
            dve.tensor_scalar(hn[:, :, :], hn[:, :, :], 0.0, None, ALU.max).then_inc(S("hn_ready"), 1)
            dve.memset(projn[:, :, :, FH:FH + 1], 1.0)
            dve.wait_ge(S("hn_ready"), 4)
            link(dve.tensor_copy(hn16[:, 0], hn[:, :, :]))
            dve.tensor_tensor(hn16[:, 1], hn[:, :, :], hn16[:, 0], ALU.subtract).then_inc(S("hn16_ready"), 1)
            for s in range(NT):
                last = dve.tensor_scalar(PT[:, s], iota[0:T, :], rank[:, s:s + 1], None, ALU.is_equal)
            last.then_inc(S("PT_ready"), 1)
            dve.tensor_scalar(far, CT[:, :, :], 0.0, FAR, ALU.is_equal, ALU.mult).then_inc(S("far_ready"), 1)
            dve.wait_ge(S("rows_late_in"), 16)
            dve.wait_ge(S("projn_ready"), 1)
            sa4 = sa.rearrange("p s (h f) -> p s h f", h=NH)
            asrc = row("a_src").rearrange("p s (h f) -> p s h f", h=NH)
            link(dve.tensor_tensor(sa4, projn[:, :, :, 0:FH], asrc, ALU.mult))
            dve.tensor_reduce(ssrc, sa4, AX_X, ALU.add).then_inc(S("ssrc_ready"), 1)
            dve.memset(xcp[:, :, 0:3], 0.0)
            def convolve():
                for c in range(C):
                    dve.wait_ge(S("xcp_ready"), c + 1)
                    link(dve.tensor_scalar(xc[:, c], xcp[:, c, 0:N], pc("conv_w", K4 * c), None, ALU.mult))
                    for k in range(1, K4):
                        last = dve.scalar_tensor_tensor(xc[:, c], xcp[:, c, k:k + N], pc("conv_w", K4 * c + k),
                                                        xc[:, c], ALU.mult, ALU.add)
                        if k < K4 - 1:
                            link(last)
                    last.then_inc(S("conv_done"), 1)

            dve.wait_ge(S("far_ready"), 1)
            for s in range(NT):
                if s == 3:
                    convolve()
                dve.wait_ge(S("v_ready"), s + 1)
                link(dve.scalar_tensor_tensor(P[:, s], V[:, s % 2], 0.2, V[:, s % 2], ALU.mult, ALU.max))
                dve.tensor_tensor_reduce(out=P[:, s], in0=P[:, s],
                                         in1=far[:, s:s + 1].to_broadcast([T, NH, N]), scale=1.0, scalar=-3.0e38,
                                         op0=ALU.add, op1=ALU.max, accum_out=mx[:, s:s + 1]
                                         ).then_inc(S("max_done"), 1)
            dve.wait_ge(S("max_done"), NT)
            dve.tensor_reduce(m1, mx, AX_X, ALU.max).then_inc(S("mx_ready"), 1)
            dve.wait_ge(S("dt_mm"), 1)
            for c in range(C):
                last = dve.tensor_scalar(dtx[:, c], PS[:, 5 * BANK + N * c:5 * BANK + N * c + N], pc("dt_b", c), None,
                                         ALU.add)
            last.then_inc(S("dt_read"), 1)
            dve.wait_ge(S("mxT"), 1)
            link(dve.tensor_reduce(gm, PS[0:T, 0:T], AX_X, ALU.max))
            dve.tensor_scalar(gm, gm, -1.0, None, ALU.mult).then_inc(S("gm_ready"), 1)
            dve.wait_ge(S("A_exp"), 1)
            dve.tensor_scalar(Aneg[:, :, :], Aneg[:, :, :], -1.0, None, ALU.mult).then_inc(S("A_ready"), 1)
            dve.wait_ge(S("dt_read"), 1)
            dve.scalar_tensor_tensor(dBx, dtx, -1.0, dtx, ALU.mult, ALU.max).then_inc(S("sp_abs"), 1)
            link(dve.tensor_scalar(dt, dtx, 0.0, None, ALU.max))

            def times_edges(s):
                dve.wait_ge(S("e_exp"), EXP_ORDER.index(s) + 1)
                dve.tensor_tensor(P[:, s], P[:, s], CT[:, s:s + 1].to_broadcast([T, NH, N]), ALU.mult
                                  ).then_inc(S("p_dve"), 1)

            times_edges(DVE_TILES[0])
            dve.wait_ge(S("dbc_ready"), 2)
            link(dve.tensor_tensor(rest, dbc, parts, ALU.subtract))
            link(dve.tensor_copy(parts[64:128], rest[64:128]))
            link(dve.tensor_tensor(rest[96:128], rest[96:128], parts[96:128], ALU.subtract))
            dve.tensor_copy(parts[96:128], rest[96:128]).then_inc(S("parts_ready"), 1)
            times_edges(DVE_TILES[1])
            times_edges(DVE_TILES[2])
            dve.wait_ge(S("sp_exp"), 1)
            dve.tensor_scalar(hc, hs, 1.0, None, ALU.add).then_inc(S("sp_w"), 1)
            dve.wait_ge(S("sp_w"), 1)
            link(dve.scalar_tensor_tensor(dBx, hc, -1.0, hs, ALU.add, ALU.subtract))
            dve.wait_ge(S("sp_ln"), 1)
            link(dve.scalar_tensor_tensor(Cs, hc, 1.0, Cs, ALU.not_equal, ALU.mult))
            link(dve.tensor_tensor(Cs, Cs, dBx, ALU.subtract))
            link(dve.tensor_tensor(dt, dt, Cs, ALU.add))
            dve.tensor_tensor(dtx, dt, xc, ALU.mult).then_inc(S("dt_ready"), 1)
            dve.wait_ge(S("att_mm"), 1)
            att = PS[0:T, 0:NT * BANK].rearrange("p (s n) -> p s n", s=NT)[:, :, 0:NH * 65] \
                .rearrange("p s (h f) -> p s h f", h=NH)
            link(dve.tensor_scalar(den, att[:, :, :, FH], 1e-16, None, ALU.add))
            link(dve.reciprocal(den, den))
            for s in range(NT):
                last = dve.tensor_tensor(sa4[:, s], att[:, s, :, 0:FH],
                                         den[:, s].rearrange("p (h f) -> p h f", f=1).to_broadcast([T, NH, FH]),
                                         ALU.mult)
            last.then_inc(S("att_used"), 1)
            dve.wait_ge(S("dt_ready"), 1)

            def inputs(n, c):
                dve.wait_ge(S("B_mm"), n + 1)
                if n >= 2:
                    dve.wait_ge(S("scanned"), C * (n - 2) + c + 1)
                dve.tensor_tensor(dBxs[n % 2][:, c], dtx[:, c], tr(0, 0), ALU.mult).then_inc(S("B_used"), 1)

            for c in range(C):
                inputs(0, c)
            for n in range(NS):
                for c in range(C):
                    k = C * n + c
                    if n < NS - 1:
                        inputs(n + 1, c)
                    dve.wait_ge(S("B_used"), k + 1)
                    dve.wait_ge(S("dA_ready"), k + 1)
                    if n >= 2:
                        dve.wait_ge(S("hc_ready"), k - 2 * C + 1)
                    dve.tensor_tensor_scan(hss[n % 2][:, c], dA[:, n % 2, c], dBxs[n % 2][:, c], 0.0,
                                           ALU.mult, ALU.add).then_inc(S("scanned"), 1)
            dve.wait_ge(S("scanned"), C * NS)
            dve.wait_ge(S("rankB_ready"), 1)
            for s in range(NT):
                last = dve.tensor_scalar(PTt[:, s], rankB, ncol[0:T, s:s + 1], None, ALU.is_equal)
            last.then_inc(S("PTt_ready"), 1)
            for c in range(C):
                dve.wait_ge(S("y_added"), C * (NS - 1) + c + 1)
                link(dve.scalar_tensor_tensor(xc[:, c], xc[:, c], pc("D", c), tr(4, c), ALU.mult, ALU.add))
                dve.tensor_tensor(xc[:, c], xc[:, c], zT[:, c], ALU.mult).then_inc(S("yT_ready"), 1)
            dve.wait_ge(S("sa_sum"), 2)
            dve.tensor_scalar(sb_, sa, 0.0, None, ALU.min).then_inc(S("elu_in"), 1)
            link(dve.tensor_scalar(sa, sa, 0.0, None, ALU.max))
            dve.wait_ge(S("elu_exp"), 1)
            link(dve.scalar_tensor_tensor(sa, sb_, -1.0, sa, ALU.add, ALU.add))
            norm(sa, hl, 5, row("lnl_g"), row("lnl_b"), hl).then_inc(S("hl_ready"), 1)
            dve.wait_ge(S("back_mm"), 1)
            dve.tensor_tensor(sa, hn[:, :, :], nat_all(4), ALU.add).then_inc(S("back_used"), 1)
            dve.wait_ge(S("back_used"), 1)
            norm(sa, ha, 6, row("lng_g"), row("lng_b"), ha).then_inc(S("ha_ready"), 1)
            dve.wait_ge(S("ha_ready"), 1)
            link(dve.tensor_tensor(sa, hl, ha, ALU.subtract))
            link(dve.tensor_tensor(x[:, :, :], x[:, :, :], row("ln2_b"), ALU.add))
            dve.wait_ge(S("gt_ready"), 1)
            link(dve.tensor_tensor(sa, sa, gt, ALU.mult))
            dve.tensor_tensor(hf, sa, ha, ALU.add).then_inc(S("hf_ready"), 1)
            dve.wait_ge(S("hf_ready"), 1)
            link(dve.tensor_tensor(sa, hf, row("ff2_b"), ALU.add))
            dve.wait_ge(S("ff2_mm"), 1)
            link(dve.tensor_tensor(sa, sa, nat_all(4), ALU.add))
            norm(sa, x, 7, row("ln2_g"), x, hl).then_inc(S("out_ready"), 1)


def kernel(x, src, dst, edge_type_16, edge_weight, edge_weight1, node_vec, L1_gnn_weight, L1_gnn_gate_weight, **w):
    import concourse.bacc as bacc
    from concourse.bass_utils import run_bass_kernel_spmd

    f = {k: np.asarray(v) for k, v in w.items()}

    def edges(a):
        return np.asarray(a).reshape(ET, T).T

    def chunks(a):
        a = np.asarray(a)
        return a.reshape(-1, 128, a.shape[1]).transpose(1, 0, 2).reshape(128, -1)

    def vec(name):
        return f[name].reshape(-1, 128).T

    L3 = "L3_gnn_"
    arrays = {
        "x": np.ascontiguousarray(x),
        "edge_int": np.ascontiguousarray(np.stack([edges(src), edges(dst), edges(edge_type_16)], 1)),
        "edge_flt": np.ascontiguousarray(np.stack([edges(edge_weight), edges(edge_weight1)], 1)),
        "noise": np.ascontiguousarray(np.asarray(node_vec).reshape(NT, T).T),
        "pcols": np.ascontiguousarray(np.concatenate(
            [vec("L0_gnn_b0"), vec("L0_gnn_b1"), vec("L0_gnn_b2"), vec("L2_gnn_bp"), chunks(f[L3 + "conv_w"]),
             vec(L3 + "conv_b"), vec(L3 + "dt_proj_b"), chunks(f[L3 + "A_log"]), vec(L3 + "D_param"),
             vec(L3 + "ff1_b"), vec(L3 + "gat_a_tgt")], 1)),
        "rows": np.ascontiguousarray(np.stack(
            [f["L0_gnn_bf"], f["L2_gnn_b1"], f["L2_gnn_b2"], f[L3 + "gat_a_src"].reshape(-1), f[L3 + "gat_b"]] +
            [f[L3 + k] for k in ("ln_local_g", "ln_local_b", "ln_global_g", "ln_global_b", "ln2_g", "ln2_b",
                                 "ff2_b")], 0)),
        "w0": np.ascontiguousarray(np.concatenate([chunks(f["L0_gnn_" + k]) for k in ("W0", "W1", "W2", "Wf")], 1)),
        "w1": np.ascontiguousarray(np.asarray(L1_gnn_weight).reshape(R, C, 128, D).transpose(2, 0, 1, 3)),
        "gw": np.ascontiguousarray(np.asarray(L1_gnn_gate_weight).reshape(R, C, 128).transpose(2, 1, 0)),
        "w2": np.ascontiguousarray(np.concatenate([chunks(f["L2_gnn_" + k].T) for k in ("Wp", "W1", "W2")], 1)),
        "w3": np.ascontiguousarray(np.concatenate(
            [chunks(f[L3 + k].T) for k in ("gat_w", "in_proj_w", "out_proj_w", "wl", "wg", "ff1_w", "ff2_w")], 1)),
        "xw": np.ascontiguousarray(chunks(f[L3 + "x_proj_w"][X_ROWS].T)),
        "dtw": np.ascontiguousarray(f[L3 + "dt_proj_w"].T),
    }
    nc = bacc.Bacc("TRN2", target_bir_lowering=False, num_devices=1)
    args = [nc.dram_tensor("in_" + name, a.shape, mybir.dt.from_np(a.dtype), kind="ExternalInput").ap()
            for name, a in arrays.items()]
    out = nc.dram_tensor("out_x", (N, D), F32, kind="ExternalOutput").ap()
    table = nc.dram_tensor("table", (R, N, D), F32, kind="Internal").ap()
    gnn_kernel(nc, *args, out, table)
    return run_bass_kernel_spmd(nc, [{"in_" + k: a for k, a in arrays.items()}], core_ids=[0]).results[0]["out_x"]
```

```python
from contextlib import ExitStack

import numpy as np
import concourse.bass as bass
from concourse import mybir

ALU = mybir.AluOpType
ACT = mybir.ActivationFunctionType
F32 = mybir.dt.float32
F16 = mybir.dt.float16
BF16 = mybir.dt.bfloat16
I32 = mybir.dt.int32
AX_X = mybir.AxisListType.X
ds = bass.ds

N = 625
T = 125
NT = N // T
NP = N + 1
E = 10000
ET = E // T
D = 256
C = D // 128
R = 16
Q = 128
NH, FH = 4, 64
NS = 16
RK = 16
DB = RK + 2 * NS
K4 = 4
EPS = 1e-5
BANK = 512
FAR = -1.0e30

PC = {}
at = 0
for name, n in [("b0", 2), ("b1", 2), ("b2", 2), ("bp", 1), ("conv_w", 8), ("conv_b", 2), ("dt_b", 2),
                ("A_log", 32), ("D", 2), ("ff1_b", 4)]:
    PC[name] = at
    at += n
PCOLS = at
ROW = {name: i for i, name in enumerate(["bf", "b1", "b2", "gat_b", "lnl_g", "lnl_b", "lng_g", "lng_b", "ln2_g",
                                         "ln2_b", "ff2_b", "a_src", "a_tgt"])}
NROW = len(ROW)
A1_WORDS = 19656
BANKED = ((0, 2), (2, 4), (4, NT))
W0SCALE = 16.0
HALVES = ((0, 0), (0, 1), (1, 0))
WSCALE = 256.0
GT = 4
GROUPS = ET // GT
LOW = NT // 2
UN = 4
MT = 5
MGROUPS = ET // MT
MRING = 4 * MT
ARING = 4 * GT
WUN = 3
WRING = WUN * GT
EARLY = 3
X_ROWS = list(range(RK)) * 2 + list(range(RK, DB)) * 3
W3 = {}
at = 0
for name, n in [("gat", C * D), ("in", C * 2 * D), ("out", C * D), ("wl", C * D), ("wg", C * D),
                ("ff1", C * 2 * D), ("ff2", 2 * C * D)]:
    W3[name] = at
    at += n
W3COLS = at


def pieces(lo, hi):
    out = []
    while lo < hi:
        end = min(hi, (lo // BANK + 1) * BANK)
        out.append((lo, end))
        lo = end
    return out


def gnn_kernel(nc, x_in, edge_int, edge_flt, noise, pcols_in, rows_in, w0_in, w1_in, gw_in, w2_in, w3_in, xw_in, dtw_in,
               out, table, counts):
    ctx = ExitStack()
    with ctx:
        def sb(name, shape, dt=F32):
            return ctx.enter_context(nc.sbuf_tensor(name, shape, dt))

        sems = {}

        def S(name):
            if name not in sems:
                sems[name] = ctx.enter_context(nc.semaphore(name))
            return sems[name]

        ident = sb("ident", [128, 128])
        ones = sb("ones", [128, 1], F16)
        iota = sb("iota", [128, NP], F16)
        pcol = sb("pcol", [128, 1])
        ncol = sb("ncol", [128, NT])
        edgei = sb("edgei", [T, 3, ET], I32)
        edgef = sb("edgef", [T, 3, ET])
        edgew = sb("edgew", [T, 2, ET])
        idx = sb("idx", [T, ET], I32)
        x = sb("x", [T, NT, D])
        pcols = sb("pcols", [128, PCOLS])
        rows_early = sb("rows_early", [128, EARLY, D])
        key = sb("key", [T, NT])
        noise_sb = sb("noise_sb", [T, NT])
        deg = sb("deg", [T, NT])
        rank = sb("rank", [T, NT])
        rank2 = sb("rank2", [T, NT])
        st = sb("st", [T, NT, 6])
        mv = sb("mv", [T, NT, 2])
        ve = sb("ve", [T, NT])
        sd = sb("sd", [T, NT])
        rstd = sb("rstd", [T, NT])
        small = sb("small", [T, 52])
        dtw = sb("dtw", [RK, D])
        Aneg = sb("Aneg", [128, C, NS])
        wst = sb("wst", [128, 2, C, NH])
        gw_sb = sb("gw_sb", [128, C * R])
        zero = sb("zero", [128, 128], F16)
        pick = sb("pick", [128, 2 * NS], BF16)
        span = sb("span", [ET, 2])
        spans = sb("spans", [1, 3, GROUPS])
        reached = sb("reached", [1, GROUPS, NT + 2], I32)
        A0 = sb("A0", [128, ET * NP // 2])
        A1 = sb("A1", [128, A1_WORDS + NT * D + NT * N])
        hn = A1[0:T, A1_WORDS:A1_WORDS + NT * D].rearrange("p (s n) -> p s n", s=NT)
        CTf = A1[0:T, A1_WORDS + NT * D:A1_WORDS + NT * D + NT * N]
        CT = CTf.rearrange("p (s n) -> p s n", s=NT)
        spans_m = A1[0:1, 19584:19584 + 3 * MGROUPS].rearrange("p (k g) -> p k g", k=3)
        reached_m = A1[0:1, 3072:3072 + MGROUPS * (NT + 2)].bitcast(I32).rearrange("p (g k) -> p g k", g=MGROUPS)
        PS = ctx.enter_context(nc.psum_tensor("PS", [128, 8 * BANK], F32))

        def a0(lo, n, rows_=128):
            return A0[0:rows_, lo:lo + n]

        def a1(lo, n, rows_=128):
            return A1[0:rows_, lo:lo + n]

        def cut(ap, k):
            return ap.rearrange("p (k n) -> p k n", k=k)

        ohd = A0[0:T, :].bitcast(F16)
        w_first, w_last = a1(10120, 3072), a1(13980, 2048)
        w_first16 = A1[:, 0:3072].bitcast(F16).rearrange("p (l k n) -> p l k n", l=3, k=2)
        w_last16 = A1[:, 3072:5120].bitcast(F16).rearrange("p (k n) -> p k n", k=2)
        wl0 = [w_first16[:, l].rearrange("p k (c n) -> p k c n", c=2 * C) for l in range(3)]
        wf = w_last16.rearrange("p k (c n) -> p k c n", c=4 * C)
        hTs = [A1[:, 5120 + 1250 * l:6370 + 1250 * l].bitcast(F16).rearrange("p (k c n) -> p k c n", k=2, c=C)
               for l in range(4)]
        g = A1[0:T, 10120:11400].bitcast(F16).rearrange("p (k s n) -> p k s n", k=2, s=NT)
        ohs = [A1[0:T, at_ + NP // 2 * j:at_ + NP // 2 * (j + 1)].bitcast(F16)
               for at_ in (17025, 6370) for j in range(ARING // 2)]
        tmp = cut(a1(11400, 1250), C)
        idxf = a1(13900, ET, T)
        rcB = a1(12650, N)
        zB = a1(13275, N)
        CTn = A1[0:T, 13900:17025].bitcast(F16).rearrange("p (k s n) -> p k s n", k=2, s=NT)
        CTn_parts = [((0, 2), cut(a1(17025, 1250, T), 2)), ((2, 4), cut(a1(18275, 1250, T), 2)),
                     ((4, 5), cut(a1(11400, 625, T), 1))]
        wring = a1(0, 2048).rearrange("p (j c n) -> p j c n", j=4, c=C)
        hT = cut(a1(2048, 1250), C)
        gate = a1(3298, NT * R, T).rearrange("p (s r) -> p s r", s=NT)
        ystage = a1(3378, 2 * NT * D, T).rearrange("p (j s n) -> p j s n", j=2, s=NT)
        w16 = [A1[:, 5938 + 512 * j:5938 + 512 * j + 512].bitcast(F16)
                      .rearrange("p (k c n) -> p k c n", k=2, c=C) for j in range(4)]
        hT16 = A1[:, 7986:7986 + 1250].bitcast(F16).rearrange("p (k c s n) -> p k c s n", k=2, c=C, s=NT)
        GR = 40
        GG = 5
        gath = [a1(D * j if j < 8 else 10880 + D * (j - 8), D, T) for j in range(GR)]

        EXTRA = (NT * D + NT * N) // D

        def gath_of(i, j):
            if j >= EXTRA:
                return gath[j]
            first = D * j if j < 8 else 10880 + D * (j - 8)
            return A1[0:T, ds(i * (A1_WORDS + D * j - first) + first, D)]

        hilo = [A1[0:T, at_ + D * j:at_ + D * j + D].bitcast(F16).rearrange("p (k n) -> p k n", k=2)
                for at_, n in ((3378, 14), (2048, 4), (19072, 2)) for j in range(n)]
        gw = gw_sb[:, :].rearrange("p (c r) -> p c r", c=C)
        AwTf = a1(6962, NT * N, T)
        AwT = cut(AwTf, NT)
        wohs = [A1[0:T, at_ + NP * j:at_ + NP * j + NP].bitcast(F16).rearrange("p (k n) -> p k n", k=2)
                for at_, n in ((3378 + 5 * NP, 6), (2048, 1), (3378, 5)) for j in range(n)]
        wsplit = cut(a1(2048 + NP, 2 * ET, T), 2)
        wsplit16 = a1(2048 + NP + 2 * ET, ET // 2, T).bitcast(F16)
        keyB = a1(3378, N, T)
        junk = a1(4003, N, T)
        low = a1(4628, N, T)
        rankB = a1(5253, N, T)
        w2 = a1(10087, 768)
        w3 = a1(10880, W3COLS)
        rows_late = a1(16000, (NROW - EARLY) * D).rearrange("p (r n) -> p r n", n=D)
        qT = a1(0, N)
        hpT = a1(625, N)
        hpn = a1(1250, NT * Q, T).rearrange("p (s n) -> p s n", s=NT)
        aggT = a1(625, N)
        P = a0(0, 12500, T).rearrange("p (s h n) -> p s h n", s=NT, h=NH)
        V = a0(12500, 5000, T).rearrange("p (j h n) -> p j h n", j=2, h=NH)
        stgt = a0(17500, 2500, T).rearrange("p (h n) -> p h n", h=NH)
        far = cut(a0(20000, NT * N, T), NT)
        trow = a0(23125, N, NH)
        wprod = cut(a1(5938, C * D), C)
        projn = a1(0, NT * NH * 65, T).rearrange("p (s h f) -> p s h f", s=NT, h=NH)
        hl = cut(a1(3378, NT * D, T), NT)
        sa = cut(a1(5938, NT * D, T), NT)
        sb_ = hl
        ha = cut(a1(8498, NT * D, T), NT)
        ssrc = small[:, 0:20].rearrange("p (s h) -> p s h", s=NT)
        m1 = small[:, 25:26]
        gm = small[:, 26:27]
        minus_gm = small[:, 27:28]
        den = small[:, 30:50].rearrange("p (s h) -> p s h", s=NT)
        den_flat = small[:, 30:50]
        mx = den
        PT = A1[0:T, 7218:7218 + 1563].bitcast(F16)[:, 0:NT * N].rearrange("p (s n) -> p s n", s=NT)
        hn16 = A1[0:T, 8782:8782 + 1280].bitcast(F16).rearrange("p (k s n) -> p k s n", k=2, s=NT)
        xsT = hT
        xcp = cut(a1(18400, 1256), C)
        zT = cut(a0(23125, 1250), C)
        xc = cut(a1(7218, 1250), C)
        dbc = a1(8498, N)
        parts = A0[:, 24632:24632 + 313].bitcast(BF16)[:, 0:N]
        rest = a0(21875, N)
        xw = cut(a0(24375, C * 128), C)
        dt = cut(a0(14375, 1250), C)
        dtx = cut(a1(3378, 1250), C)
        dBx = cut(a0(16875, 1250), 2)
        hs = cut(a0(18125, 1250), 2)
        Cs = cut(a0(19375, 1250), 2)
        hc = cut(a0(20625, 1250), 2)
        dBxs, hss = [dBx, cut(a0(8200, 1250), C)], [hs, cut(a0(9450, 1250), C)]
        dA = a0(0, 2500).rearrange("p (j c n) -> p j c n", j=2, c=C)
        PTt = cut(a0(2500, NT * N, T), NT)
        yn = cut(a0(5625, NT * D, T), NT)
        attT = a0(5625, NH * N, FH + 1)
        hlT = cut(a0(5400, 1250), C)
        haT = cut(a0(6650, 1250), C)
        hfT = cut(a0(7900, 1250), C)
        f1T = cut(a0(9150, 2500), 2 * C)
        gt = cut(a0(0, NT * D, T), NT)
        hf = cut(a0(1280, NT * D, T), NT)

        def row(name):
            i = ROW[name]
            src = rows_early[:, i:i + 1, :] if i < EARLY else rows_late[:, i - EARLY:i - EARLY + 1, :]
            return src[0:T].to_broadcast([T, NT, D])

        def pc(name, c=0):
            return pcols[:, PC[name] + c:PC[name] + c + 1]

        def W(name, n):
            return w3[:, W3[name]:W3[name] + n]

        def nat(b, s):
            return PS[0:T, b * BANK + s * D:b * BANK + s * D + D]

        def nat_all(b):
            return PS[0:T, b * BANK:b * BANK + NT * D].rearrange("p (s n) -> p s n", s=NT)

        def adjacency(lo, hi):
            return PS[0:T, 128 * lo:128 * hi].rearrange("p (b n) -> p b n", n=128)[:, :, 0:T]

        def squares(flat, lo, hi):
            return flat[:, T * lo:T * hi].rearrange("p (b n) -> p b n", n=T)

        def tr(b, c, rows_=128):
            return PS[0:rows_, (b + 2 * c) * BANK:(b + 2 * c) * BANK + N]

        EXP_ORDER = (1, 0, 2, 3, 4)
        POOL_TILES, DVE_TILES, P_ORDER = (0, 3), (1, 2, 4), (1, 0, 2, 3, 4)
        keyB_ps = PS[0:T, 3 * BANK:3 * BANK + 640].rearrange("p (s n) -> p s n", s=NT)[:, :, 0:T]
        block = ctx.enter_context(nc.Block())

        @block.sync
        def _(sp):
            sp.dma_start(edgei[:, :, :], edge_int).then_inc(S("edges_in"), 16)
            sp.dma_start(x[:, :, :], x_in.rearrange("(s p) f -> p s f", p=T)).then_inc(S("x_in"), 16)
            sp.dma_start(edgew[:, :, :], edge_flt).then_inc(S("edgew_in"), 16)
            sp.dma_start(pcols[:, :], pcols_in).then_inc(S("params_in"), 16)
            sp.dma_start(w_first, w0_in[:, 0:3072]).then_inc(S("w0_in"), 16)
            sp.dma_start(w_last, w0_in[:, 3072:5120]).then_inc(S("w0_in"), 16)
            sp.dma_start(rows_early[:, :, :], rows_in[0:EARLY].partition_broadcast(128)).then_inc(S("rows_in"), 16)
            sp.dma_start(gw_sb[:, :], gw_in).then_inc(S("params_in"), 16)
            sp.dma_start(noise_sb[:, :], noise).then_inc(S("params_in"), 16)
            sp.dma_start(dtw[:, :], dtw_in).then_inc(S("params_in"), 16)
            sp.wait_ge(S("l0_mm_done"), 1)
            for r in range(4):
                sp.dma_start(wring[:, r], w1_in[:, r]).then_inc(S(f"wr_in{r}"), 16)
            sp.wait_ge(S("CT_act"), 1)
            sp.wait_ge(S("CT_dve"), 1)
            sp.dma_start(counts, CTf).then_inc(S("CT_moved"), 16)
            def store_rows(r, j):
                sp.wait_ge(S("y_act"), r + 1)
                sp.wait_ge(S("y_dve"), r + 1)
                sp.dma_start(table[ds(r, 1)].rearrange("r (p s) n -> p (r s) n", s=NT),
                             ystage[:, j % 2]).then_inc(S(f"y_stored{j % 2}"), 16)

            with sp.Fori(0, R // 4 - 1) as i:
                for j in range(4):
                    sp.wait_ge(S("wlow_ready"), i * 4 + j + 1)
                    sp.dma_start(wring[:, j], w1_in[:, ds(i * 4 + j + 4, 1)].rearrange("p r c n -> p (r c) n")
                                 ).then_inc(S(f"wr_in{j}"), 16)
                    store_rows(i * 4 + j, j)
            for j in range(4):
                store_rows(R - 4 + j, j)
            for j in range(2):
                sp.wait_ge(S(f"y_stored{j}"), 16 * R // 2)
            sp.sem_inc(S("table_ready"), 1)
            sp.wait_ge(S("adjacency_done"), 2)
            sp.dma_start(w2, w2_in).then_inc(S("w2_in"), 16)
            sp.wait_ge(S("lo_ready"), GR + EXTRA)
            sp.wait_ge(S("CT_moved"), 16)
            sp.dma_start(CTf, counts).then_inc(S("CT_moved"), 16)
            sp.wait_ge(S("lo_ready"), ET)
            sp.dma_start(w3, w3_in).then_inc(S("w3_in"), 16)
            sp.dma_start(rows_late, rows_in[EARLY:NROW].partition_broadcast(128)).then_inc(S("rows_late_in"), 16)
            sp.wait_ge(S("hn_ready"), 3)
            sp.dma_start(xw, xw_in).then_inc(S("xw_in"), 16)
            sp.wait_ge(S("out_ready"), 1)
            sp.dma_start(out.rearrange("(s p) f -> p s f", p=T), x[:, :, :]).then_inc(S("out_done"), 16)
            sp.wait_ge(S("out_done"), 16)

        @block.gpsimd
        def _(pool):
            pool.iota(iota[:, :], pattern=[[1, NP]], base=0, channel_multiplier=0,
                      allow_small_or_imprecise_dtypes=True).then_inc(S("iota_ready"), 1)
            pool.iota(pcol[:, :], pattern=[[1, 1]], base=0, channel_multiplier=1,
                      allow_small_or_imprecise_dtypes=True).then_inc(S("iota_ready"), 1)
            pool.iota(ncol[:, :], pattern=[[T, NT]], base=0, channel_multiplier=1,
                      allow_small_or_imprecise_dtypes=True).then_inc(S("iota_ready"), 1)
            pool.memset(zero[:, :], 0.0).then_inc(S("constants_ready"), 1)
            pool.memset(ones[:, :], 1.0).then_inc(S("constants_ready"), 1)
            pool.wait_ge(S("w0_in"), 32)
            for l in range(3):
                wl = cut(w_first[:, 1024 * l:1024 * l + 1024], 2)
                pool.tensor_tensor(wl[:, 0], wl[:, 0], wl[:, 1], ALU.subtract).then_inc(S("wd_ready"), 1)
            pool.wait_ge(S("w0_high"), 2)
            pool.tensor_tensor(w_first16[:, :, 1], cut(w_first, 3), w_first16[:, :, 0], ALU.subtract
                               ).then_inc(S("w0_low"), 1)
            pool.tensor_tensor(w_last16[:, 1], w_last, w_last16[:, 0], ALU.subtract).then_inc(S("w0_low"), 1)
            pool.wait_ge(S("idx_ready"), 1)
            pool.wait_ge(S("table_ready"), 1)
            for t in range(ET):
                if t in range(GR, GR + EXTRA, GG):
                    pool.wait_ge(S(f"gathered{(t - GR) // GG}"), 16 * GG)
                if t == GR + NT:
                    pool.wait_ge(S("CT_moved"), 16)
                if t >= GR + EXTRA:
                    pool.wait_ge(S("lo_ready"), t - GR + 1)
                pool.indirect_dma_start(gath_of(t // GR, t % GR), None, table.rearrange("r n f -> (r n) f"),
                                        bass.IndirectOffsetOnAxis(idx[:, t:t + 1], 0)
                                        ).then_inc(S(f"gathered{t % GR // GG}"), 16)
            for s in POOL_TILES:
                pool.wait_ge(S("e_exp"), EXP_ORDER.index(s) + 1)
                pool.tensor_tensor(P[:, s], P[:, s], CT[:, s:s + 1].to_broadcast([T, NH, N]), ALU.mult
                                   ).then_inc(S("p_pool"), 1)
            for n in range(NS):
                for c in range(C):
                    k = C * n + c
                    pool.wait_ge(S("scanned"), k + 1)
                    pool.wait_ge(S("C_ready"), n + 1)
                    if k >= 2:
                        pool.wait_ge(S("y_added"), k - 1)
                    pool.tensor_tensor(hc[:, c], hss[n % 2][:, c], Cs[:, n % 2], ALU.mult).then_inc(S("hc_ready"), 1)
            pool.wait_ge(S("att_used"), 1)
            pool.tensor_tensor(sa, sa, hn[:, :, :], ALU.add).then_inc(S("sa_sum"), 1)
            pool.wait_ge(S("rows_late_in"), 16)
            pool.wait_ge(S("sa_sum"), 1)
            pool.tensor_tensor(sa, sa, row("gat_b"), ALU.add).then_inc(S("sa_sum"), 1)

        @block.scalar
        def _(act):
            count = [0]

            def link(ins):
                count[0] += 1
                ins.then_inc(S("act_chain"), 1)
                act.wait_ge(S("act_chain"), count[0])

            def norm_sqrt(k):
                act.wait_ge(S("var_ready"), k)
                act.activation(sd[:, :], ve[:, :], ACT.Sqrt).then_inc(S("std_ready"), 1)

            norm_sqrt(1)
            act.wait_ge(S("tr_done"), 1)
            for c in range(C):
                act.activation(hTs[0][:, 0, c], PS[:, 2 * c * BANK:2 * c * BANK + 640]
                               .rearrange("p (s n) -> p s n", s=NT)[:, :, 0:T], ACT.Relu).then_inc(S("hT_ready"), 1)
            act.wait_ge(S("wd_ready"), 3)
            act.activation(w_first, w_first, ACT.Copy, scale=W0SCALE)
            link(act.activation(w_last, w_last, ACT.Copy, scale=W0SCALE))
            act.activation(w_first16[:, :, 0], cut(w_first, 3), ACT.Copy).then_inc(S("w0_high"), 1)
            act.activation(w_last16[:, 0], w_last, ACT.Copy).then_inc(S("w0_high"), 1)
            act.wait_ge(S("adjacency_done"), 1)
            act.activation(squares(CTf, 0, 12), adjacency(0, 12), ACT.Copy).then_inc(S("CT_act"), 1)
            for l in range(3):
                act.wait_ge(S("g_mm"), l + 1)
                act.activation(g[:, 0], nat_all(0), ACT.Copy).then_inc(S("g_ready"), 1)
                if l == 0:
                    for k, ((lo, hi), part) in enumerate(CTn_parts):
                        act.wait_ge(S("CTn_part"), k + 1)
                        act.activation(CTn[:, 0, lo:hi], part, ACT.Copy).then_inc(S("CTn_high"), 1)
                for c in range(C):
                    act.wait_ge(S("pre_masked"), C * l + c + 1)
                    act.activation(hTs[l + 1][:, 0, c], tmp[:, c], ACT.Relu).then_inc(S("hT_ready"), 1)

            def relu_transposed(k, dst):
                act.wait_ge(S("tr_done"), k)
                for c in range(C):
                    act.activation(dst[:, c], PS[:, 2 * c * BANK:2 * c * BANK + 640]
                                   .rearrange("p (s n) -> p s n", s=NT)[:, :, 0:T], ACT.Relu
                                   ).then_inc(S("hT_ready"), 1)

            norm_sqrt(2)
            relu_transposed(2, hT)
            act.wait_ge(S("gate_mm"), 1)
            act.activation(gate, PS[0:T, 6 * BANK:6 * BANK + NT * R].rearrange("p (s r) -> p s r", s=NT),
                           ACT.Sigmoid).then_inc(S("gate_ready"), 1)
            act.wait_ge(S("gate_ready"), 1)
            act.activation(gate, gate, ACT.Copy, scale=1 / WSCALE).then_inc(S("gate_ready"), 1)
            act.wait_ge(S("gate_ready"), 2)

            def high_weights(i, j):
                act.wait_ge(S(f"wr_in{j % 4}"), 16 * (i + j // 4 + 1))
                act.activation(w16[j % 4][:, 0], wring[:, j % 4], ACT.Copy, scale=WSCALE
                               ).then_inc(S("whigh_ready"), 1)

            def two_rows(i, j):
                act.wait_ge(S("y_mm"), i * 4 + j + 1)
                if j >= 2 or not isinstance(i, int) or i:
                    act.wait_ge(S(f"y_stored{j % 2}"), 16 * (i * 2 + j // 2))
                for s in range(2):
                    last = act.activation(ystage[:, j % 2, s], nat(3 * (j % 2), s), ACT.Copy,
                                          scale=gate[:, s, ds(i * 4 + j, 1)])
                last.then_inc(S("y_act"), 1)

            high_weights(0, 0)
            high_weights(0, 1)
            with act.Fori(0, R // 4 - 1) as i:
                for j in range(4):
                    high_weights(i, j + 2)
                    two_rows(i, j)
            for j in range(4):
                if j < 2:
                    high_weights(R // 4 - 1, j + 2)
                two_rows(R // 4 - 1, j)

            act.wait_ge(S("adjacency_done"), 2)
            act.activation(squares(AwTf, 0, 12), adjacency(0, 12), ACT.Copy).then_inc(S("AwT_act"), 1)
            act.wait_ge(S("edgew_in"), 16)
            with act.Fori(0, ET // GR) as i:
                for j in range(GR):
                    t = i * GR + j
                    if j % GG == 0:
                        act.wait_ge(S(f"gathered{j // GG}"), 16 * GG * (i + 1))
                    act.wait_ge(S("split_free"), t + 1)
                    act.activation(hilo[j % MRING][:, 0], gath_of(i, j), ACT.Copy, scale=edgew[:, 1, ds(t, 1)]
                                   ).then_inc(S("hi_ready"), 1)
            act.wait_ge(S("keyB_mm"), 1)
            act.activation(keyB.rearrange("p (s n) -> p s n", s=NT), keyB_ps, ACT.Copy).then_inc(S("keyB_ready"), 1)
            norm_sqrt(3)
            relu_transposed(3, hT)
            act.wait_ge(S("q_mm"), 1)
            act.activation(qT, tr(0, 0), ACT.Relu, bias=pc("bp")).then_inc(S("qT_ready"), 1)
            act.wait_ge(S("qT_ready"), 1)
            act.activation(hpT, qT, ACT.Square).then_inc(S("hpT_ready"), 1)
            act.wait_ge(S("hpn_mm"), 1)
            act.activation(hpn, PS[0:T, 2 * BANK:2 * BANK + NT * Q].rearrange("p (s n) -> p s n", s=NT), ACT.Copy
                           ).then_inc(S("hpn_ready"), 1)
            act.wait_ge(S("agg2_mm"), 1)
            act.activation(aggT, tr(0, 0), ACT.Sqrt).then_inc(S("aggT_ready"), 1)
            act.wait_ge(S("keyB_mm"), 2)
            act.activation(rankB.rearrange("p (s n) -> p s n", s=NT), keyB_ps, ACT.Copy).then_inc(S("rankB_ready"), 1)
            norm_sqrt(4)
            relu_transposed(4, hT)
            act.wait_ge(S("trow_mm"), 1)
            act.activation(trow, PS[0:NH, 6 * BANK:6 * BANK + N], ACT.Copy).then_inc(S("trow_ready"), 1)
            act.wait_ge(S("stgt_mm"), 1)
            act.activation(stgt, PS[0:T, 0:NH * N].rearrange("p (h n) -> p h n", h=NH), ACT.Copy
                           ).then_inc(S("stgt_ready"), 1)
            act.wait_ge(S("stgt_ready"), 1)
            act.wait_ge(S("ssrc_ready"), 1)

            def add_source(s):
                if s >= 2:
                    act.wait_ge(S("leaky_done"), s - 1)
                for h in range(NH):
                    last = act.activation(V[:, s % 2, h], stgt[:, h], ACT.Identity, bias=ssrc[:, s, h:h + 1])
                last.then_inc(S("v_ready"), 1)

            add_source(0)
            act.wait_ge(S("proj_mm"), 1)
            act.activation(projn[:, :, :, 0:FH], nat_all(5).rearrange("p s (h f) -> p s h f", h=NH), ACT.Copy
                           ).then_inc(S("projn_ready"), 1)
            add_source(1)
            act.wait_ge(S("xs_mm"), 1)
            for c in range(C):
                act.activation(xsT[:, c], tr(4, c), ACT.Copy).then_inc(S("xsT_ready"), 1)
            add_source(2)
            act.wait_ge(S("in_mm"), 1)
            for c in range(C):
                act.activation(xcp[:, c, 3:3 + N], tr(0, c), ACT.Copy).then_inc(S("xcp_ready"), 1)
            add_source(3)
            for c in range(C):
                act.activation(zT[:, c], tr(4, c), ACT.Silu).then_inc(S("zT_ready"), 1)
            add_source(4)
            for c in range(C):
                act.wait_ge(S("conv_done"), c + 1)
                act.activation(xc[:, c], xc[:, c], ACT.Silu, bias=pc("conv_b", c)).then_inc(S("xc_ready"), 1)

            def exponentials(s):
                act.wait_ge(S("leaky_done"), s + 1)
                if s in POOL_TILES:
                    link(act.activation(P[:, s], P[:, s], ACT.Relu, scale=-1.0, bias=gm))
                    act.activation(P[:, s], P[:, s], ACT.Exp, scale=-1.0).then_inc(S("e_exp"), 1)
                else:
                    act.activation(P[:, s], P[:, s], ACT.Exp, bias=minus_gm).then_inc(S("e_exp"), 1)

            act.activation(Aneg[:, :, :], pcols[:, PC["A_log"]:PC["A_log"] + C * NS]
                           .rearrange("p (c n) -> p c n", c=C), ACT.Exp).then_inc(S("A_exp"), 1)
            act.wait_ge(S("gm_ready"), 1)
            exponentials(EXP_ORDER[0])
            act.wait_ge(S("dbc_mm"), 1)
            act.activation(dbc, PS[:, 5 * BANK:5 * BANK + N], ACT.Copy).then_inc(S("dbc_ready"), 1)
            act.activation(parts, PS[:, 5 * BANK:5 * BANK + N], ACT.Copy).then_inc(S("dbc_ready"), 1)
            exponentials(EXP_ORDER[1])
            act.wait_ge(S("sp_abs"), 1)
            act.activation(hs, dBx, ACT.Exp, scale=-1.0).then_inc(S("sp_exp"), 1)
            for s in EXP_ORDER[2:]:
                exponentials(s)
            act.wait_ge(S("sp_w"), 1)
            act.activation(Cs, hc, ACT.Ln).then_inc(S("sp_ln"), 1)
            act.wait_ge(S("attT_mm"), 1)
            act.activation(attT[:, 0:3 * BANK], PS[0:FH + 1, 0:3 * BANK], ACT.Copy).then_inc(S("attT_act"), 1)
            act.wait_ge(S("dt_ready"), 1)
            act.wait_ge(S("A_ready"), 1)
            for n in range(NS):
                for c in range(C):
                    k = C * n + c
                    if k >= 2 * C:
                        act.wait_ge(S("scanned"), k - 2 * C + 1)
                    act.activation(dA[:, n % 2, c], dt[:, c], ACT.Exp, scale=Aneg[:, c, n:n + 1]
                                   ).then_inc(S("dA_ready"), 1)
                act.wait_ge(S("C_mm"), n + 1)
                if n >= 2:
                    act.wait_ge(S("hc_ready"), C * (n - 1))
                act.activation(Cs[:, n % 2], tr(2, 0), ACT.Copy).then_inc(S("C_ready"), 1)
            act.wait_ge(S("yn_mm"), 1)
            act.activation(yn, nat_all(0), ACT.Copy).then_inc(S("yn_ready"), 1)
            act.wait_ge(S("elu_in"), 1)
            act.activation(sb_, sb_, ACT.Exp).then_inc(S("elu_exp"), 1)
            norm_sqrt(5)
            norm_sqrt(6)
            for k, dst in ((5, hlT), (6, haT)):
                act.wait_ge(S("tr_done"), k)
                for c in range(C):
                    act.activation(dst[:, c], PS[:, 2 * c * BANK:2 * c * BANK + 640]
                                   .rearrange("p (s n) -> p s n", s=NT)[:, :, 0:T], ACT.Copy
                                   ).then_inc(S("hT_ready"), 1)
            for k, (lo, hi) in enumerate(BANKED):
                act.wait_ge(S("g2_mm"), k + 1)
                act.activation(gt[:, lo:hi], nat_all(4)[:, lo:hi], ACT.Sigmoid).then_inc(S("gt_ready"), 1)
            act.wait_ge(S("tr_done"), 7)
            for c in range(C):
                act.activation(hfT[:, c], PS[:, 2 * c * BANK:2 * c * BANK + 640]
                               .rearrange("p (s n) -> p s n", s=NT)[:, :, 0:T], ACT.Copy
                               ).then_inc(S("hT_ready"), 1)
            for m in range(2 * C):
                act.wait_ge(S("ff1_mm"), m + 1)
                act.activation(f1T[:, m], tr(0, m % 2), ACT.Relu, bias=pc("ff1_b", m)).then_inc(S("f1_ready"), 1)
            norm_sqrt(7)

        @block.tensor
        def _(pe):
            mm = pe.matmul

            def transposes(src, k):
                for c in range(C):
                    for s in range(NT):
                        last = pe.transpose(PS[:, 2 * c * BANK + 128 * s:2 * c * BANK + 128 * s + T],
                                            src[:, s, 128 * c:128 * c + 128], ident[0:T, 0:T])
                last.then_inc(S("tr_done"), 1)

            def rows_product(bank, lT, r, first, banks_done=None):
                for lo, hi in BANKED:
                    for s in range(lo, hi):
                        last = mm(nat(bank, s), lT[:, s * T:s * T + T], r, start=first and s == lo, stop=False,
                                  skip_group_check=True)
                    if banks_done:
                        last.then_inc(S(banks_done), 1)
                return last

            def wide(out_at, rows_, ops):
                for lo, hi in pieces(out_at, out_at + N):
                    for i, (l, r) in enumerate(ops):
                        last = mm(PS[0:rows_, lo:hi], l, r[:, lo - out_at:hi - out_at],
                                  start=i == 0, stop=i == len(ops) - 1)
                return last

            pe.wait_ge(S("ident_ready"), 1)
            pe.wait_ge(S("edgef_ready"), 1)
            pe.transpose(PS[0:ET, 7 * BANK:7 * BANK + T], edgef[:, 1], ident[0:T, 0:T]).then_inc(S("targets_mm"), 1)
            pe.wait_ge(S("hn_ready"), 1)
            transposes(hn, 1)
            pe.wait_ge(S("hlow_ready"), 2)

            pe.wait_ge(S("span_ready"), 1)
            for k in range(2):
                last = pe.transpose(PS[0:1, 7 * BANK + 128 * k:7 * BANK + 128 * k + ET], span[:, k:k + 1],
                                    ident[0:ET, 0:ET])
            last.then_inc(S("spans_mm"), 1)
            pe.wait_ge(S("reached_ready"), 1)
            reached_regs = [pe.alloc_register(f"reached{d}") for d in range(UN * (NT + 2))]

            def for_reached(table_, i, u, add, un=UN, count=None):
                if u == 0:
                    count = count or un
                    pe.load(reached_regs[0:count * (NT + 2)], table_[0:1, ds(i * un, count)])
                reached_reg = reached_regs[(NT + 2) * u:]
                for half_, tiles in enumerate((range(LOW), range(LOW, NT))):
                    with pe.If_ne(reached_reg[NT + half_], 0):
                        for d in tiles:
                            with pe.If_ne(reached_reg[d], 0):
                                add(d)

            def clear(banks):
                for b in banks:
                    mm(PS[:, b * BANK:(b + 1) * BANK], zero[0:T, :], iota[0:T, 0:BANK], start=True, stop=False,
                       skip_group_check=True)

            def keep_warm(bank, count):
                for _ in range(count):
                    mm(PS[:, bank * BANK:(bank + 1) * BANK], zero[0:T, :], iota[0:T, 0:BANK], start=True, stop=True)

            def close(at_):
                return mm(PS[:, at_:at_ + 16], zero[0:T, :], iota[0:T, 0:16], start=False, stop=False,
                          skip_group_check=True)

            def add_edges(i, u, sources, counted=False, un=UN, count=None):
                def add(d):
                    for j in range(GT):
                        onehot = ohd[:, ds(i * (un * GT * NP) + ((GT * u + j) * NP + d * T), T)]
                        for s in range(NT):
                            at_ = d * 128 + s * 640
                            for src_ in sources[j]:
                                mm(PS[0:T, at_:at_ + T], src_[:, s * T:s * T + T], onehot, start=False,
                                   stop=False, skip_group_check=True)
                        if counted:
                            at_ = (NT * NT + d) * 128
                            mm(PS[:, at_:at_ + T], ones[0:T, :].to_broadcast([T, 128]), onehot,
                               start=False, stop=False, skip_group_check=True)

                for_reached(reached, i, u, add, un, count)

            pe.wait_ge(S("constants_ready"), 2)
            clear(range(8))
            pe.sem_inc(S("ohs_used"), ARING)
            with pe.Fori(0, GROUPS // UN) as i:
                for u in range(UN):
                    pe.wait_ge(S("onehots"), 2 * GT * (i * UN + u + 1))
                    add_edges(i, u, [[ohs[(GT * u + j) % ARING]] for j in range(GT)], True)
                    close(0).then_inc(S("ohs_used"), GT)
            close(0).then_inc(S("adjacency_done"), 1)
            pe.wait_ge(S("w0_low"), 2)
            pe.wait_ge(S("CT_act"), 1)
            for l in range(3):
                h, w = hTs[l], wl0[l]
                for c in range(C):
                    if l:
                        pe.wait_ge(S("hlow_ready"), C * l + c + 1)
                    for a, b in HALVES:
                        last = rows_product(0, h[:, a, c], w[:, b, 2 + c], c + a + b == 0)
                last.then_inc(S("g_mm"), 1)
                if l == 0:
                    pe.wait_ge(S("CT_dve"), 1)
                    pe.wait_ge(S("cnt_used"), 1)

                def sums(m, ops, first):
                    at_ = (3 + 2 * m) * BANK
                    for lo, hi in pieces(at_, at_ + N):
                        for i, (l_, r) in enumerate(ops):
                            last = mm(PS[:, lo:hi], l_, r[:, lo - at_:hi - at_], start=first and i == 0, stop=False,
                                      skip_group_check=True)
                    return last

                for m in range(C):
                    sums(m, [(w[:, b, c, 128 * m:128 * m + 128], h[:, a, c]) for c in range(C) for a, b in HALVES],
                         True)
                pe.wait_ge(S("glow_ready"), l + 1)
                pe.wait_ge(S("CTn_ready"), len(CTn_parts))
                for m in range(C):
                    sums(m, [(g[:, a, s, 128 * m:128 * m + 128], CTn[:, b, s]) for s in range(NT) for a, b in HALVES],
                         False).then_inc(S("pre_mm"), 1)
            for k in range(4 * C):
                if k >= 3 * C:
                    pe.wait_ge(S("hlow_ready"), k + 1)
                for a, b in HALVES:
                    last = rows_product(0, hTs[k // C][:, a, k % C], wf[:, b, k], k + a + b == 0)
            last.then_inc(S("l0_mm_done"), 1)
            pe.wait_ge(S("hn_ready"), 2)
            transposes(hn, 2)
            pe.wait_ge(S("hT_ready"), 10)
            pe.wait_ge(S("params_in"), 64)

            def spread(c, s):
                return hT[:, c].rearrange("p (n s) -> p s n", s=NT)[:, s]

            for s in range(NT):
                for c in range(C):
                    last = mm(PS[0:T, 6 * BANK + s * R:6 * BANK + s * R + R], spread(c, s), gw[:, c],
                              start=c == 0, stop=c == C - 1)
            last.then_inc(S("gate_mm"), 1)
            pe.wait_ge(S("hT16_ready"), 1)
            def relation(i, j, first):
                pe.wait_ge(S("wlow_ready"), i * 4 + j + 1)
                if not first:
                    pe.wait_ge(S("y_act"), i * 4 + j - 1)
                    pe.wait_ge(S("y_dve"), i * 4 + j - 1)
                for s in range(NT):
                    for c in range(C):
                        for k, (a, b) in enumerate(HALVES):
                            last = mm(nat(3 * (j % 2), s), hT16[:, a, c, s], w16[j][:, b, c],
                                      start=c + k == 0, stop=c + k == C + 1)
                last.then_inc(S("y_mm"), 1)

            for j in range(4):
                relation(0, j, j < 2)
            with pe.Fori(1, R // 4) as i:
                for j in range(4):
                    relation(i, j, False)
            pe.wait_ge(S("y_act"), R)
            pe.wait_ge(S("y_dve"), R)
            clear(range(7))
            pe.sem_inc(S("wohs_used"), WRING)

            def weighted_groups(i, count):
                for u in range(count):
                    pe.wait_ge(S("wonehots"), GT * (i * WUN + u + 1))
                    add_edges(i, u, [[wohs[GT * u + j][:, k] for k in range(2)] for j in range(GT)], un=WUN,
                              count=count)
                    close(0).then_inc(S("wohs_used"), GT)

            with pe.Fori(0, GROUPS // WUN) as i:
                weighted_groups(i, WUN)
            weighted_groups(GROUPS // WUN, GROUPS % WUN)
            close(0).then_inc(S("adjacency_done"), 1)
            pe.wait_ge(S("AwT_act"), 1)
            pe.wait_ge(S("AwT_dve"), 1)

            clear(range(3))
            pe.wait_ge(S("reached_ready"), 2)
            pe.sem_inc(S("split_free"), MRING)
            with pe.Fori(0, MGROUPS // UN) as i:
                for u in range(UN):
                    pe.wait_ge(S("hi_ready"), MT * (i * UN + u + 1))
                    pe.wait_ge(S("lo_ready"), MT * (i * UN + u + 1))

                    def add(d):
                        for j in range(MT * u, MT * (u + 1)):
                            for k in range(2):
                                mm(PS[0:T, d * D:d * D + D], ohd[:, ds(i * (UN * MT * NP) + (j * NP + d * T), T)],
                                   hilo[j % MRING][:, k], start=False, stop=False, skip_group_check=True)

                    for_reached(reached_m, i, u, add)
                    close(0).then_inc(S("split_free"), MT)

            def along_columns(col):
                for s in range(NT):
                    last = pe.transpose(PS[0:T, 3 * BANK + s * 128:3 * BANK + s * 128 + T],
                                        col[:, s:s + 1].to_broadcast([T, T]), ident[0:T, 0:T])
                last.then_inc(S("keyB_mm"), 1)

            along_columns(key)
            pe.wait_ge(S("keyB_ready"), 1)
            keep_warm(4, 12)
            pe.wait_ge(S("hn_ready"), 3)
            transposes(hn, 3)
            pe.wait_ge(S("hT_ready"), 12)
            pe.wait_ge(S("w2_in"), 16)
            wide(0, 128, [(w2[:, 128 * c:128 * c + 128], hT[:, c]) for c in range(C)]).then_inc(S("q_mm"), 1)
            pe.wait_ge(S("qT_ready"), 1)
            rows_product(5, qT, w2[:, 256:512], True)
            pe.wait_ge(S("hpT_ready"), 1)
            for s in range(NT):
                last = pe.transpose(PS[0:T, 2 * BANK + s * Q:2 * BANK + s * Q + Q], hpT[:, s * T:s * T + T],
                                    ident[:, :])
            last.then_inc(S("hpn_mm"), 1)
            pe.wait_ge(S("hpn_ready"), 1)
            wide(0, 128, [(hpn[:, s], AwT[:, s]) for s in range(NT)]).then_inc(S("agg2_mm"), 1)
            pe.wait_ge(S("rank_ready"), 1)
            along_columns(rank)
            pe.wait_ge(S("aggT_ready"), 1)
            rows_product(5, aggT, w2[:, 512:768], False).then_inc(S("l2_mm"), 1)
            pe.wait_ge(S("w3_in"), 16)
            pe.wait_ge(S("rankB_ready"), 1)
            pe.wait_ge(S("hn_ready"), 4)
            transposes(hn, 4)
            pe.wait_ge(S("hT_ready"), 14)
            pe.wait_ge(S("wst_ready"), 1)
            wide(6 * BANK, NH, [(wst[:, 1, c], hT[:, c]) for c in range(C)]).then_inc(S("trow_mm"), 1)
            for s in range(NT):
                for c in range(C):
                    last = mm(PS[0:T, 5 * BANK + s * NH:5 * BANK + s * NH + NH], hT[:, c, s * T:s * T + T],
                              wst[:, 0, c], start=s + c == 0, stop=False, skip_group_check=True)
            last.then_inc(S("ssrc_mm"), 1)
            pe.wait_ge(S("trow_ready"), 1)
            for h in range(NH):
                for lo, hi in pieces(h * N, h * N + N):
                    last = mm(PS[0:T, lo:hi], ident[0:NH, h:h + 1].to_broadcast([NH, T]),
                              trow[:, lo - h * N:hi - h * N], start=True, stop=True)
            last.then_inc(S("stgt_mm"), 1)
            pe.wait_ge(S("ssrc_ready"), 1)
            gatw = W("gat", C * D).rearrange("p (c n) -> p c n", c=C)
            for s in range(NT):
                for c in range(C):
                    last = mm(nat(5, s), hT[:, c, s * T:s * T + T], gatw[:, c], start=c == 0, stop=c == C - 1)
            last.then_inc(S("proj_mm"), 1)
            pe.wait_ge(S("hn16_ready"), 1)
            pe.wait_ge(S("stgt_ready"), 1)
            pe.wait_ge(S("projn_ready"), 1)
            for m in range(C):
                last = wide((4 + 2 * m) * BANK, 128, [(hn16[:, k, s, 128 * m:128 * m + 128], PT[:, s])
                                                      for s in range(NT) for k in range(2)])
            last.then_inc(S("xs_mm"), 1)
            pe.wait_ge(S("xsT_ready"), 2)
            inw = W("in", 2 * C * D).rearrange("p (c n) -> p c n", c=C)
            for m in range(2 * C):
                last = wide(2 * m * BANK, 128, [(inw[:, c, 128 * m:128 * m + 128], xsT[:, c]) for c in range(C)])
            last.then_inc(S("in_mm"), 1)
            pe.wait_ge(S("xcp_ready"), 2)
            pe.wait_ge(S("mx_ready"), 1)
            pe.transpose(PS[0:T, 0:T], m1.to_broadcast([T, T]), ident[0:T, 0:T]).then_inc(S("mxT"), 1)
            pe.wait_ge(S("xc_ready"), 2)
            pe.wait_ge(S("zT_ready"), 2)
            pe.wait_ge(S("xw_in"), 16)
            wide(5 * BANK, 128, [(xw[:, c], xc[:, c]) for c in range(C)]).then_inc(S("dbc_mm"), 1)
            pe.wait_ge(S("dbc_ready"), 2)
            for m in range(C):
                last = wide(5 * BANK + N * m, 128, [(dtw[:, 128 * m:128 * m + 128], dbc[0:RK])])
            last.then_inc(S("dt_mm"), 1)
            started = set()
            for k, s in enumerate(P_ORDER):
                if s in POOL_TILES:
                    pe.wait_ge(S("p_pool"), POOL_TILES.index(s) + 1)
                else:
                    pe.wait_ge(S("p_dve"), DVE_TILES.index(s) + 1)
                for h in range(NH):
                    for lo, hi in pieces(h * N, h * N + N):
                        first = lo // BANK not in started
                        started.add(lo // BANK)
                        last = mm(PS[0:FH + 1, lo:hi], projn[:, s, h], P[:, s, h, lo - h * N:hi - h * N],
                                  start=first, stop=k == NT - 1, skip_group_check=True)
            last.then_inc(S("attT_mm"), 1)
            pe.wait_ge(S("attT_act"), 1)
            pe.wait_ge(S("attT_dve"), 1)
            for d in range(NT):
                for h in range(NH):
                    last = pe.transpose(PS[0:T, d * BANK + h * 65:d * BANK + h * 65 + 65],
                                        attT[:, h * N + d * T:h * N + d * T + T], ident[0:FH + 1, 0:FH + 1])
            last.then_inc(S("att_mm"), 1)
            pe.wait_ge(S("att_used"), 1)
            pe.wait_ge(S("dt_ready"), 1)
            pe.wait_ge(S("parts_ready"), 1)

            def add_states(n):
                for c in range(C):
                    pe.wait_ge(S("hc_ready"), C * n + c + 1)
                    for lo, hi in pieces(0, N):
                        last = mm(tr(4, c)[:, lo:hi], ident[:, :], hc[:, c, lo:hi],
                                  start=n == 0, stop=n == NS - 1, skip_group_check=True)
                    last.then_inc(S("y_added"), 1)

            for n in range(NS):
                for k, name in enumerate("BC"):
                    if n:
                        pe.wait_ge(S("C_ready" if k else "B_used"), n if k else C * n)
                    row_ = pick[:, k * NS + n:k * NS + n + 1].to_broadcast([128, 128])
                    wide(2 * k * BANK, 128, [(row_, parts)]).then_inc(S(f"{name}_mm"), 1)
                if n >= 2:
                    add_states(n - 2)
            add_states(NS - 2)
            add_states(NS - 1)
            pe.wait_ge(S("C_ready"), NS)
            ow = W("out", C * D).rearrange("p (c n) -> p c n", c=C)
            for c in range(C):
                pe.wait_ge(S("yT_ready"), c + 1)
                last = rows_product(0, xc[:, c], ow[:, c], c == 0)
            last.then_inc(S("yn_mm"), 1)
            pe.wait_ge(S("yn_ready"), 1)
            pe.wait_ge(S("PTt_ready"), 1)
            for lo, hi in BANKED:
                for d in range(lo, hi):
                    for s in range(NT):
                        last = mm(nat(4, d), PTt[:, s, d * T:d * T + T], yn[:, s], start=s == 0, stop=s == NT - 1)
                last.then_inc(S("back_mm"), 1)
            pe.wait_ge(S("hl_ready"), 1)
            transposes(hl, 5)
            pe.wait_ge(S("hT_ready"), 16)
            pe.wait_ge(S("back_used"), len(BANKED))
            wl = W("wl", C * D).rearrange("p (c n) -> p c n", c=C)
            wg = W("wg", C * D).rearrange("p (c n) -> p c n", c=C)
            for c in range(C):
                rows_product(4, hlT[:, c], wl[:, c], c == 0)
            pe.wait_ge(S("ha_ready"), 1)
            transposes(ha, 6)
            pe.wait_ge(S("hT_ready"), 18)
            for c in range(C):
                rows_product(4, haT[:, c], wg[:, c], False, "g2_mm" if c == C - 1 else None)
            for k, (lo, hi) in enumerate(BANKED):
                pe.wait_ge(S("hf_ready"), k + 1)
                for s in range(lo, hi):
                    for c in range(C):
                        last = pe.transpose(PS[:, 2 * c * BANK + 128 * s:2 * c * BANK + 128 * s + T],
                                            hf[:, s, 128 * c:128 * c + 128], ident[0:T, 0:T])
            last.then_inc(S("tr_done"), 1)
            pe.wait_ge(S("hT_ready"), 20)
            w1 = W("ff1", 2 * C * D).rearrange("p (c n) -> p c n", c=C)
            w2_ = W("ff2", 2 * C * D).rearrange("p (c n) -> p c n", c=2 * C)
            for m in range(2 * C + 1):
                if m < 2 * C:
                    if m >= 2:
                        pe.wait_ge(S("f1_ready"), m - 1)
                    wide(2 * (m % 2) * BANK, 128, [(w1[:, c, 128 * m:128 * m + 128], hfT[:, c]) for c in range(C)]
                         ).then_inc(S("ff1_mm"), 1)
                if m:
                    pe.wait_ge(S("f1_ready"), m)
                    rows_product(4, f1T[:, m - 1], w2_[:, m - 1], m == 1, "ff2_mm" if m == 2 * C else None)

        @block.vector
        def _(dve):
            count = [0]

            def link(ins):
                count[0] += 1
                ins.then_inc(S("dve_chain"), 1)
                dve.wait_ge(S("dve_chain"), count[0])

            def norm(src, dst, k, g=None, b=None, middle=None, make=None):
                for k_, (lo, hi) in enumerate(BANKED):
                    if make:
                        make(k_, lo, hi)
                    for s in range(lo, hi):
                        last = dve.bn_stats(st[:, s], src[:, s])
                link(last)
                for s in range(NT):
                    last = dve.bn_aggr(mv[:, s], st[:, s])
                link(last)
                dve.tensor_scalar(ve[:, :], mv[:, :, 1], EPS, None, ALU.add).then_inc(S("var_ready"), 1)
                dve.wait_ge(S("std_ready"), k)
                link(dve.reciprocal(rstd[:, :], sd[:, :]))
                link(dve.tensor_tensor(sd[:, :], rstd[:, :], rstd[:, :], ALU.mult))
                link(dve.tensor_tensor(sd[:, :], sd[:, :], ve[:, :], ALU.mult))
                link(dve.tensor_scalar(sd[:, :], sd[:, :], -0.5, 1.5, ALU.mult, ALU.add))
                link(dve.tensor_tensor(rstd[:, :], rstd[:, :], sd[:, :], ALU.mult))
                for s in range(NT):
                    if g is None:
                        last = dve.tensor_scalar(dst[:, s], src[:, s], mv[:, s, 0:1], rstd[:, s:s + 1],
                                                 ALU.subtract, ALU.mult)
                    else:
                        last = dve.scalar_tensor_tensor(middle[:, s], src[:, s], mv[:, s, 0:1], g[:, s],
                                                        ALU.subtract, ALU.mult)
                if g is not None:
                    link(last)
                    for s in range(NT):
                        last = dve.scalar_tensor_tensor(dst[:, s], middle[:, s], rstd[:, s:s + 1], b[:, s],
                                                        ALU.mult, ALU.add)
                return last

            dve.wait_ge(S("iota_ready"), 3)
            dve.tensor_scalar(ident[:, :], iota[:, 0:128], pcol[:, 0:1], None, ALU.is_equal
                              ).then_inc(S("ident_ready"), 1)
            dve.wait_ge(S("ident_ready"), 1)
            link(dve.tensor_tensor(pick[:, :], ident[:, 32:64], ident[:, 64:96], ALU.add))
            dve.tensor_tensor(pick[:, :], pick[:, :], ident[:, 96:128], ALU.add)
            dve.wait_ge(S("edges_in"), 16)
            dve.tensor_copy(edgef[:, :, :], edgei[:, :, :]).then_inc(S("edgef_ready"), 1)
            dve.wait_ge(S("edgef_ready"), 1)
            dve.wait_ge(S("targets_mm"), 1)
            dve.tensor_reduce(span[:, 0:1], PS[0:ET, 7 * BANK:7 * BANK + T], AX_X, ALU.min)
            dve.tensor_reduce(span[:, 1:2], PS[0:ET, 7 * BANK:7 * BANK + T], AX_X, ALU.max
                              ).then_inc(S("span_ready"), 1)
            dve.wait_ge(S("x_in"), 16)
            norm(x, hn, 1).then_inc(S("hn_ready"), 1)
            dve.wait_ge(S("hT_ready"), C)
            for c in range(C):
                dve.scalar_tensor_tensor(cut(hTs[0][:, 1, c], NT), PS[:, 2 * c * BANK:2 * c * BANK + 640]
                                         .rearrange("p (s n) -> p s n", s=NT)[:, :, 0:T], 0.0,
                                         cut(hTs[0][:, 0, c], NT), ALU.max, ALU.subtract
                                         ).then_inc(S("hlow_ready"), 1)
            dve.wait_ge(S("spans_mm"), 1)
            for k, op in enumerate((ALU.min, ALU.max)):
                at_ = 7 * BANK + 128 * k
                dve.tensor_reduce(spans_m[:, k], PS[0:1, at_:at_ + ET].rearrange("p (g j) -> p g j", j=MT), AX_X, op)
                link(dve.tensor_reduce(spans[:, k], PS[0:1, at_:at_ + ET].rearrange("p (g j) -> p g j", j=GT),
                                       AX_X, op))

            def reach(spans_, table_):
                for k, (first, end) in enumerate([(d, d + 1) for d in range(NT)] + [(0, LOW), (LOW, NT)]):
                    link(dve.tensor_scalar(spans_[:, 2], spans_[:, 0], float(T * end), None, ALU.is_lt))
                    link(dve.scalar_tensor_tensor(table_[:, :, k], spans_[:, 1], float(T * first), spans_[:, 2],
                                                  ALU.is_ge, ALU.mult))

            reach(spans, reached)
            dve.sem_inc(S("reached_ready"), 1)
            link(dve.tensor_scalar(idxf, edgef[:, 2], float(N), None, ALU.mult))
            link(dve.tensor_tensor(idxf, idxf, edgef[:, 0], ALU.add))
            dve.tensor_copy(idx[:, :], idxf).then_inc(S("idx_ready"), 1)
            with dve.Fori(0, ET // ARING) as i:
                for j in range(ARING):
                    t = i * ARING + j
                    dve.tensor_scalar(ohd[:, ds(t * NP, NP)], iota[0:T, :], edgef[:, 1, ds(t, 1)], None, ALU.is_equal
                                      ).then_inc(S("onehots"), 1)
                    dve.wait_ge(S("ohs_used"), t + 1)
                    dve.tensor_scalar(ohs[j], iota[0:T, :], edgef[:, 0, ds(t, 1)], None, ALU.is_equal
                                      ).then_inc(S("onehots"), 1)
            dve.wait_ge(S("adjacency_done"), 1)
            dve.wait_ge(S("w0_low"), 2)
            cnt = PS[:, NT * NT * 128:(NT * NT + NT) * 128].rearrange("p (d n) -> p d n", d=NT)[:, :, 0:T]
            link(dve.tensor_scalar(cut(rcB, NT), cnt, 1.0, None, ALU.max))
            dve.tensor_scalar(cut(zB, NT), cnt, 1.0, 1 / W0SCALE, ALU.min, ALU.mult).then_inc(S("cnt_used"), 1)
            link(dve.reciprocal(rcB, rcB))
            dve.tensor_copy(squares(CTf, 12, 25), adjacency(12, 25)).then_inc(S("CT_dve"), 1)
            dve.wait_ge(S("CT_dve"), 1)
            dve.wait_ge(S("CT_act"), 1)
            for (lo, hi), part in CTn_parts:
                dve.tensor_tensor(part, CT[:, lo:hi], A1[0:T, 12650:12650 + N].rearrange("p (s n) -> p s n", s=1)
                                  .to_broadcast([T, hi - lo, N]), ALU.mult).then_inc(S("CTn_part"), 1)
            for l in range(3):
                dve.wait_ge(S("g_ready"), l + 1)
                dve.tensor_tensor(g[:, 1], nat_all(0), g[:, 0], ALU.subtract).then_inc(S("glow_ready"), 1)
                if l == 0:
                    for k, ((lo, hi), part) in enumerate(CTn_parts):
                        dve.wait_ge(S("CTn_high"), k + 1)
                        dve.tensor_tensor(CTn[:, 1, lo:hi], part, CTn[:, 0, lo:hi], ALU.subtract
                                          ).then_inc(S("CTn_ready"), 1)
                    link(dve.tensor_reduce(deg[:, :], CT[:, :, :], AX_X, ALU.add))
                    dve.wait_ge(S("params_in"), 64)
                    link(dve.tensor_tensor(key[:, :], deg[:, :], noise_sb[:, :], ALU.add))
                    dve.wait_ge(S("rows_in"), 16)
                    link(dve.tensor_tensor(x[:, :, :], x[:, :, :], row("bf"), ALU.add))
                    dve.wait_ge(S("params_in"), 64)
                    link(dve.tensor_scalar(pcols[:, 0:3 * C], pcols[:, 0:3 * C], W0SCALE, None, ALU.mult))
                for c in range(C):
                    dve.wait_ge(S("pre_mm"), C * l + c + 1)
                    dve.scalar_tensor_tensor(tmp[:, c], tr(3, c), pc(f"b{l}", c), zB, ALU.add, ALU.mult
                                             ).then_inc(S("pre_masked"), 1)
                    dve.wait_ge(S("hT_ready"), C * (l + 1) + c + 1)
                    dve.scalar_tensor_tensor(hTs[l + 1][:, 1, c], tmp[:, c], 0.0, hTs[l + 1][:, 0, c],
                                             ALU.max, ALU.subtract).then_inc(S("hlow_ready"), 1)
            dve.wait_ge(S("l0_mm_done"), 1)
            link(dve.scalar_tensor_tensor(x[:, :, :], nat_all(0), 1 / W0SCALE, x[:, :, :], ALU.mult, ALU.add))
            norm(x, hn, 2).then_inc(S("hn_ready"), 1)
            dve.wait_ge(S("hT_ready"), 10)
            hTs_ = hT.rearrange("p c (n s) -> p c s n", s=NT)
            link(dve.tensor_copy(hT16[:, 0], hTs_))
            dve.tensor_tensor(hT16[:, 1], hTs_, hT16[:, 0], ALU.subtract).then_inc(S("hT16_ready"), 1)

            def low_weights(i, j):
                dve.wait_ge(S("whigh_ready"), i * 4 + j + 1)
                dve.scalar_tensor_tensor(w16[j % 4][:, 1], wring[:, j % 4], WSCALE, w16[j % 4][:, 0],
                                         ALU.mult, ALU.subtract).then_inc(S("wlow_ready"), 1)

            def three_rows(i, j):
                dve.wait_ge(S("y_mm"), i * 4 + j + 1)
                if j >= 2 or not isinstance(i, int) or i:
                    dve.wait_ge(S(f"y_stored{j % 2}"), 16 * (i * 2 + j // 2))
                dve.tensor_tensor(ystage[:, j % 2, 2:5], nat_all(3 * (j % 2))[:, 2:5],
                                  gate[:, 2:5, ds(i * 4 + j, 1)].to_broadcast([T, 3, D]), ALU.mult
                                  ).then_inc(S("y_dve"), 1)

            low_weights(0, 0)
            low_weights(0, 1)
            dve.wait_ge(S("gate_ready"), 1)
            reach(spans_m, reached_m)
            dve.sem_inc(S("reached_ready"), 1)
            dve.wait_ge(S("edgew_in"), 16)
            link(dve.tensor_copy(wsplit16, edgew[:, 0]))
            link(dve.tensor_copy(wsplit[:, 0], wsplit16))
            link(dve.tensor_tensor(wsplit[:, 1], edgew[:, 0], wsplit[:, 0], ALU.subtract))
            dve.wait_ge(S("gate_ready"), 2)
            with dve.Fori(0, R // 4 - 1) as i:
                for j in range(4):
                    low_weights(i, j + 2)
                    three_rows(i, j)
            for j in range(4):
                if j < 2:
                    low_weights(R // 4 - 1, j + 2)
                three_rows(R // 4 - 1, j)

            def weighted_onehots(i, count):
                for j in range(count):
                    t = i * WRING + j
                    dve.wait_ge(S("wohs_used"), t + 1)
                    if j == 7:
                        dve.wait_ge(S("y_stored0"), 16 * R // 2)
                        dve.wait_ge(S("y_stored1"), 16 * R // 2)
                    for k in range(2):
                        last = dve.tensor_scalar(wohs[j][:, k], iota[0:T, :], edgef[:, 0, ds(t, 1)],
                                                 wsplit[:, k, ds(t, 1)], ALU.is_equal, ALU.mult)
                    last.then_inc(S("wonehots"), 1)

            with dve.Fori(0, ET // WRING) as i:
                weighted_onehots(i, WRING)
            weighted_onehots(ET // WRING, ET % WRING)
            dve.wait_ge(S("adjacency_done"), 2)
            dve.tensor_copy(squares(AwTf, 12, 25), adjacency(12, 25)).then_inc(S("AwT_dve"), 1)
            with dve.Fori(0, ET // GR) as i:
                for j in range(GR):
                    t = i * GR + j
                    dve.wait_ge(S("hi_ready"), t + 1)
                    dve.scalar_tensor_tensor(hilo[j % MRING][:, 1], gath_of(i, j), edgew[:, 1, ds(t, 1)],
                                             hilo[j % MRING][:, 0], ALU.mult, ALU.subtract).then_inc(S("lo_ready"), 1)
            dve.wait_ge(S("split_free"), MRING + ET)
            link(dve.scalar_tensor_tensor(x[:, :, :], nat_all(0), 0.0, x[:, :, :], ALU.max, ALU.add))
            norm(x, hn, 3).then_inc(S("hn_ready"), 1)
            dve.wait_ge(S("keyB_ready"), 1)
            for s in range(NT):
                link(dve.tensor_scalar(low, iota[0:T, 0:N], ncol[0:T, s:s + 1], None, ALU.is_lt))
                link(dve.tensor_scalar(junk, keyB, key[:, s:s + 1], None, ALU.is_lt, ALU.add,
                                       accum_out=rank[:, s:s + 1]))
                link(dve.scalar_tensor_tensor(junk, keyB, key[:, s:s + 1], low, ALU.is_equal, ALU.mult,
                                              accum_out=rank2[:, s:s + 1]))
            dve.tensor_tensor(rank[:, :], rank[:, :], rank2[:, :], ALU.add).then_inc(S("rank_ready"), 1)
            link(dve.tensor_tensor(x[:, :, :], x[:, :, :], row("b1"), ALU.add))
            link(dve.tensor_tensor(x[:, :, :], x[:, :, :], row("b2"), ALU.add))
            dve.wait_ge(S("w3_in"), 16)
            dve.wait_ge(S("rows_late_in"), 16)
            for k, name in enumerate(("a_src", "a_tgt")):
                i = ROW[name] - EARLY
                link(dve.tensor_tensor(wprod, W("gat", C * D).rearrange("p (c n) -> p c n", c=C),
                                       rows_late[:, i:i + 1, :].to_broadcast([128, C, D]), ALU.mult))
                link(dve.tensor_reduce(wst[:, k], wprod.rearrange("p c (h f) -> p c h f", h=NH), AX_X, ALU.add))
            dve.sem_inc(S("wst_ready"), 1)
            dve.wait_ge(S("CT_moved"), 32)
            link(dve.tensor_scalar(far, CT[:, :, :], 0.0, FAR, ALU.is_equal, ALU.mult))
            dve.wait_ge(S("rank_ready"), 1)
            dve.wait_ge(S("agg2_mm"), 1)
            for s in range(NT):
                dve.tensor_scalar(PT[:, s], iota[0:T, 0:N], rank[:, s:s + 1], None, ALU.is_equal)
            dve.wait_ge(S("l2_mm"), 1)
            link(dve.tensor_tensor(x[:, :, :], x[:, :, :], nat_all(5), ALU.add))
            link(norm(x, hn, 4))
            dve.tensor_scalar(hn[:, :, :], hn[:, :, :], 0.0, None, ALU.max).then_inc(S("hn_ready"), 1)
            dve.memset(projn[:, :, :, FH:FH + 1], 1.0)
            dve.wait_ge(S("hn_ready"), 4)
            link(dve.tensor_copy(hn16[:, 0], hn[:, :, :]))
            dve.tensor_tensor(hn16[:, 1], hn[:, :, :], hn16[:, 0], ALU.subtract).then_inc(S("hn16_ready"), 1)
            dve.wait_ge(S("ssrc_mm"), 1)
            dve.tensor_copy(ssrc, PS[0:T, 5 * BANK:5 * BANK + NT * NH].rearrange("p (s h) -> p s h", s=NT)
                            ).then_inc(S("ssrc_ready"), 1)
            sa4 = sa.rearrange("p s (h f) -> p s h f", h=NH)
            dve.memset(xcp[:, :, 0:3], 0.0)
            def convolve():
                for c in range(C):
                    dve.wait_ge(S("xcp_ready"), c + 1)
                    link(dve.tensor_scalar(xc[:, c], xcp[:, c, 0:N], pc("conv_w", K4 * c), None, ALU.mult))
                    for k in range(1, K4):
                        last = dve.scalar_tensor_tensor(xc[:, c], xcp[:, c, k:k + N], pc("conv_w", K4 * c + k),
                                                        xc[:, c], ALU.mult, ALU.add)
                        if k < K4 - 1:
                            link(last)
                    last.then_inc(S("conv_done"), 1)

            dve.wait_ge(S("stgt_ready"), 1)
            for s in range(NT):
                for h in range(NH):
                    last = dve.tensor_tensor_reduce(out=P[:, s, h], in0=stgt[:, h], in1=far[:, s], scale=1.0,
                                                    scalar=-3.0e38, op0=ALU.add, op1=ALU.max,
                                                    accum_out=mx[:, s, h:h + 1])
            link(last)
            dve.wait_ge(S("ssrc_ready"), 1)
            link(dve.tensor_tensor(mx, mx, ssrc, ALU.add))
            dve.tensor_reduce(m1, den_flat, AX_X, ALU.max).then_inc(S("mx_ready"), 1)

            def leaky(s):
                dve.wait_ge(S("v_ready"), s + 1)
                dve.scalar_tensor_tensor(P[:, s], V[:, s % 2], 0.2, V[:, s % 2], ALU.mult, ALU.max
                                         ).then_inc(S("leaky_done"), 1)

            leaky(0)
            leaky(1)
            leaky(2)
            convolve()
            dve.wait_ge(S("mxT"), 1)
            link(dve.tensor_reduce(gm, PS[0:T, 0:T], AX_X, ALU.max))
            link(dve.scalar_tensor_tensor(gm, gm, 0.2, gm, ALU.mult, ALU.max))
            dve.tensor_scalar(minus_gm, gm, -1.0, None, ALU.mult).then_inc(S("gm_ready"), 1)
            leaky(3)
            leaky(4)

            def times_edges(s):
                dve.wait_ge(S("e_exp"), EXP_ORDER.index(s) + 1)
                dve.scalar_tensor_tensor(P[:, s], P[:, s], 1.0, CT[:, s:s + 1].to_broadcast([T, NH, N]),
                                         ALU.min, ALU.mult).then_inc(S("p_dve"), 1)

            times_edges(DVE_TILES[0])
            dve.wait_ge(S("leaky_done"), NT)
            dve.wait_ge(S("dbc_ready"), 2)
            link(dve.tensor_tensor(rest, dbc, parts, ALU.subtract))
            link(dve.tensor_copy(parts[64:128], rest[64:128]))
            link(dve.tensor_tensor(rest[96:128], rest[96:128], parts[96:128], ALU.subtract))
            dve.tensor_copy(parts[96:128], rest[96:128]).then_inc(S("parts_ready"), 1)
            dve.wait_ge(S("dt_mm"), 1)
            for c in range(C):
                last = dve.tensor_scalar(dtx[:, c], PS[:, 5 * BANK + N * c:5 * BANK + N * c + N], pc("dt_b", c), None,
                                         ALU.add)
            last.then_inc(S("dt_read"), 1)
            dve.wait_ge(S("A_exp"), 1)
            dve.tensor_scalar(Aneg[:, :, :], Aneg[:, :, :], -1.0, None, ALU.mult).then_inc(S("A_ready"), 1)
            dve.wait_ge(S("dt_read"), 1)
            dve.scalar_tensor_tensor(dBx, dtx, -1.0, dtx, ALU.mult, ALU.max).then_inc(S("sp_abs"), 1)
            link(dve.tensor_scalar(dt, dtx, 0.0, None, ALU.max))

            times_edges(DVE_TILES[1])
            times_edges(DVE_TILES[2])
            dve.wait_ge(S("sp_exp"), 1)
            dve.tensor_scalar(hc, hs, 1.0, None, ALU.add).then_inc(S("sp_w"), 1)
            dve.wait_ge(S("sp_w"), 1)
            link(dve.scalar_tensor_tensor(dBx, hc, -1.0, hs, ALU.add, ALU.subtract))
            dve.wait_ge(S("sp_ln"), 1)
            link(dve.scalar_tensor_tensor(Cs, hc, 1.0, Cs, ALU.not_equal, ALU.mult))
            link(dve.tensor_tensor(Cs, Cs, dBx, ALU.subtract))
            link(dve.tensor_tensor(dt, dt, Cs, ALU.add))
            dve.tensor_tensor(dtx, dt, xc, ALU.mult).then_inc(S("dt_ready"), 1)
            dve.wait_ge(S("attT_mm"), 1)
            dve.tensor_copy(attT[:, 3 * BANK:NH * N], PS[0:FH + 1, 3 * BANK:NH * N]).then_inc(S("attT_dve"), 1)
            dve.wait_ge(S("att_mm"), 1)
            att = PS[0:T, 0:NT * BANK].rearrange("p (s n) -> p s n", s=NT)[:, :, 0:NH * 65] \
                .rearrange("p s (h f) -> p s h f", h=NH)
            link(dve.tensor_scalar(den, att[:, :, :, FH], 1e-16, None, ALU.add))
            link(dve.reciprocal(den, den))
            for s in range(NT):
                last = dve.tensor_tensor(sa4[:, s], att[:, s, :, 0:FH],
                                         den[:, s].rearrange("p (h f) -> p h f", f=1).to_broadcast([T, NH, FH]),
                                         ALU.mult)
            last.then_inc(S("att_used"), 1)
            dve.wait_ge(S("dt_ready"), 1)

            def inputs(n, c):
                dve.wait_ge(S("B_mm"), n + 1)
                if n >= 2:
                    dve.wait_ge(S("scanned"), C * (n - 2) + c + 1)
                dve.tensor_tensor(dBxs[n % 2][:, c], dtx[:, c], tr(0, 0), ALU.mult).then_inc(S("B_used"), 1)

            for c in range(C):
                inputs(0, c)
            for n in range(NS):
                for c in range(C):
                    k = C * n + c
                    if n < NS - 1:
                        inputs(n + 1, c)
                    dve.wait_ge(S("B_used"), k + 1)
                    dve.wait_ge(S("dA_ready"), k + 1)
                    if n >= 2:
                        dve.wait_ge(S("hc_ready"), k - 2 * C + 1)
                    dve.tensor_tensor_scan(hss[n % 2][:, c], dA[:, n % 2, c], dBxs[n % 2][:, c], 0.0,
                                           ALU.mult, ALU.add).then_inc(S("scanned"), 1)
            dve.wait_ge(S("scanned"), C * NS)
            dve.wait_ge(S("rankB_ready"), 1)
            for s in range(NT):
                last = dve.tensor_scalar(PTt[:, s], rankB, ncol[0:T, s:s + 1], None, ALU.is_equal)
            last.then_inc(S("PTt_ready"), 1)
            for c in range(C):
                dve.wait_ge(S("y_added"), C * (NS - 1) + c + 1)
                link(dve.scalar_tensor_tensor(xc[:, c], xc[:, c], pc("D", c), tr(4, c), ALU.mult, ALU.add))
                dve.tensor_tensor(xc[:, c], xc[:, c], zT[:, c], ALU.mult).then_inc(S("yT_ready"), 1)
            dve.wait_ge(S("sa_sum"), 2)
            dve.tensor_scalar(sb_, sa, 0.0, None, ALU.min).then_inc(S("elu_in"), 1)
            link(dve.tensor_scalar(sa, sa, 0.0, None, ALU.max))
            dve.wait_ge(S("elu_exp"), 1)
            link(dve.scalar_tensor_tensor(sa, sb_, -1.0, sa, ALU.add, ALU.add))
            norm(sa, hl, 5, row("lnl_g"), row("lnl_b"), hl).then_inc(S("hl_ready"), 1)

            def make_global(k, lo, hi):
                dve.wait_ge(S("back_mm"), k + 1)
                dve.tensor_tensor(sa[:, lo:hi], hn[:, lo:hi], nat_all(4)[:, lo:hi], ALU.add
                                  ).then_inc(S("back_used"), 1)
                dve.wait_ge(S("back_used"), k + 1)

            norm(sa, ha, 6, row("lng_g"), row("lng_b"), ha, make_global).then_inc(S("ha_ready"), 1)
            dve.wait_ge(S("ha_ready"), 1)
            link(dve.tensor_tensor(sa, hl, ha, ALU.subtract))
            link(dve.tensor_tensor(x[:, :, :], x[:, :, :], row("ln2_b"), ALU.add))
            for k, (lo, hi) in enumerate(BANKED):
                dve.wait_ge(S("gt_ready"), k + 1)
                link(dve.tensor_tensor(sa[:, lo:hi], sa[:, lo:hi], gt[:, lo:hi], ALU.mult))
                dve.tensor_tensor(hf[:, lo:hi], sa[:, lo:hi], ha[:, lo:hi], ALU.add).then_inc(S("hf_ready"), 1)
            dve.wait_ge(S("hf_ready"), len(BANKED))
            link(dve.tensor_tensor(sa, hf, row("ff2_b"), ALU.add))

            def make_sum(k, lo, hi):
                dve.wait_ge(S("ff2_mm"), k + 1)
                link(dve.tensor_tensor(sa[:, lo:hi], sa[:, lo:hi], nat_all(4)[:, lo:hi], ALU.add))

            norm(sa, x, 7, row("ln2_g"), x, hl, make_sum).then_inc(S("out_ready"), 1)


def kernel(x, src, dst, edge_type_16, edge_weight, edge_weight1, node_vec, L1_gnn_weight, L1_gnn_gate_weight, **w):
    import concourse.bacc as bacc
    from concourse.bass_utils import run_bass_kernel_spmd

    f = {k: np.asarray(v) for k, v in w.items()}

    def edges(a):
        return np.asarray(a).reshape(ET, T).T

    def chunks(a):
        a = np.asarray(a)
        return a.reshape(-1, 128, a.shape[1]).transpose(1, 0, 2).reshape(128, -1)

    def vec(name):
        return f[name].reshape(-1, 128).T

    L3 = "L3_gnn_"
    arrays = {
        "x": np.ascontiguousarray(x),
        "edge_int": np.ascontiguousarray(np.stack([edges(src), edges(dst), edges(edge_type_16)], 1)),
        "edge_flt": np.ascontiguousarray(np.stack([edges(edge_weight), edges(edge_weight1)], 1)),
        "noise": np.ascontiguousarray(np.asarray(node_vec).reshape(NT, T).T),
        "pcols": np.ascontiguousarray(np.concatenate(
            [vec("L0_gnn_b0"), vec("L0_gnn_b1"), vec("L0_gnn_b2"), vec("L2_gnn_bp"), chunks(f[L3 + "conv_w"]),
             vec(L3 + "conv_b"), vec(L3 + "dt_proj_b"), chunks(f[L3 + "A_log"]), vec(L3 + "D_param"),
             vec(L3 + "ff1_b")], 1)),
        "rows": np.ascontiguousarray(np.stack(
            [f[k] for k in ("L0_gnn_bf", "L2_gnn_b1", "L2_gnn_b2")] +
            [f[L3 + k] for k in ("gat_b", "ln_local_g", "ln_local_b", "ln_global_g", "ln_global_b", "ln2_g", "ln2_b",
                                 "ff2_b")] + [f[L3 + k].reshape(-1) for k in ("gat_a_src", "gat_a_tgt")], 0)),
        "w0": np.ascontiguousarray(np.concatenate([chunks(f["L0_gnn_" + k]) for k in ("W0", "W1", "W2", "Wf")], 1)),
        "w1": np.ascontiguousarray(np.asarray(L1_gnn_weight).reshape(R, C, 128, D).transpose(2, 0, 1, 3)),
        "gw": np.ascontiguousarray(np.asarray(L1_gnn_gate_weight).reshape(R, C, 128).transpose(2, 1, 0)),
        "w2": np.ascontiguousarray(np.concatenate([chunks(f["L2_gnn_" + k].T) for k in ("Wp", "W1", "W2")], 1)),
        "w3": np.ascontiguousarray(np.concatenate(
            [chunks(f[L3 + k].T) for k in ("gat_w", "in_proj_w", "out_proj_w", "wl", "wg", "ff1_w", "ff2_w")], 1)),
        "xw": np.ascontiguousarray(chunks(f[L3 + "x_proj_w"][X_ROWS].T)),
        "dtw": np.ascontiguousarray(f[L3 + "dt_proj_w"].T),
    }
    nc = bacc.Bacc("TRN2", target_bir_lowering=False, num_devices=1)
    args = [nc.dram_tensor("in_" + name, a.shape, mybir.dt.from_np(a.dtype), kind="ExternalInput").ap()
            for name, a in arrays.items()]
    out = nc.dram_tensor("out_x", (N, D), F32, kind="ExternalOutput").ap()
    table = nc.dram_tensor("table", (R, N, D), F32, kind="Internal").ap()
    counts = nc.dram_tensor("counts", (T, NT * N), F32, kind="Internal").ap()
    gnn_kernel(nc, *args, out, table, counts)
    return run_bass_kernel_spmd(nc, [{"in_" + k: a for k, a in arrays.items()}], core_ids=[0]).results[0]["out_x"]
```
